# Optimizing a Trainium2 kernel written in Bass

```python
import numpy as np
import jax
import jax.numpy as jnp

def _softmax(x, axis=-1):
    return jax.nn.softmax(x, axis=axis)
def _gelu(x):
    return jax.nn.gelu(x, approximate=True)
def _silu(x):
    return jax.nn.silu(x)
def _sigmoid(x):
    return jax.nn.sigmoid(x)
def _layernorm(x, axis=-1, eps=1e-5):
    m = jnp.mean(x, axis=axis, keepdims=True)
    v = jnp.var(x, axis=axis, keepdims=True)
    return (x - m) / jnp.sqrt(v + eps)
def _scatter_add(tgt, idx, src, axis=0):
    return tgt.at[idx].add(src)
def _segment_sum(src, seg, n):
    return jax.ops.segment_sum(src, seg, n)

kernel_name = 'mk_metaformer_d1_conv_nchw256_801570'

def setup_inputs(seed: int = 0):
    np.random.seed(seed)
    _w = jnp.asarray
    def _rec_inputs():
        import jax
        import jax.numpy as jnp
        _gk = jax.random.key(seed)
        x = -0.0005207 + 1.001 * jax.random.normal(jax.random.fold_in(_gk, 1), (2, 256, 64, 64), jnp.float32)
        return x
    x = _rec_inputs()
    def _L0_conv_setup():
        import jax, jax.numpy as jnp
        import numpy as np
        B, C, H, W = (2, 256, 64, 64)
        NUM_HEADS = 4
        DIM_HEAD_QK = 64
        DIM_HEAD_V = 64
        DIM_OUT_QK = NUM_HEADS * DIM_HEAD_QK
        DIM_OUT_V = NUM_HEADS * DIM_HEAD_V
        SCALE = DIM_HEAD_QK ** (-0.5)

        def rel_logits_1d(q, rel_k, permute):
            Bh, Hq, Wq, d = q.shape
            R = 2 * Wq - 1
            x = jnp.einsum('bhwd,rd->bhwr', q, rel_k)
            x = x.reshape(-1, Wq, R)
            x_pad = jnp.pad(x, ((0, 0), (0, 0), (0, 1))).reshape(x.shape[0], -1)
            x_pad = jnp.pad(x_pad, ((0, 0), (0, Wq - 1)))
            x_pad = x_pad.reshape(-1, Wq + 1, R)
            x = x_pad[:, :Wq, Wq - 1:]
            x = x.reshape(Bh, Hq, 1, Wq, Wq)
            x = jnp.broadcast_to(x, (Bh, Hq, Hq, Wq, Wq))
            return jnp.transpose(x, permute)

        def pos_embed_rel(q, height_rel, width_rel):
            Bh = q.shape[0]
            qr = q.reshape(Bh, H, W, -1)
            rel_w = rel_logits_1d(qr, width_rel, (0, 1, 3, 2, 4))
            qt = jnp.transpose(qr, (0, 2, 1, 3))
            rel_h = rel_logits_1d(qt, height_rel, (0, 3, 1, 4, 2))
            return (rel_h + rel_w).reshape(Bh, H * W, H * W)
        key = jax.random.key(seed)
        k1, k2, k3, k4 = jax.random.split(key, 4)
        x = jax.random.normal(k1, (B, C, H, W), dtype=jnp.float32)
        qkv_w = jax.random.normal(k2, (2 * DIM_OUT_QK + DIM_OUT_V, C), dtype=jnp.float32) * C ** (-0.5)
        height_rel = jax.random.normal(k3, (2 * H - 1, DIM_HEAD_QK), dtype=jnp.float32) * SCALE
        width_rel = jax.random.normal(k4, (2 * W - 1, DIM_HEAD_QK), dtype=jnp.float32) * SCALE
        return {'x': x, 'qkv_w': qkv_w, 'height_rel': height_rel, 'width_rel': width_rel}
    _L0_conv_all = _L0_conv_setup()
    _L0_conv_in = {k: v for k, v in _L0_conv_all.items() if k in ('qkv_w', 'height_rel', 'width_rel', )}
    del _L0_conv_all

    def _L0_ffn_setup():
        import math
        import jax, jax.numpy as jnp
        import numpy as np
        CAPACITY_FACTOR = 1.25
        key = jax.random.key(seed)
        ks = jax.random.split(key, 5)
        B, L, D, F, E = (8, 8192, 256, 1024, 8)
        h = jax.random.normal(ks[0], (B, L, D), dtype=jnp.float32)
        gate_w = jax.random.normal(ks[1], (D, E), dtype=jnp.float32) * 0.02
        gate_b = jnp.zeros((E,), dtype=jnp.float32)
        w1 = jax.random.normal(ks[2], (E, D, F), dtype=jnp.float32) * (1.0 / math.sqrt(D))
        b1 = jnp.zeros((E, F), dtype=jnp.float32)
        w2 = jax.random.normal(ks[3], (E, F, D), dtype=jnp.float32) * (1.0 / math.sqrt(F))
        b2 = jnp.zeros((E, D), dtype=jnp.float32)
        return {'h': h, 'gate_w': gate_w, 'gate_b': gate_b, 'w1': w1, 'b1': b1, 'w2': w2, 'b2': b2}
    _L0_ffn_all = _L0_ffn_setup()
    _L0_ffn_in = {k: v for k, v in _L0_ffn_all.items() if k in ('gate_w', 'gate_b', 'w1', 'b1', 'w2', 'b2', )}
    del _L0_ffn_all

    return {
        "x": x,
        "L0_conv_qkv_w": _L0_conv_in["qkv_w"],
        "L0_conv_height_rel": _L0_conv_in["height_rel"],
        "L0_conv_width_rel": _L0_conv_in["width_rel"],
        "L0_ffn_gate_w": _L0_ffn_in["gate_w"],
        "L0_ffn_gate_b": _L0_ffn_in["gate_b"],
        "L0_ffn_w1": _L0_ffn_in["w1"],
        "L0_ffn_b1": _L0_ffn_in["b1"],
        "L0_ffn_w2": _L0_ffn_in["w2"],
        "L0_ffn_b2": _L0_ffn_in["b2"],
    }

def reference(x, L0_conv_qkv_w, L0_conv_height_rel, L0_conv_width_rel, L0_ffn_gate_w, L0_ffn_gate_b, L0_ffn_w1, L0_ffn_b1, L0_ffn_w2, L0_ffn_b2):
    import jax
    import jax.numpy as jnp
    def _L0_conv_ref(x, qkv_w, height_rel, width_rel):
        import jax, jax.numpy as jnp
        import numpy as np
        B, C, H, W = (2, 256, 64, 64)
        NUM_HEADS = 4
        DIM_HEAD_QK = 64
        DIM_HEAD_V = 64
        DIM_OUT_QK = NUM_HEADS * DIM_HEAD_QK
        DIM_OUT_V = NUM_HEADS * DIM_HEAD_V
        SCALE = DIM_HEAD_QK ** (-0.5)

        def rel_logits_1d(q, rel_k, permute):
            Bh, Hq, Wq, d = q.shape
            R = 2 * Wq - 1
            x = jnp.einsum('bhwd,rd->bhwr', q, rel_k)
            x = x.reshape(-1, Wq, R)
            x_pad = jnp.pad(x, ((0, 0), (0, 0), (0, 1))).reshape(x.shape[0], -1)
            x_pad = jnp.pad(x_pad, ((0, 0), (0, Wq - 1)))
            x_pad = x_pad.reshape(-1, Wq + 1, R)
            x = x_pad[:, :Wq, Wq - 1:]
            x = x.reshape(Bh, Hq, 1, Wq, Wq)
            x = jnp.broadcast_to(x, (Bh, Hq, Hq, Wq, Wq))
            return jnp.transpose(x, permute)

        def pos_embed_rel(q, height_rel, width_rel):
            Bh = q.shape[0]
            qr = q.reshape(Bh, H, W, -1)
            rel_w = rel_logits_1d(qr, width_rel, (0, 1, 3, 2, 4))
            qt = jnp.transpose(qr, (0, 2, 1, 3))
            rel_h = rel_logits_1d(qt, height_rel, (0, 3, 1, 4, 2))
            return (rel_h + rel_w).reshape(Bh, H * W, H * W)
        qkv = jnp.einsum('bchw,oc->bohw', x, qkv_w)
        q, k, v = jnp.split(qkv, [DIM_OUT_QK, 2 * DIM_OUT_QK], axis=1)
        HW = H * W
        q = q.reshape(B * NUM_HEADS, DIM_HEAD_QK, HW).transpose(0, 2, 1)
        k = k.reshape(B * NUM_HEADS, DIM_HEAD_QK, HW)
        v = v.reshape(B * NUM_HEADS, DIM_HEAD_V, HW).transpose(0, 2, 1)
        attn = jnp.einsum('bnd,bdm->bnm', q, k) * SCALE + pos_embed_rel(q, height_rel, width_rel)
        attn = jax.nn.softmax(attn, axis=-1)
        out = jnp.einsum('bnm,bmd->bnd', attn, v)
        out = out.transpose(0, 2, 1).reshape(B, DIM_OUT_V, H, W)
        return out

    def _L0_ffn_ref(h, gate_w, gate_b, w1, b1, w2, b2):
        import math
        import jax, jax.numpy as jnp
        import numpy as np
        CAPACITY_FACTOR = 1.25
        B, L, D = h.shape
        E = gate_w.shape[1]
        T = B * L
        C = max(1, math.ceil(CAPACITY_FACTOR * T / E))
        x = h.reshape(T, D)
        logits = x @ gate_w + gate_b
        probs = jax.nn.softmax(logits, axis=-1)
        idx = jnp.argmax(probs, axis=-1)
        prb = jnp.take_along_axis(probs, idx[:, None], axis=1)[:, 0]
        one_hot = jax.nn.one_hot(idx, E, dtype=jnp.float32)
        pos = (jnp.cumsum(one_hot, axis=0) * one_hot).sum(-1).astype(jnp.int32) - 1
        kept = pos < C
        pos_safe = jnp.where(kept, pos, C)
        buf = jnp.zeros((E, C, D), dtype=h.dtype).at[idx, pos_safe].set(x, mode='drop')
        hmid = jax.nn.relu(jnp.einsum('ecd,edf->ecf', buf, w1) + b1[:, None, :])
        ybuf = jnp.einsum('ecf,efd->ecd', hmid, w2) + b2[:, None, :]
        pos_g = jnp.minimum(pos, C - 1)
        y_tok = ybuf[idx, pos_g] * (prb * kept)[:, None]
        y = y_tok.reshape(B, L, D)
        y = jnp.nan_to_num(y, nan=0.0, posinf=10000.0, neginf=-10000.0)
        return y

    def _gn(v, G=32, eps=1e-5):
        B_, C_, H_, W_ = v.shape
        g = v.reshape(B_, G, C_ // G, H_, W_)
        m = jnp.mean(g, axis=(2, 3, 4), keepdims=True)
        s = jnp.var(g, axis=(2, 3, 4), keepdims=True)
        return ((g - m) / jnp.sqrt(s + eps)).reshape(v.shape)

    def _ln_c(v, eps=1e-6):
        m = jnp.mean(v, axis=1, keepdims=True)
        s = jnp.var(v, axis=1, keepdims=True)
        return (v - m) / jnp.sqrt(s + eps)

    def _ln_t(v, eps=1e-5):
        m = jnp.mean(v, axis=-1, keepdims=True)
        s = jnp.var(v, axis=-1, keepdims=True)
        return (v - m) / jnp.sqrt(s + eps)

    def _to_tokens(v):
        B_, C_, H_, W_ = v.shape
        return v.reshape(B_, C_, H_ * W_).transpose(0, 2, 1)
    def _from_tokens(t, like):
        B_, C_, H_, W_ = like.shape
        return t.transpose(0, 2, 1).reshape(B_, C_, H_, W_)

    x = x + _L0_conv_ref(_ln_c(x), L0_conv_qkv_w, L0_conv_height_rel, L0_conv_width_rel)
    t = _to_tokens(x)
    t = t + _L0_ffn_ref(_ln_t(t), L0_ffn_gate_w, L0_ffn_gate_b, L0_ffn_w1, L0_ffn_b1, L0_ffn_w2, L0_ffn_b2)
    x = _from_tokens(t, x)
    return x


_drawn_inputs = setup_inputs


def setup_inputs(seed=0):
    import zlib

    import numpy as np

    out = dict(_drawn_inputs(seed))
    spreads = {'L0_ffn_gate_b': (0.0, 0.1), 'L0_ffn_b1': (0.0, 0.613), 'L0_ffn_b2': (0.0, 0.433)}
    factors = {}
    for name, (base, spread) in spreads.items():
        noise = np.random.default_rng([zlib.crc32(name.encode()), seed]).standard_normal(out[name].shape)
        drawn = base * np.exp(spread * noise) if base else spread * noise
        out[name] = jnp.asarray(drawn.astype(out[name].dtype))
    for name, factor in factors.items():
        out[name] = (out[name] * factor).astype(out[name].dtype)
    return out
```

```python
import concourse.bass as bass
from concourse import mybir
from contextlib import ExitStack

F32 = mybir.dt.float32
F16 = mybir.dt.float16
I32 = mybir.dt.int32
U32 = mybir.dt.uint32
ALU = mybir.AluOpType
ACT = mybir.ActivationFunctionType
AX = mybir.AxisListType

P = 128
BATCH, C, SIDE = 2, 256, 64
TOK = SIDE * SIDE
HEADS, DH = 4, 64
KC = C // P
NT = TOK // P
QB = 512
NB = TOK // QB
SUB = QB // P
ROWS = QB // SIDE
UNITS = TOK // (2 * P)
NBUF = 4
VW = 2 * DH + 1
WIN = 2 * SIDE - 1
WINP = SIDE - 1 + P

EXPERTS, FF, CAP = 8, 1024, 1280
TT = BATCH * NT
ST = CAP // P
SLOTS = EXPERTS * CAP
KF = FF // P
CHUNKS = [(0, 4), (4, 3), (7, 3)]

S16 = 16.0
QK = S16 * DH ** -0.5
SHIFT = 7.0

MAXU = [[] for _ in range(UNITS)]
_n = 0
for _u in range(UNITS):
    for _ in range(2 if _u in (0, 3, 6, 9) else 1):
        if _n < UNITS and _u < 12:
            MAXU[_u].append(_n)
            _n += 1
assert _n == UNITS
U_RH, U_R = 12, 13


def wait_apart(eng, sem, count, passed):
    eng.wait_ge(sem, count)
    eng.sem_inc(passed, 1)


def attention_and_norm(nc, ctx, xc, xt, whead, wv, hrt, wrt, onehots, ident_h, gate_w, t_dram, xn_dram, LG):
    def sb(name, shape, dt):
        return ctx.enter_context(nc.sbuf_tensor(name, shape, dt))

    def sem(name):
        return ctx.enter_context(nc.semaphore(name))

    XN = sb("XN", [P, KC, TOK], F32)
    T = sb("T", [P, NT, C], F32)
    V = sb("V", [P, HEADS, NT, VW + 1], F16)
    VS = sb("VS", [P, NT, VW + 1], F16)
    QA = sb("QA", [P, TOK], F16)
    QBf = sb("QBf", [P, TOK], F16)
    QC = sb("QC", [P, TOK], F16)
    QD = sb("QD", [DH, TOK], F16)
    KA = sb("KA", [P, TOK], F16)
    KB = sb("KB", [P, TOK], F16)
    KCC = sb("KCC", [P, TOK], F16)
    KD = sb("KD", [DH, TOK], F16)
    PH = sb("PH", [P, NBUF, 2, QB], F16)
    PL = sb("PL", [P, NBUF, 2, QB], F16)
    PF = sb("PF", [P, 2, 2, QB], F32)
    WH = sb("WH", [P, KC, 2 * DH], F32)
    WV = sb("WV", [P, KC, HEADS * DH], F32)
    RELH = sb("RELH", [DH, 2, WINP], F16)
    RELL = sb("RELL", [DH, 2, WINP], F16)
    G = sb("G", [P, SUB, SIDE], F32)
    G2 = sb("G2", [P, SUB, SIDE], F32)
    MROW = sb("MROW", [P, SUB], F32)
    MNEG = sb("MNEG", [P, SUB], F32)
    DIAG = sb("DIAG", [P, SUB, P], F16)
    IDH = sb("IDH", [P, P], F16)
    IDF = sb("IDF", [P, P], F32)
    ONEH = sb("ONEH", [P, P], F16)
    AVG = sb("AVG", [P, P], F32)
    PVS = sb("PVS", [P, SUB, VW], F32)
    PVR = sb("PVR", [P, SUB], F32)
    PVO = G2
    EPS6 = sb("EPS6", [P, 1], F32)
    EPS5 = sb("EPS5", [P, 1], F32)
    MV = sb("MV", [P, NT, 2], F32)
    RSTD = sb("RSTD", [P, NT], F32)
    RSTD2 = sb("RSTD2", [P, NT], F32)
    PLF = PL[:].rearrange("p a b n -> p (a b n)").bitcast(F32)
    XNT = PLF[:, 0:2 * C].rearrange("p (a c) -> p a c", a=2)
    REL = PLF[0:DH, 0:2 * WINP].rearrange("p (a w) -> p a w", a=2)
    XTT = PLF[:, 2 * C:4 * C].rearrange("p (a c) -> p a c", a=2)
    STAT = PLF[:, 4 * C:4 * C + 6 * NT].rearrange("p (t s) -> p t s", s=6)
    GW = sb("GW", [P, KC, EXPERTS], F32)
    SQ = PF
    RS = PH[:, 0:2, :, :].rearrange("p a b n -> p a (b n)").bitcast(F32)

    SP = ctx.enter_context(nc.psum_tensor("SP", [P, 4, 512], F32))
    MX = ctx.enter_context(nc.psum_tensor("MX", [P, 2, 512], F32))
    PV = ctx.enter_context(nc.psum_tensor("PV", [P, 2, 512], F32))

    s_passed = sem("s_passed")
    s_const = sem("s_const")
    s_ones = sem("s_ones")
    s_rel = sem("s_rel")
    s_x = sem("s_x")
    s_t = sem("s_t")
    s_wh = sem("s_wh")
    s_mean = sem("s_mean")
    s_cent = sem("s_cent")
    s_sq = sem("s_sq")
    s_var = sem("s_var")
    s_std = sem("s_std")
    s_rstd = sem("s_rstd")
    s_xn = sem("s_xn")
    s_vps = sem("s_vps")
    s_vh = sem("s_vh")
    s_vl = sem("s_vl")
    s_qk = sem("s_qk")
    s_qkh = sem("s_qkh")
    s_qkl = sem("s_qkl")
    s_dup = sem("s_dup")
    s_rw = sem("s_rw")
    s_rwh = sem("s_rwh")
    s_rwl = sem("s_rwl")
    s_mx = sem("s_mx")
    s_mxr = sem("s_mxr")
    s_rh = sem("s_rh")
    s_g2 = sem("s_g2")
    s_mrow = sem("s_mrow")
    s_mneg = sem("s_mneg")
    s_diag = sem("s_diag")
    s_r = sem("s_r")
    s_rhh = sem("s_rhh")
    s_rhl = sem("s_rhl")
    s_s = sem("s_s")
    s_e = sem("s_e")
    s_pl = sem("s_pl")
    s_pv = sem("s_pv")
    s_pvs = sem("s_pvs")
    s_pvr = sem("s_pvr")
    s_pvo = sem("s_pvo")
    s_out = sem("s_out")
    s_st = sem("s_st")
    s_mv = sem("s_mv")
    s_ts = sem("s_ts")
    s_tr = sem("s_tr")
    s_tn = sem("s_tn")
    s_tx = sem("s_tx")
    s_te = sem("s_te")
    s_lg = sem("s_lg")
    s_lge = sem("s_lge")
    s_td = sem("s_td")
    s_xd = [sem("s_xd0"), sem("s_xd1")]

    with nc.Block() as block:

        @block.sync
        def _(sp):
            sp.dma_start(REL[:, 0, 0:WIN], hrt).then_inc(s_const, 16)
            sp.dma_start(REL[:, 1, 0:WIN], wrt).then_inc(s_const, 16)
            sp.dma_start(WV[:], wv.rearrange("(k p) n -> p k n", p=P)).then_inc(s_const, 16)
            sp.dma_start(KA[DH:P, :], onehots[0]).then_inc(s_const, 16)
            sp.dma_start(KB[DH:P, :], onehots[0]).then_inc(s_const, 16)
            sp.dma_start(KCC[DH:P, :], onehots[1]).then_inc(s_const, 16)
            sp.dma_start(KD[:], onehots[1]).then_inc(s_const, 16)
            sp.dma_start(IDF[:], ident_h).then_inc(s_const, 16)
            sp.dma_start(GW[:], gate_w.rearrange("(k p) e -> p k e", p=P)).then_inc(s_const, 16)
            with sp.Fori(0, BATCH) as b:
                sp.wait_ge(s_qkl, b * (HEADS * NB))
                for k in range(KC):
                    sp.dma_start(XN[:, k, :], xc[bass.ds(b, 1), k * P:(k + 1) * P, :].rearrange("o p n -> p (o n)"))\
                      .then_inc(s_x, 16)
                sp.wait_ge(s_td, b * 16)
                sp.wait_ge(s_lge, b * NT)
                sp.dma_start(T[:], xt[bass.ds(b, 1)].rearrange("o (t p) c -> p (o t) c", p=P)).then_inc(s_t, 16)
                with sp.Fori(0, HEADS) as h:
                    sp.wait_ge(s_qkl, (b * HEADS + h) * NB)
                    sp.dma_start(WH[:], whead[bass.ds(h, 1)].rearrange("o (k p) n -> p (o k) n", p=P)).then_inc(s_wh, 16)
                sp.wait_ge(s_out, (b + 1) * (HEADS * NB))
                sp.dma_start(t_dram[bass.ds(b * NT, NT)].rearrange("t p c -> p t c"), T[:]).then_inc(s_td, 16)
                with sp.Fori(0, NT // 2) as i:
                    for par in range(2):
                        sp.wait_ge(s_tn, b * NT + i * 2 + par + 1)
                        sp.dma_start(xn_dram[bass.ds(b * NT + i * 2 + par, 1)].rearrange("t p c -> p (t c)"),
                                     XNT[:, par, :]).then_inc(s_xd[par], 16)
            sp.wait_ge(s_td, BATCH * 16)
            for par in range(2):
                sp.wait_ge(s_xd[par], BATCH * NT // 2 * 16)

        @block.gpsimd
        def _(pool):
            nc.gpsimd.memset(AVG[:], 1.0 / C)
            nc.gpsimd.memset(ONEH[:], 1.0)
            nc.gpsimd.memset(REL[:, :, WIN:WINP], 0.0)
            nc.gpsimd.memset(EPS6[:], 1e-6)
            nc.gpsimd.memset(EPS5[:], 1e-5)
            nc.gpsimd.memset(V[:, :, :, DH:DH + 1], S16).then_inc(s_ones, 1)
            with pool.Fori(0, BATCH) as b, pool.Fori(0, HEADS) as h, pool.Fori(0, NB) as j:
                n = (b * HEADS + h) * NB + j
                pool.wait_ge(s_rel, 3)
                pool.wait_ge(s_r, n)
                wait_apart(pool, s_mneg, n + 1, s_passed)
                for ns in range(SUB):
                    last = nc.gpsimd.tensor_scalar(DIAG[:, ns, :], IDH[:], MNEG[:, ns:ns + 1], 1.0, ALU.mult, ALU.mult)
                last.then_inc(s_diag, 1)

        @block.tensor
        def _(pe):
            mm = nc.tensor.matmul

            def cols(j, size=QB):
                return bass.ds(j * size, size)

            def scores(n, j, u, buf_unit):
                bank = 2 * (buf_unit % 2)
                pe.wait_ge(s_e, n * UNITS + buf_unit + NBUF - 1)
                for i in range(2):
                    key = slice((2 * u + i) * P, (2 * u + i + 1) * P)
                    out = SP[:, bank + i, :]
                    mm(out, KA[:, key], QA[:, cols(j)], start=True, stop=False)
                    mm(out, KB[:, key], QBf[:, cols(j)], start=False, stop=False)
                    mm(out, KCC[:, key], QC[:, cols(j)], start=False, stop=False)
                    last = mm(out, KD[:, key], QD[:, cols(j)], start=False, stop=True)
                last.then_inc(s_s, 1)

            def add_values(n, u):
                pe.wait_ge(s_pl, n * UNITS + u + 1 + NBUF)
                if u == 0:
                    pe.wait_ge(s_pvs, n)
                for ns in range(SUB):
                    out = PV[:, ns // 2, (ns % 2) * VW:(ns % 2 + 1) * VW]
                    for i in range(2):
                        t = 2 * u + i
                        first = t == 0 and ns % 2 == 0
                        mm(out, PH[:, u % NBUF, i, ns * P:(ns + 1) * P], VS[:, t, 0:VW], start=first,
                           stop=False, skip_group_check=True)
                        last = mm(out[:, 0:DH + 1], PL[:, u % NBUF, i, ns * P:(ns + 1) * P], VS[:, t, 0:DH + 1], start=False,
                                  stop=(t == NT - 1), skip_group_check=True)
                last.then_inc(s_pv, 1)

            def max_unit(n, j, k):
                pe.wait_ge(s_mxr, n * UNITS + k)
                if k == 0:
                    pe.wait_ge(s_rhl, n)
                for i in range(2):
                    last = mm(MX[:, i, :], QA[:, bass.ds(j * QB + (k // 4) * P, P)],
                              KA[:, (k % 4) * 1024 + i * 512:(k % 4) * 1024 + (i + 1) * 512], start=True, stop=True)
                last.then_inc(s_mx, 1)

            def height_by_token(n, j):
                pe.wait_ge(s_mxr, (n + 1) * UNITS)
                for ns in range(SUB):
                    last = mm(MX[:, 0, ns * (SIDE + 1):(ns + 1) * (SIDE + 1)], QA[0:DH, bass.ds(j * QB + ns * P, P)],
                              RELH[:, 0, bass.ds((SIDE - 2 - 2 * ns) - j * (2 * SUB), SIDE + 1)],
                              start=(ns == 0), stop=(ns == SUB - 1), skip_group_check=True)
                last.then_inc(s_rh, 1)

            def height_minus_max(n, j):
                pe.wait_ge(s_diag, n + 1)
                for ns in range(SUB):
                    mm(MX[:, 1, ns * P:(ns + 1) * P], ONEH[:], DIAG[:, ns, :], start=(ns == 0), stop=False,
                       skip_group_check=True)
                for r in range(ROWS):
                    win = bass.ds((SIDE - 1 - r) - j * ROWS, P)
                    tok = bass.ds(j * QB + r * SIDE, SIDE)
                    out = MX[:, 1, r * SIDE:(r + 1) * SIDE]
                    mm(out, RELH[:, 0, win], QA[0:DH, tok], start=False, stop=False, skip_group_check=True)
                    mm(out, RELL[:, 0, win], QA[0:DH, tok], start=False, stop=False, skip_group_check=True)
                    last = mm(out, RELH[:, 0, win], QC[0:DH, tok], start=False, stop=True, skip_group_check=True)
                last.then_inc(s_r, 1)

            pe.sem_inc(s_e, NBUF)
            pe.sem_inc(s_pl, NBUF)
            pe.sem_inc(s_pv, NBUF)
            pe.wait_ge(s_ones, 1)
            pe.wait_ge(s_const, 9 * 16)
            pe.wait_ge(s_rel, 3)
            with pe.Fori(0, BATCH) as b:
                def mean(m, par, j):
                    pe.wait_ge(s_cent, m)
                    for k in range(KC):
                        last = mm(SP[:, par, :], AVG[:], XN[:, k, cols(j)], start=(k == 0), stop=(k == KC - 1))
                    last.then_inc(s_mean, 1)

                def variance(m, par):
                    pe.wait_ge(s_sq, m + 1)
                    for k in range(KC):
                        last = mm(SP[:, 2 + par, :], AVG[:], SQ[:, par, k, :], start=(k == 0), stop=(k == KC - 1))
                    last.then_inc(s_var, 1)
                pe.wait_ge(s_x, (b + 1) * (16 * KC))
                wait_apart(pe, s_te, b * NT, s_passed)
                with pe.Fori(0, NB // 2) as i:
                    for par in range(2):
                        m = b * NB + i * 2 + par
                        mean(m, par, i * 2 + par)
                        variance(m, par)
                pe.wait_ge(s_xn, (b + 1) * NB)
                for t in range(NT):
                    if t % 2 == 0 and t // 2 >= 2:
                        pe.wait_ge(s_vl, b * (NT // 2) + t // 2 - 1)
                    for k in range(KC):
                        last = mm(SP[:, (t // 2) % 2, (t % 2) * C:(t % 2 + 1) * C], XN[:, k, t * P:(t + 1) * P], WV[:, k, :],
                                  start=(k == 0 and t % 2 == 0), stop=(k == KC - 1), skip_group_check=True)
                    if t % 2:
                        last.then_inc(s_vps, 1)
                wait_apart(pe, s_vl, (b + 1) * (NT // 2), s_passed)
                with pe.Fori(0, HEADS) as h:
                    hh = b * HEADS + h
                    pe.wait_ge(s_wh, (hh + 1) * 16)
                    wait_apart(pe, s_e, hh * (NB * UNITS) + NBUF, s_passed)
                    with pe.Fori(0, NB // 2) as i:
                        for par in range(2):
                            pe.wait_ge(s_qkl, hh * NB + i * 2)
                            for k in range(KC):
                                last = mm(SP[:, par, :], WH[:, k, :], XN[:, k, cols(i * 2 + par)], start=(k == 0),
                                          stop=(k == KC - 1))
                            last.then_inc(s_qk, 1)
                    wait_apart(pe, s_qkl, (hh + 1) * NB, s_passed)
                    with pe.Fori(0, NB // 2) as i:
                        for par in range(2):
                            pe.wait_ge(s_rwl, hh * NB + i * 2)
                            for w in range(ROWS):
                                win = bass.ds((SIDE - 1 - par * ROWS - w) - i * (2 * ROWS), P)
                                tok = bass.ds(i * (2 * ROWS) + par * ROWS + w, SIDE, SIDE)
                                out = SP[:, par, w * SIDE:(w + 1) * SIDE]
                                mm(out, RELH[:, 1, win], QA[0:DH, tok], start=(w == 0), stop=False, skip_group_check=True)
                                mm(out, RELL[:, 1, win], QA[0:DH, tok], start=False, stop=False, skip_group_check=True)
                                last = mm(out, RELH[:, 1, win], QC[0:DH, tok], start=False, stop=True, skip_group_check=True)
                            last.then_inc(s_rw, 1)
                    pe.wait_ge(s_rwl, (hh + 1) * NB)
                    pe.wait_ge(s_dup, hh + 1)
                    n0 = hh * NB
                    for k in range(UNITS):
                        max_unit(n0, 0, k)
                    height_by_token(n0, 0)
                    height_minus_max(n0, 0)
                    pe.wait_ge(s_rhl, n0 + 1)
                    scores(n0, 0, 0, 0)
                    scores(n0, 0, 1, 1)

                    def block_of(n, j, more):
                        for u in range(UNITS):
                            if u == UNITS - 2 and more:
                                pe.wait_ge(s_rhl, n + 2)
                            if u < UNITS - 2:
                                scores(n, j, u + 2, u + 2)
                            elif more:
                                scores(n, j + 1, u + 2 - UNITS, u + 2)
                            if more:
                                for k in MAXU[u]:
                                    max_unit(n + 1, j + 1, k)
                                if u == U_RH:
                                    height_by_token(n + 1, j + 1)
                                if u == U_R:
                                    height_minus_max(n + 1, j + 1)
                            add_values(n, u)
                    with pe.Fori(0, NB - 1) as j:
                        block_of(n0 + j, j, True)
                    block_of(n0 + NB - 1, NB - 1, False)
                with pe.Fori(0, NT // 2) as i:
                    for par in range(2):
                        m = b * NT + i * 2 + par
                        pe.wait_ge(s_tn, m + 1)
                        for k in range(KC):
                            last = nc.tensor.transpose(SP[:, par, k * P:(k + 1) * P], XNT[:, par, k * P:(k + 1) * P], IDF[:])
                        last.then_inc(s_tx, 1)
                        pe.wait_ge(s_te, m + 1)
                        for k in range(KC):
                            last = mm(MX[:, par, 0:EXPERTS], XTT[:, par, k * P:(k + 1) * P], GW[:, k, :], start=(k == 0),
                                      stop=(k == KC - 1))
                        last.then_inc(s_lg, 1)

        @block.scalar
        def _(act):
            A = nc.scalar.activation

            def exp_unit(n, buf_unit):
                w = n * UNITS + buf_unit
                act.wait_ge(s_s, w + 1)
                act.wait_ge(s_pv, w + 1)
                act.wait_ge(s_pl, w + NBUF - 1)
                src = SP[:, 2 * (buf_unit % 2):2 * (buf_unit % 2) + 2, :]
                A(PH[:, buf_unit % NBUF, :, :], src, ACT.Exp, scale=1.0 / (S16 * S16))
                A(PF[:, buf_unit % 2, :, :], src, ACT.Exp, scale=1.0 / (S16 * S16)).then_inc(s_e, 1)

            def height_high(n, j):
                wait_apart(act, s_r, n + 1, s_passed)
                A(QC[DH:P, bass.ds(j * QB, QB)], MX[0:DH, 1, :], ACT.Copy).then_inc(s_rhh, 1)

            act.wait_ge(s_const, 9 * 16)
            act.wait_ge(s_ones, 1)
            A(RELH[:], REL[:], ACT.Copy).then_inc(s_rel, 1)
            A(IDH[:], IDF[:], ACT.Copy).then_inc(s_rel, 1)
            with act.Fori(0, BATCH) as b:
                with act.Fori(0, NB // 2) as i:
                    for par in range(2):
                        m = b * NB + i * 2 + par
                        wait_apart(act, s_cent, m + 1, s_passed)
                        A(SQ[:, par, :, :], XN[:, :, bass.ds((i * 2 + par) * QB, QB)], ACT.Square).then_inc(s_sq, 1)
                        act.wait_ge(s_var, m + 1)
                        act.wait_ge(s_xn, m)
                        A(RS[:, par, :], SP[:, 2 + par, :], ACT.Sqrt, bias=EPS6[:]).then_inc(s_std, 1)
                for i in range(NT // 2):
                    act.wait_ge(s_vps, b * (NT // 2) + i + 1)
                    for t in range(2):
                        last = A(V[:, :, 2 * i + t, 0:DH], SP[:, i % 2, t * C:(t + 1) * C].rearrange("p (h d) -> p h d", h=HEADS),
                                 ACT.Copy, scale=S16)
                    last.then_inc(s_vh, 1)
                with act.Fori(0, HEADS) as h:
                    hh = b * HEADS + h
                    with act.Fori(0, NB // 2) as i:
                        for par in range(2):
                            col = bass.ds((i * 2 + par) * QB, QB)
                            wait_apart(act, s_qk, hh * NB + i * 2 + par + 1, s_passed)
                            A(QA[0:DH, col], SP[0:DH, par, :], ACT.Copy, scale=S16)
                            A(KA[0:DH, col], SP[DH:P, par, :], ACT.Copy, scale=QK).then_inc(s_qkh, 1)
                    with act.Fori(0, NB // 2) as i:
                        for par in range(2):
                            wait_apart(act, s_rw, hh * NB + i * 2 + par + 1, s_passed)
                            A(QA[DH:P, :].rearrange("p (h w) -> p w h", w=SIDE)[:, bass.ds((i * 2 + par) * ROWS, ROWS), :],
                              SP[0:DH, par, :].rearrange("p (w h) -> p w h", w=ROWS), ACT.Copy).then_inc(s_rwh, 1)
                    n0 = hh * NB
                    height_high(n0, 0)
                    exp_unit(n0, 0)
                    exp_unit(n0, 1)

                    def block_of(n, j, more):
                        for u in range(UNITS):
                            if u == UNITS - 2 and more:
                                height_high(n + 1, j + 1)
                            if u < UNITS - 2 or more:
                                exp_unit(n, u + 2)
                        act.wait_ge(s_pv, (n + 1) * UNITS + NBUF)
                        act.wait_ge(s_out, n)
                        for i in range(2):
                            last = A(PVS[:, 2 * i:2 * i + 2, :], PV[:, i, 0:2 * VW].rearrange("p (s v) -> p s v", s=2), ACT.Copy)
                        last.then_inc(s_pvs, 1)
                    with act.Fori(0, NB - 1) as j:
                        block_of(n0 + j, j, True)
                    block_of(n0 + NB - 1, NB - 1, False)
                act.wait_ge(s_mv, b + 1)
                A(RSTD[:], MV[:, :, 1], ACT.Sqrt, bias=EPS5[:]).then_inc(s_ts, 1)
                with act.Fori(0, NT // 2) as i:
                    for par in range(2):
                        m = b * NT + i * 2 + par
                        act.wait_ge(s_tx, m + 1)
                        A(XTT[:, par, :], SP[:, par, 0:C], ACT.Copy).then_inc(s_te, 1)

        @block.vector
        def _(dve):
            def low_unit(n, buf_unit):
                dve.wait_ge(s_e, n * UNITS + buf_unit + 1 + NBUF)
                nc.vector.tensor_tensor(PL[:, buf_unit % NBUF, :, :], PF[:, buf_unit % 2, :, :], PH[:, buf_unit % NBUF, :, :],
                                        ALU.subtract).then_inc(s_pl, 1)

            def reduce_unit(n, k):
                dve.wait_ge(s_mx, n * UNITS + k + 1)
                nc.vector.tensor_reduce(G[:, k // 4, (k % 4) * 16:(k % 4 + 1) * 16],
                                        MX[:].rearrange("p a (h w) -> p (a h) w", w=SIDE), AX.X, ALU.max).then_inc(s_mxr, 1)

            def row_maximum(n):
                dve.wait_ge(s_rh, n + 1)
                rh = MX[:, 0, 0:SUB * (SIDE + 1)].rearrange("p (s w) -> p s w", s=SUB)
                dve.wait_ge(s_mxr, (n + 1) * UNITS)
                nc.vector.scalar_tensor_tensor(G2[0:64], rh[0:64, :, 1:SIDE + 1], S16, G[0:64], ALU.mult, ALU.add)
                nc.vector.scalar_tensor_tensor(G2[64:P], rh[64:P, :, 0:SIDE], S16, G[64:P], ALU.mult, ALU.add).then_inc(s_g2, 1)
                dve.wait_ge(s_g2, n + 1)
                nc.vector.tensor_reduce(MROW[:], G2[:], AX.X, ALU.max).then_inc(s_mrow, 1)
                dve.wait_ge(s_mrow, n + 1)
                dve.wait_ge(s_diag, n)
                nc.vector.tensor_scalar(MNEG[:], MROW[:], -1.0 / S16, S16 * SHIFT, ALU.mult, ALU.add).then_inc(s_mneg, 1)

            def height_low(n, j):
                col = bass.ds(j * QB, QB)
                dve.wait_ge(s_rhh, n + 1)
                nc.vector.tensor_tensor(QD[:, col], MX[0:DH, 1, :], QC[DH:P, col], ALU.subtract).then_inc(s_rhl, 1)

            dve.wait_ge(s_rel, 1)
            nc.vector.tensor_tensor(RELL[:], REL[:], RELH[:], ALU.subtract).then_inc(s_rel, 1)
            with dve.Fori(0, BATCH) as b:
                def normalise(m, par, j):
                    dve.wait_ge(s_std, m + 1)
                    nc.vector.reciprocal(RS[:, par, :], RS[:, par, :]).then_inc(s_rstd, 1)
                    dve.wait_ge(s_rstd, m + 1)
                    for k in range(KC):
                        col = bass.ds(j * QB, QB)
                        last = nc.vector.tensor_tensor(XN[:, k, col], XN[:, k, col], RS[:, par, :], ALU.mult)
                    last.then_inc(s_xn, 1)
                with dve.Fori(0, NB // 2) as i:
                    for par in range(2):
                        m = b * NB + i * 2 + par
                        dve.wait_ge(s_mean, m + 1)
                        for k in range(KC):
                            col = bass.ds((i * 2 + par) * QB, QB)
                            last = nc.vector.tensor_tensor(XN[:, k, col], XN[:, k, col], SP[:, par, :], ALU.subtract)
                        last.then_inc(s_cent, 1)
                        normalise(m, par, i * 2 + par)
                for i in range(NT // 2):
                    dve.wait_ge(s_vh, b * (NT // 2) + i + 1)
                    for t in range(2):
                        last = nc.vector.scalar_tensor_tensor(
                            V[:, :, 2 * i + t, DH + 1:VW], SP[:, i % 2, t * C:(t + 1) * C].rearrange("p (h d) -> p h d", h=HEADS),
                            S16, V[:, :, 2 * i + t, 0:DH], ALU.mult, ALU.subtract)
                    last.then_inc(s_vl, 1)
                dve.wait_ge(s_t, (b + 1) * 16)
                for par in range(2):
                    wait_apart(dve, s_xd[par], b * (NT // 2 * 16), s_passed)
                with dve.Fori(0, HEADS) as h:
                    hh = b * HEADS + h
                    with dve.Fori(0, NB // 2) as i:
                        for par in range(2):
                            col = bass.ds((i * 2 + par) * QB, QB)
                            dve.wait_ge(s_qkh, hh * NB + i * 2 + par + 1)
                            nc.vector.scalar_tensor_tensor(QC[0:DH, col], SP[0:DH, par, :], S16, QA[0:DH, col], ALU.mult, ALU.subtract)
                            nc.vector.scalar_tensor_tensor(KB[0:DH, col], SP[DH:P, par, :], QK, KA[0:DH, col], ALU.mult,
                                                           ALU.subtract).then_inc(s_qkl, 1)
                    nc.vector.tensor_copy(VS[:, :, 0:VW], V[:, bass.ds(h, 1), :, 0:VW].rearrange("p o t v -> p (o t) v"))
                    nc.vector.tensor_copy(QBf[0:DH, :], QA[0:DH, :])
                    nc.vector.tensor_copy(KCC[0:DH, :], KA[0:DH, :]).then_inc(s_dup, 1)
                    with dve.Fori(0, NB // 2) as i:
                        for par in range(2):
                            def wide(t):
                                return t[DH:P, :].rearrange("p (h w) -> p w h", w=SIDE)[:, bass.ds((i * 2 + par) * ROWS, ROWS), :]
                            dve.wait_ge(s_rwh, hh * NB + i * 2 + par + 1)
                            nc.vector.tensor_tensor(wide(QBf), SP[0:DH, par, :].rearrange("p (w h) -> p w h", w=ROWS), wide(QA),
                                                    ALU.subtract).then_inc(s_rwl, 1)
                    n0 = hh * NB
                    for k in range(UNITS):
                        reduce_unit(n0, k)
                    row_maximum(n0)
                    height_low(n0, 0)
                    low_unit(n0, 0)

                    def block_of(n, j, more):
                        for u in range(UNITS):
                            if u < UNITS - 1 or more:
                                low_unit(n, u + 1)
                            if more:
                                for k in MAXU[u]:
                                    reduce_unit(n + 1, k)
                                if u == U_RH:
                                    row_maximum(n + 1)
                                if u == U_R:
                                    height_low(n + 1, j + 1)
                        dve.wait_ge(s_pvs, n + 1)
                        nc.vector.reciprocal(PVR[:], PVS[:, :, DH]).then_inc(s_pvr, 1)
                        nc.vector.tensor_tensor(PVO[:], PVS[:, :, 0:DH], PVS[:, :, DH + 1:VW], ALU.add).then_inc(s_pvo, 1)
                        dve.wait_ge(s_pvr, n + 1)
                        dve.wait_ge(s_pvo, n + 1)
                        for ns in range(SUB):
                            res = T[:, bass.ds(j * SUB + ns, 1), bass.ds(h * DH, DH)].rearrange("p o d -> p (o d)")
                            last = nc.vector.scalar_tensor_tensor(res, PVO[:, ns, :], PVR[:, ns:ns + 1], res, ALU.mult, ALU.add)
                        last.then_inc(s_out, 1)
                    with dve.Fori(0, NB - 1) as j:
                        block_of(n0 + j, j, True)
                    block_of(n0 + NB - 1, NB - 1, False)
                dve.wait_ge(s_out, (b + 1) * (HEADS * NB))
                for t in range(NT):
                    last = nc.vector.bn_stats(STAT[:, t, :], T[:, t, :])
                last.then_inc(s_st, 1)
                wait_apart(dve, s_st, b + 1, s_passed)
                for t in range(NT):
                    last = nc.vector.bn_aggr(MV[:, t, :], STAT[:, t, :])
                last.then_inc(s_mv, 1)
                dve.wait_ge(s_ts, b + 1)
                nc.vector.reciprocal(RSTD2[:], RSTD[:]).then_inc(s_tr, 1)
                wait_apart(dve, s_tr, b + 1, s_passed)

                with dve.Fori(0, NT // 2) as i:
                    for par in range(2):
                        m = b * NT + i * 2 + par
                        dve.wait_ge(s_xd[par], (b * (NT // 2) + i) * 16)
                        dve.wait_ge(s_lg, b * NT + i * 2)
                        t1 = bass.ds(i * 2 + par, 1)
                        nc.vector.tensor_scalar(XNT[:, par, :], T[:, t1, :].rearrange("p o c -> p (o c)"),
                                                MV[:, t1, 0], RSTD2[:, t1], ALU.subtract, ALU.mult).then_inc(s_tn, 1)
                    for par in range(2):
                        m = b * NT + i * 2 + par
                        dve.wait_ge(s_lg, m + 1)
                        nc.vector.tensor_copy(LG[:, bass.ds(m, 1), :].rearrange("p o e -> p (o e)"), MX[:, par, 0:EXPERTS])\
                          .then_inc(s_lge, 1)


def build(nc, xc, xt, whead, wv, hrt, wrt, onehots, ident, utri, iota_e, tok_ids, gate_w, gate_b, w1, b1, w2, b2, out):
    t_dram = nc.dram_tensor("t_dram", [TT, P, C], F32, kind="Internal").ap()
    xn_dram = nc.dram_tensor("xn_dram", [TT, P, C], F32, kind="Internal").ap()
    with ExitStack() as keep:
        LG = keep.enter_context(nc.sbuf_tensor("LG", [P, TT, EXPERTS], F32))
        with ExitStack() as ctx:
            attention_and_norm(nc, ctx, xc, xt, whead, wv, hrt, wrt, onehots, ident, gate_w, t_dram, xn_dram, LG)
        with ExitStack() as ctx:
            experts(nc, ctx, LG, ident, utri, iota_e, tok_ids, gate_b, w1, b1, w2, b2, t_dram, xn_dram, out)


def experts(nc, ctx, LG, ident, utri, iota_e, tok_ids, gate_b, w1, b1, w2, b2, t_dram, xn_dram, out):
    slot_tok = nc.dram_tensor("slot_tok", [SLOTS, 1], I32, kind="Internal").ap()
    y_dram = nc.dram_tensor("y_dram", [SLOTS, C], F32, kind="Internal").ap()
    XS, WS, HS = 16.0, 256.0, 16.0
    NXG = 5
    NPC = 8
    PIECE = KC * FF // NPC
    NTB = TT // 4

    def sb(name, shape, dt):
        return ctx.enter_context(nc.sbuf_tensor(name, shape, dt))

    def sem(name):
        return ctx.enter_context(nc.semaphore(name))

    UT = sb("UT", [P, P], F32)
    ONE = sb("ONE", [P, P], F32)
    ID = sb("ID", [P, P], F32)
    GB = sb("GB", [P, EXPERTS], F32)
    IE = sb("IE", [P, EXPERTS], F32)
    IDS = sb("IDS", [P, TT], I32)
    SH = sb("SH", [P, TT, EXPERTS], F32)
    EX = sb("EX", [P, TT, EXPERTS], F32)
    CA = sb("CA", [P, TT, EXPERTS], F32)
    OH = sb("OH", [P, TT, EXPERTS], F32)
    CUM = sb("CUM", [P, EXPERTS, TT], F32)
    TOTS = sb("TOTS", [P, TT, EXPERTS], F32)
    ONES_T = sb("ONES_T", [P, TT], F32)
    POS = sb("POS", [P, TT, EXPERTS], F32)
    r = {k: sb("r_" + k, [P, TT], F32) for k in
         ("max", "sum", "prob", "code", "pos", "kept", "base", "keep_slot", "drop", "scatter", "posc", "gather", "w")}
    SCAT = sb("SCAT", [P, TT], I32)
    GATH = sb("GATH", [P, TT], I32)
    ZERO = sb("ZERO", [P, SLOTS // P], I32)
    SLOT = sb("SLOT", [P, SLOTS // P], I32)
    PS = ctx.enter_context(nc.psum_tensor("PS", [P, 8, 512], F32))
    TRP, HP, YP = PS[:, 0:2, :], PS[:, 2:5, :], PS[:, 5:8, :]

    s_c = sem("r_const")
    s_m = sem("r_ones")
    s_v = sem("r_chain")
    s_ex = sem("r_exp")
    s_oh = sem("r_onehot")
    s_cnt = sem("r_count")
    s_slots = sem("r_slots")
    s_zero = sem("r_zero")
    s_sc = sem("r_scatter")
    s_idx = sem("r_index")

    with nc.Block() as block:
        @block.sync
        def _(sp):
            sp.dma_start(UT[:], utri).then_inc(s_c, 16)
            sp.dma_start(ID[:], ident).then_inc(s_c, 16)
            sp.dma_start(GB[:], gate_b.partition_broadcast(P)).then_inc(s_c, 16)
            sp.dma_start(IE[:], iota_e).then_inc(s_c, 16)
            sp.dma_start(IDS[:], tok_ids).then_inc(s_c, 16)
            sp.wait_ge(s_m, 1)
            sp.dma_start(slot_tok.rearrange("(p t) o -> p (t o)", p=P), ZERO[:]).then_inc(s_zero, 16)
            sp.wait_ge(s_sc, TT * 16)
            sp.dma_start(SLOT[:], slot_tok.rearrange("(t p) o -> p (t o)", p=P), allow_slow_non_contiguous=True).then_inc(s_idx, 16)
            sp.wait_ge(s_idx, 16)

        @block.gpsimd
        def _(pool):
            nc.gpsimd.memset(ONE[:], 1.0)
            nc.gpsimd.memset(ONES_T[:], 1.0)
            nc.gpsimd.memset(ZERO[:], 0).then_inc(s_m, 1)
            pool.wait_ge(s_slots, 1)
            pool.wait_ge(s_zero, 16)
            for tt in range(TT):
                nc.gpsimd.indirect_dma_start(slot_tok, bass.IndirectOffsetOnAxis(ap=SCAT[:, tt:tt + 1], axis=0),
                                             IDS[:, tt:tt + 1], None, bounds_check=SLOTS - 1, oob_is_err=False)\
                  .then_inc(s_sc, 16)
            pool.wait_ge(s_sc, TT * 16)

        @block.scalar
        def _(act):
            act.wait_ge(s_v, 3)
            nc.scalar.activation(EX[:], SH[:], ACT.Exp).then_inc(s_ex, 1)

        @block.tensor
        def _(pe):
            pe.wait_ge(s_c, 5 * 16)
            pe.wait_ge(s_m, 1)
            pe.wait_ge(s_oh, 1)
            oh = OH[:].rearrange("p t e -> p (t e)")
            nc.tensor.matmul(PS[:, 0, :], UT[:], oh, start=True, stop=True)
            nc.tensor.matmul(PS[:, 1, :], ONE[:], oh, start=True, stop=True).then_inc(s_cnt, 1)

        @block.vector
        def _(dve):
            steps = [0]

            def link(ins):
                steps[0] += 1
                ins.then_inc(s_v, 1)
                dve.wait_ge(s_v, steps[0])

            def wide(a):
                return a[:].unsqueeze(2).broadcast_to([P, TT, EXPERTS])

            def per_tile(a):
                return a[:].unsqueeze(1).broadcast_to([P, TT, EXPERTS])
            V_ = nc.vector
            dve.wait_ge(s_c, 5 * 16)
            dve.wait_ge(s_m, 1)
            link(V_.tensor_tensor(SH[:], LG[:], per_tile(GB), ALU.add))
            link(V_.tensor_reduce(r["max"][:], SH[:], AX.X, ALU.max))
            link(V_.tensor_tensor(SH[:], SH[:], wide(r["max"]), ALU.subtract))
            dve.wait_ge(s_ex, 1)
            link(V_.tensor_reduce(r["sum"][:], EX[:], AX.X, ALU.add))
            link(V_.reciprocal(r["prob"][:], r["sum"][:]))
            link(V_.scalar_tensor_tensor(CA[:], SH[:], 0.0, per_tile(IE), ALU.is_ge, ALU.mult))
            link(V_.tensor_reduce(r["code"][:], CA[:], AX.X, ALU.max))
            steps[0] += 0
            V_.tensor_tensor(OH[:], CA[:], wide(r["code"]), ALU.is_equal).then_inc(s_oh, 1)
            dve.wait_ge(s_oh, 1)
            dve.wait_ge(s_cnt, 1)
            link(V_.tensor_copy(TOTS[:], PS[:, 1, :].rearrange("p (t e) -> p t e", e=EXPERTS)))
            for e in range(EXPERTS):
                last = V_.tensor_tensor_scan(CUM[:, e, :], ONES_T[:], TOTS[:, :, e], 0.0, ALU.mult, ALU.add)
            link(last)
            link(V_.tensor_tensor(POS[:], CUM[:].rearrange("p e t -> p t e"), TOTS[:], ALU.subtract))
            link(V_.tensor_tensor(CA[:], PS[:, 0, :].rearrange("p (t e) -> p t e", e=EXPERTS), POS[:], ALU.add))
            link(V_.tensor_tensor(POS[:], CA[:], OH[:], ALU.mult))
            link(V_.tensor_reduce(r["pos"][:], POS[:], AX.X, ALU.add))
            link(V_.tensor_scalar(r["kept"][:], r["pos"][:], float(CAP), None, ALU.is_lt))
            link(V_.tensor_scalar(r["base"][:], r["code"][:], -float(CAP), float(EXPERTS * CAP), ALU.mult, ALU.add))
            link(V_.tensor_tensor(r["keep_slot"][:], r["base"][:], r["pos"][:], ALU.add))
            link(V_.tensor_scalar(r["drop"][:], r["kept"][:], -float(2 * SLOTS), float(2 * SLOTS), ALU.mult, ALU.add))
            link(V_.tensor_tensor(r["scatter"][:], r["keep_slot"][:], r["drop"][:], ALU.add))
            link(V_.tensor_scalar(r["posc"][:], r["pos"][:], float(CAP - 1), None, ALU.min))
            link(V_.tensor_tensor(r["gather"][:], r["base"][:], r["posc"][:], ALU.add))
            link(V_.tensor_tensor(r["w"][:], r["prob"][:], r["kept"][:], ALU.mult))
            V_.tensor_copy(SCAT[:], r["scatter"][:])
            V_.tensor_copy(GATH[:], r["gather"][:]).then_inc(s_slots, 1)

    xg = ctx.enter_context(ExitStack())

    def sbx(name, shape, dt):
        return xg.enter_context(nc.sbuf_tensor(name, shape, dt))
    W1F = sbx("W1F", [P, KC * FF], F32)
    W2F = sbx("W2F", [P, KF * C], F32)
    W1P = [sbx(f"W1P{i}", [P, 2, KC * FF], F16) for i in range(2)]
    W2P = [sbx(f"W2P{i}", [P, 2, KF * C], F16) for i in range(2)]
    B1F = sbx("B1F", [P, EXPERTS, KF], F32)
    B1 = sbx("B1", [P, EXPERTS, KF], F32)
    B2 = sbx("B2", [P, EXPERTS, C], F32)
    SLOTC = sbx("SLOTC", [P, 2, ST], I32)
    XG = sbx("XG", [P, NXG, C], F32)
    XTH = sbx("XTH", [P, 2, KC, CAP], F16)
    XTL = sbx("XTL", [P, 2, KC, CAP], F16)
    HH = sbx("HH", [P, 3, KF, 512], F16)
    HL = sbx("HL", [P, 3, KF, 512], F16)
    HF = sbx("HF", [P, 2, 512], F32)
    YS = sbx("YS", [P, NXG, C], F32)

    s_passed = sem("e_passed")
    s_b = sem("e_bias")
    s_b1 = sem("e_bias_scaled")
    s_w = sem("e_weights")
    s_wh = sem("e_w_high")
    s_wl = sem("e_w_low")
    s_xg = [sem(f"e_gathered{i}") for i in range(NXG)]
    s_ic = sem("e_index")
    s_xt = sem("e_turned")
    s_xh = sem("e_x_high")
    s_xl = sem("e_x_low")
    s_h = sem("e_hidden")
    s_hh = sem("e_h_high")
    s_hl = sem("e_h_low")
    s_y = sem("e_y")
    s_ye = sem("e_y_out")
    s_yd = [sem(f"e_y_dram{i}") for i in range(NXG)]
    NCH = len(CHUNKS)
    HU = NCH * KF

    with nc.Block() as block:
        def each_expert(eng, body):
            with eng.Fori(0, EXPERTS // 2 - 1) as i:
                body(i * 2, 0, True)
                body(i * 2 + 1, 1, True)
            body(EXPERTS - 2, 0, True)
            body(EXPERTS - 1, 1, False)

        @block.sync
        def _(sp):
            sp.dma_start(B1F[:], b1).then_inc(s_b, 16)
            sp.dma_start(B2[:], b2.rearrange("e c -> (e c)").partition_broadcast(P).rearrange("p (e c) -> p e c", c=C))\
              .then_inc(s_b, 16)

            def load(m):
                sp.dma_start(W1F[:].rearrange("p (k f) -> p k f", k=KC), w1[m].rearrange("(k p) f -> p k f", p=P)).then_inc(s_w, 16)
                sp.dma_start(W2F[:].rearrange("p (k c) -> p k c", k=KF), w2[m].rearrange("(k p) c -> p k c", p=P)).then_inc(s_w, 16)

            def load_next(m):
                sp.wait_ge(s_wl, m * (2 * NPC))
                sp.dma_start(W1F[:].rearrange("p (k f) -> p k f", k=KC),
                             w1[bass.ds(m, 1)].rearrange("o (k p) f -> p (o k) f", p=P)).then_inc(s_w, 16)
                sp.dma_start(W2F[:].rearrange("p (k c) -> p k c", k=KF),
                             w2[bass.ds(m, 1)].rearrange("o (k p) c -> p (o k) c", p=P)).then_inc(s_w, 16)

            def stores(m, lo, hi):
                for s in range(lo, hi):
                    sp.wait_ge(s_ye, m * ST + s + 1)
                    sp.dma_start(y_dram[bass.ds(m * CAP + s * P, P), :], YS[:, s % NXG, :]).then_inc(s_yd[s % NXG], 16)

            load(0)
            load_next(1)

            def body(m, par, more):
                stores(m, 0, CHUNKS[0][1])
                if more and not (isinstance(m, int) and m + 2 >= EXPERTS):
                    load_next(m + 2)
                stores(m, CHUNKS[0][1], ST)
            each_expert(sp, body)
            for i in range(NXG):
                sp.wait_ge(s_yd[i], EXPERTS * (ST // NXG) * 16)

        @block.gpsimd
        def _(pool):
            xn = xn_dram.rearrange("t p c -> (t p) c")

            def gathers(m, par):
                wait_apart(pool, s_xt, m * ST, s_passed)
                nc.gpsimd.tensor_copy(SLOTC[:, par, :], SLOT[:, bass.ds(m * ST, ST)]).then_inc(s_ic, 1)
                wait_apart(pool, s_ic, m + 1, s_passed)
                for s in range(ST):
                    wait_apart(pool, s_xt, m * ST + s + 1, s_passed)
                    nc.gpsimd.indirect_dma_start(XG[:, s % NXG, :], None, xn,
                                                 bass.IndirectOffsetOnAxis(ap=SLOTC[:, par, s:s + 1], axis=0),
                                                 bounds_check=TT * P - 1, oob_is_err=False).then_inc(s_xg[s % NXG], 16)
            with pool.Fori(0, EXPERTS // 2) as i:
                gathers(i * 2, 0)
                gathers(i * 2 + 1, 1)

        @block.tensor
        def _(pe):
            mm = nc.tensor.matmul
            pe.sem_inc(s_xt, NXG)
            pe.sem_inc(s_y, ST)
            pe.sem_inc(s_hh, 3)

            def body(m, par, more):
                for s in range(ST):
                    pe.wait_ge(s_xg[s % NXG], (m * (ST // NXG) + s // NXG + 1) * 16)
                    if s >= 2:
                        pe.wait_ge(s_xl, m * ST + s - 1)
                    else:
                        pe.wait_ge(s_xl, m * ST)
                    for k in range(KC):
                        last = nc.tensor.transpose(TRP[:, s % 2, k * P:(k + 1) * P], XG[:, s % NXG, k * P:(k + 1) * P], ID[:])
                    last.then_inc(s_xt, 1)
                pe.wait_ge(s_wl, (m + 1) * (2 * NPC))
                pe.wait_ge(s_xl, (m + 1) * ST)
                w1p = W1P[par][:].rearrange("p a (k f) -> p a k f", k=KC)
                w2p = W2P[par][:].rearrange("p a (k c) -> p a k c", k=KF)

                def hidden(c):
                    t0, nt = CHUNKS[c]
                    sl = slice(t0 * P, (t0 + nt) * P)
                    for f in range(KF):
                        g = c * KF + f
                        pe.wait_ge(s_hh, m * HU + g + 1)
                        out = HP[:, g % 3, 0:nt * P]
                        fs = slice(f * P, (f + 1) * P)
                        for k in range(KC):
                            mm(out, w1p[:, 0, k, fs], XTH[:, par, k, sl], start=(k == 0), stop=False)
                            mm(out, w1p[:, 1, k, fs], XTH[:, par, k, sl], start=False, stop=False)
                            last = mm(out, w1p[:, 0, k, fs], XTL[:, par, k, sl], start=False, stop=(k == KC - 1))
                        last.then_inc(s_h, 1)

                def rows(c):
                    t0, nt = CHUNKS[c]
                    pe.wait_ge(s_hl, m * HU + (c + 1) * KF)
                    for t in range(nt):
                        s = t0 + t
                        if s >= 3:
                            pe.wait_ge(s_ye, m * ST + s - 2)
                        else:
                            pe.wait_ge(s_ye, m * ST)
                        out = YP[:, s % 3, 0:C]
                        for f in range(KF):
                            hs = slice(t * P, (t + 1) * P)
                            mm(out, HH[:, c, f, hs], w2p[:, 0, f, :], start=(f == 0), stop=False)
                            mm(out, HH[:, c, f, hs], w2p[:, 1, f, :], start=False, stop=False)
                            last = mm(out, HL[:, c, f, hs], w2p[:, 0, f, :], start=False, stop=(f == KF - 1))
                        last.then_inc(s_y, 1)
                hidden(0)
                hidden(1)
                rows(0)
                hidden(2)
                rows(1)
                rows(2)
            each_expert(pe, body)

        def piece(buf, par, part, q):
            src, dst = (W1F, W1P[par]) if q < NPC else (W2F, W2P[par])
            sl = slice((q % NPC) * PIECE, (q % NPC + 1) * PIECE)
            return src[:, sl], dst[:, part, sl]

        @block.scalar
        def _(act):
            A = nc.scalar.activation

            def split_high(m, par, q):
                act.wait_ge(s_w, (m + 1) * 32)
                act.wait_ge(s_y, m * ST)
                src, dst = piece(None, par, 0, q)
                A(dst, src, ACT.Copy, scale=WS).then_inc(s_wh, 1)

            act.wait_ge(s_b, 32)
            A(B1[:], B1F[:], ACT.Copy, scale=HS).then_inc(s_b1, 1)
            act.wait_ge(s_b1, 1)
            for q in range(2 * NPC):
                split_high(0, 0, q)

            def body(m, par, more):
                for s in range(ST):
                    act.wait_ge(s_xt, m * ST + s + 1 + NXG)
                    A(XTH[:, par, :, s * P:(s + 1) * P], TRP[:, s % 2, 0:C].rearrange("p (k n) -> p k n", k=KC), ACT.Copy,
                      scale=XS).then_inc(s_xh, 1)
                for c in range(NCH):
                    t0, nt = CHUNKS[c]
                    act.wait_ge(s_y, m * ST + t0 + nt)
                    for f in range(KF):
                        g = c * KF + f
                        wait_apart(act, s_h, m * HU + g + 1, s_passed)
                        src = HP[:, g % 3, 0:nt * P]
                        bias = B1[:, bass.ds(m, 1), f]
                        A(HH[:, c, f, 0:nt * P], src, ACT.Relu, bias=bias, scale=HS / (XS * WS))
                        wait_apart(act, s_hl, m * HU + max(g - 1, 0), s_passed)
                        A(HF[:, g % 2, 0:nt * P], src, ACT.Relu, bias=bias, scale=HS / (XS * WS)).then_inc(s_hh, 1)
                        if more and g < 2 * NPC:
                            split_high(m + 1, 1 - par, g)
            each_expert(act, body)

        @block.vector
        def _(dve):
            V_ = nc.vector

            def split_low(m, par, q):
                dve.wait_ge(s_wh, m * (2 * NPC) + q + 1)
                src, lo = piece(None, par, 1, q)
                _, hi = piece(None, par, 0, q)
                V_.scalar_tensor_tensor(lo, src, WS, hi, ALU.mult, ALU.subtract).then_inc(s_wl, 1)

            for q in range(2 * NPC):
                split_low(0, 0, q)

            def body(m, par, more):
                for s in range(ST):
                    dve.wait_ge(s_xh, m * ST + s + 1)
                    V_.scalar_tensor_tensor(XTL[:, par, :, s * P:(s + 1) * P],
                                            TRP[:, s % 2, 0:C].rearrange("p (k n) -> p k n", k=KC), XS,
                                            XTH[:, par, :, s * P:(s + 1) * P], ALU.mult, ALU.subtract).then_inc(s_xl, 1)

                def low(c):
                    t0, nt = CHUNKS[c]
                    for f in range(KF):
                        g = c * KF + f
                        dve.wait_ge(s_hh, m * HU + g + 1 + 3)
                        V_.tensor_tensor(HL[:, c, f, 0:nt * P], HF[:, g % 2, 0:nt * P], HH[:, c, f, 0:nt * P],
                                         ALU.subtract).then_inc(s_hl, 1)
                        if more and g < 2 * NPC:
                            split_low(m + 1, 1 - par, g)

                def rows(c):
                    t0, nt = CHUNKS[c]
                    for s in range(t0, t0 + nt):
                        dve.wait_ge(s_y, m * ST + s + 1 + ST)
                        dve.wait_ge(s_yd[s % NXG], (m * (ST // NXG) + s // NXG) * 16)
                        V_.scalar_tensor_tensor(YS[:, s % NXG, :], YP[:, s % 3, 0:C], 1.0 / (HS * WS),
                                                B2[:, bass.ds(m, 1), :].rearrange("p o c -> p (o c)"), ALU.mult, ALU.add)\
                          .then_inc(s_ye, 1)
                low(0)
                low(1)
                rows(0)
                low(2)
                rows(1)
                rows(2)
            dve.wait_ge(s_b, 32)
            each_expert(dve, body)
    xg.close()

    combine(nc, ctx, GATH, r["w"], y_dram, t_dram, out)


def combine(nc, ctx, GATH, WT, y_dram, t_dram, out):
    FMAX = 3.4028234663852886e38
    GRP = 4
    NG = TT // GRP
    NBF = 2

    def sb(name, shape, dt):
        return ctx.enter_context(nc.sbuf_tensor(name, shape, dt))

    def sem(name):
        return ctx.enter_context(nc.semaphore(name))
    Y = sb("Y", [P, NBF, GRP, C], F32)
    TX = sb("TX", [P, NBF, GRP, C], F32)
    PP = sb("PP", [P, NBF, GRP, C], F32)
    NN = sb("NN", [P, NBF, GRP, C], F32)
    MP = sb("MP", [P, NBF, GRP, C], I32)
    MN = sb("MN", [P, NBF, GRP, C], I32)
    GATHC = sb("GATHC", [P, NBF, GRP], I32)
    LIM = sb("LIM", [P, 2, GRP, C], F32)
    s_g = [sem(f"c_rows{i}") for i in range(NBF)]
    s_t = [sem(f"c_t{i}") for i in range(NBF)]
    s_o = [sem(f"c_out{i}") for i in range(NBF)]
    s_passed = sem("c_passed")
    s_ic = sem("c_index")
    s_lim = sem("c_lim")
    s_pn = sem("c_posneg")
    s_mk = sem("c_mask")
    s_fx = sem("c_fixed")
    s_ta = sem("c_added")
    s_f = sem("c_final")

    with nc.Block() as block:
        @block.sync
        def _(sp):
            with sp.Fori(0, NG // NBF) as i:
                for b in range(NBF):
                    sp.wait_ge(s_o[b], i * 16)
                    sp.dma_start(TX[:, b], t_dram[bass.ds((i * NBF + b) * GRP, GRP)].rearrange("t p c -> p t c")).then_inc(s_t[b], 16)

        @block.scalar
        def _(act):
            with act.Fori(0, NG // NBF) as i:
                for b in range(NBF):
                    act.wait_ge(s_f, i * NBF + b + 1)
                    act.dma_start(out[bass.ds((i * NBF + b) * GRP, GRP)].rearrange("t p c -> p t c"), TX[:, b]).then_inc(s_o[b], 16)
            for b in range(NBF):
                act.wait_ge(s_o[b], NG // NBF * 16)

        @block.gpsimd
        def _(pool):
            nc.gpsimd.memset(LIM[:, 0], 10000.0)
            nc.gpsimd.memset(LIM[:, 1], -10000.0).then_inc(s_lim, 1)
            with pool.Fori(0, NG // NBF) as i:
                for b in range(NBF):
                    wait_apart(pool, s_f, i * NBF, s_passed)
                    nc.gpsimd.tensor_copy(GATHC[:, b, :], GATH[:, bass.ds((i * NBF + b) * GRP, GRP)]).then_inc(s_ic, 1)
                    wait_apart(pool, s_ic, i * NBF + b + 1, s_passed)
                    for g in range(GRP):
                        nc.gpsimd.indirect_dma_start(Y[:, b, g, :], None, y_dram,
                                                     bass.IndirectOffsetOnAxis(ap=GATHC[:, b, g:g + 1], axis=0),
                                                     bounds_check=SLOTS - 1, oob_is_err=False).then_inc(s_g[b], 16)

        @block.vector
        def _(dve):
            V_ = nc.vector
            dve.wait_ge(s_lim, 1)
            with dve.Fori(0, NG // NBF) as i:
                for b in range(NBF):
                    n = i * NBF + b
                    dve.wait_ge(s_g[b], (i + 1) * (16 * GRP))
                    for g in range(GRP):
                        w = WT[:, bass.ds(n * GRP + g, 1)]
                        V_.tensor_scalar(PP[:, b, g, :], Y[:, b, g, :], w, 0.0, ALU.mult, ALU.max)
                        last = V_.tensor_scalar(NN[:, b, g, :], Y[:, b, g, :], w, 0.0, ALU.mult, ALU.min)
                    last.then_inc(s_pn, 1)
                    dve.wait_ge(s_pn, n + 1)
                    V_.tensor_scalar(MP[:, b], PP[:, b], FMAX, None, ALU.is_gt)
                    V_.tensor_scalar(MN[:, b], NN[:, b], -FMAX, None, ALU.is_lt).then_inc(s_mk, 1)
                    wait_apart(dve, s_mk, n + 1, s_passed)
                    V_.copy_predicated(PP[:, b], MP[:, b], LIM[:, 0])
                    V_.copy_predicated(NN[:, b], MN[:, b], LIM[:, 1]).then_inc(s_fx, 1)
                    dve.wait_ge(s_fx, n + 1)
                    dve.wait_ge(s_t[b], (i + 1) * 16)
                    V_.tensor_tensor(TX[:, b], TX[:, b], PP[:, b], ALU.add).then_inc(s_ta, 1)
                    dve.wait_ge(s_ta, n + 1)
                    V_.tensor_tensor(TX[:, b], TX[:, b], NN[:, b], ALU.add).then_inc(s_f, 1)


def kernel(**inputs):
    import numpy as np
    import concourse.bacc as bacc
    from concourse.bass_utils import run_bass_kernel_spmd

    nc = bacc.Bacc("TRN2", target_bir_lowering=False, num_devices=1)
    x = np.asarray(inputs["x"]).reshape(BATCH, C, TOK)
    qkv = np.asarray(inputs["L0_conv_qkv_w"])
    heads = qkv.reshape(3, HEADS, DH, C)
    col = np.arange(TOK) % SIDE
    row = np.arange(TOK) // SIDE
    side = np.arange(SIDE)[:, None]
    arrays = {
        "xc": x,
        "xt": x.transpose(0, 2, 1),
        "whead": heads[:2].transpose(1, 3, 0, 2).reshape(HEADS, C, 2 * DH),
        "wv": heads[2].transpose(2, 0, 1).reshape(C, HEADS * DH),
        "hrt": np.asarray(inputs["L0_conv_height_rel"]).T,
        "wrt": np.asarray(inputs["L0_conv_width_rel"]).T,
        "onehots": (S16 * np.stack([side == col, side == row])).astype(np.float16),
        "ident": np.eye(P, dtype=np.float32),
        "utri": np.triu(np.ones((P, P), np.float32), 1),
        "iota_e": np.tile(np.arange(EXPERTS, 0, -1, dtype=np.float32), (P, 1)),
        "tok_ids": (np.arange(TT)[None, :] * P + np.arange(P)[:, None]).astype(np.int32),
        "gate_w": np.asarray(inputs["L0_ffn_gate_w"]),
        "gate_b": np.asarray(inputs["L0_ffn_gate_b"]),
        "w1": np.asarray(inputs["L0_ffn_w1"]),
        "b1": np.asarray(inputs["L0_ffn_b1"]).reshape(EXPERTS, KF, P).transpose(2, 0, 1),
        "w2": np.asarray(inputs["L0_ffn_w2"]),
        "b2": np.asarray(inputs["L0_ffn_b2"]),
    }
    feeds, args = {}, []
    for name, a in arrays.items():
        a = np.ascontiguousarray(a)
        feeds["in_" + name] = a
        args.append(nc.dram_tensor("in_" + name, a.shape, mybir.dt.from_np(a.dtype), kind="ExternalInput").ap())
    out = nc.dram_tensor("out_dram", (TT, P, C), F32, kind="ExternalOutput").ap()
    build(nc, *args, out)
    r = run_bass_kernel_spmd(nc, [feeds], core_ids=[0])
    y = r.results[0]["out_dram"].reshape(BATCH, TOK, C).transpose(0, 2, 1)
    return np.ascontiguousarray(y).reshape(BATCH, C, SIDE, SIDE)
```

```python
import concourse.bass as bass
from concourse import mybir
from contextlib import ExitStack

F32 = mybir.dt.float32
F16 = mybir.dt.float16
I32 = mybir.dt.int32
U32 = mybir.dt.uint32
ALU = mybir.AluOpType
ACT = mybir.ActivationFunctionType
AX = mybir.AxisListType

P = 128
BATCH, C, SIDE = 2, 256, 64
TOK = SIDE * SIDE
HEADS, DH = 4, 64
KC = C // P
NT = TOK // P
QB = 512
NB = TOK // QB
SUB = QB // P
ROWS = QB // SIDE
UNITS = TOK // (2 * P)
NBUF = 4
VW = 2 * DH + 1
WIN = 2 * SIDE - 1
WINP = SIDE - 1 + P

EXPERTS, FF, CAP = 8, 1024, 1280
TT = BATCH * NT
ST = CAP // P
SLOTS = EXPERTS * CAP
KF = FF // P
CHUNKS = [(0, 4), (4, 3), (7, 3)]

S16 = 16.0
QK = S16 * DH ** -0.5
SHIFT = 7.0

HALVES = 2 * UNITS
MAXH = [[] for _ in range(UNITS)]
for _k in range(HALVES):
    MAXH[_k * 12 // HALVES].append(_k)
U_CHAIN = 12
START = 1


def wait_apart(eng, sem, count, passed):
    eng.wait_ge(sem, count)
    eng.sem_inc(passed, 1)


def attention_and_norm(nc, ctx, xc, xt, whead, wv, hrt, wrt, onehots, ident_h, utri, iota_e, gate_w, gate_b, t_dram, xn_dram,
                       slot_tab, y_dram, GATH):
    def sb(name, shape, dt):
        return ctx.enter_context(nc.sbuf_tensor(name, shape, dt))

    def sem(name):
        return ctx.enter_context(nc.semaphore(name))

    XN = sb("XN", [P, KC, TOK], F32)
    T = sb("T", [P, NT, C], F32)
    V = sb("V", [P, HEADS, NT, VW + 1], F16)
    VS = sb("VS", [P, NT, VW + 1], F16)
    QA = sb("QA", [P, TOK], F16)
    QBf = sb("QBf", [P, TOK], F16)
    QC = [sb(f"QC{i}", [P, TOK], F16) for i in range(2)]
    KA = sb("KA", [P, TOK], F16)
    KB = sb("KB", [P, TOK], F16)
    KCC = sb("KCC", [P, TOK], F16)
    PH = sb("PH", [P, NBUF, 2, QB], F16)
    PL = sb("PL", [P, NBUF, 2, QB], F16)
    PF = sb("PF", [P, 2, 2, QB], F32)
    WH = sb("WH", [P, KC, 2 * DH], F32)
    WV = sb("WV", [P, KC, HEADS * DH], F32)
    RELH = sb("RELH", [DH, 2, WINP], F16)
    RELL = sb("RELL", [DH, 2, WINP], F16)
    G = sb("G", [P, SUB, SIDE], F32)
    G2 = sb("G2", [P, SUB, SIDE], F32)
    MROW = sb("MROW", [P, SUB], F32)
    MNEG = sb("MNEG", [P, SUB], F32)
    DIAG = sb("DIAG", [P, SUB, P], F16)
    IDH = sb("IDH", [P, P], F16)
    IDF = sb("IDF", [P, P], F32)
    ONEH = sb("ONEH", [P, P], F16)
    AVG = sb("AVG", [P, P], F32)
    PVS = sb("PVS", [P, SUB, VW], F32)
    PVR = sb("PVR", [P, SUB], F32)
    PVO = G2
    EPS6 = sb("EPS6", [P, 1], F32)
    EPS5 = sb("EPS5", [P, 1], F32)
    MV = sb("MV", [P, NT, 2], F32)
    RSTD = sb("RSTD", [P, NT], F32)
    RSTD2 = sb("RSTD2", [P, NT], F32)
    PLF = PL[:].rearrange("p a b n -> p (a b n)").bitcast(F32)
    XNT = PLF[:, 0:4 * C].rearrange("p (a c) -> p a c", a=4)
    REL = PLF[0:DH, 0:2 * WINP].rearrange("p (a w) -> p a w", a=2)
    XTT = PLF[:, 4 * C:6 * C].rearrange("p (a c) -> p a c", a=2)
    STAT = PLF[:, 6 * C:6 * C + 6 * NT].rearrange("p (t s) -> p t s", s=6)
    GW = sb("GW", [P, KC, EXPERTS], F32)
    SQ = PF
    RS = PH[:, 0:2, :, :].rearrange("p a b n -> p a (b n)").bitcast(F32)

    SP = ctx.enter_context(nc.psum_tensor("SP", [P, 4, 512], F32))
    MX = ctx.enter_context(nc.psum_tensor("MX", [P, 2, 512], F32))
    PV = ctx.enter_context(nc.psum_tensor("PV", [P, 2, 512], F32))

    NG4 = 4
    UT = sb("UT", [P, P], F32)
    ONE = sb("ONE", [P, P], F32)
    GB = sb("GB", [P, EXPERTS], F32)
    IE = sb("IE", [P, EXPERTS], F32)
    IDS = sb("IDS", [P, TT], I32)
    LG = sb("LG", [P, NT, EXPERTS], F32)
    CNT = sb("CNT", [P, EXPERTS], F32)
    ONES_T = sb("ONES_T", [P, NT], F32)
    SCAT = sb("SCAT", [P, NT], I32)
    IDW = sb("IDW", [P, NT, 2], I32)
    ZERO = PH[:].rearrange("p a b n -> p (a b n)").bitcast(I32)[:, 1024:1024 + C]
    PFF = PF[:].rearrange("p a b n -> p (a b n)")
    EX, CA, OH, TOTS, POS = (PFF[:, i * NT * EXPERTS:(i + 1) * NT * EXPERTS].rearrange("p (t e) -> p t e", e=EXPERTS)
                             for i in range(5))
    CUM = PFF[:, 5 * NT * EXPERTS:6 * NT * EXPERTS].rearrange("p (e t) -> p e t", e=EXPERTS)
    RTAB = sb("RTAB", [P, 10, NT], F32)
    RNAMES = ("max", "sum", "prob", "code", "pos", "kept", "rel", "rel2", "slot", "w")

    def R_(name):
        return RTAB[:, RNAMES.index(name), :]

    s_passed = sem("s_passed")
    s_zero = sem("s_zero")
    s_ids = sem("s_ids")
    s_v = sem("s_v")
    s_sh = sem("s_sh")
    s_ex = sem("s_ex")
    s_oh = sem("s_oh")
    s_cnt = sem("s_cnt")
    s_slots = sem("s_slots")
    s_sc = sem("s_sc")
    s_scd = sem("s_scd")
    s_const = sem("s_const")
    s_ones = sem("s_ones")
    s_rel = sem("s_rel")
    s_x = sem("s_x")
    s_t = sem("s_t")
    s_wh = sem("s_wh")
    s_mean = sem("s_mean")
    s_cent = sem("s_cent")
    s_sq = sem("s_sq")
    s_var = sem("s_var")
    s_std = sem("s_std")
    s_rstd = sem("s_rstd")
    s_xn = sem("s_xn")
    s_vps = sem("s_vps")
    s_vh = sem("s_vh")
    s_vl = sem("s_vl")
    s_qk = sem("s_qk")
    s_qkh = sem("s_qkh")
    s_qkl = sem("s_qkl")
    s_dup = sem("s_dup")
    s_rw = sem("s_rw")
    s_rwh = sem("s_rwh")
    s_rwl = sem("s_rwl")
    s_mx = sem("s_mx")
    s_mxr = sem("s_mxr")
    s_rh = sem("s_rh")
    s_g2 = sem("s_g2")
    s_mrow = sem("s_mrow")
    s_mneg = sem("s_mneg")
    s_diag = sem("s_diag")
    s_r = sem("s_r")
    s_rhh = sem("s_rhh")
    s_rhl = sem("s_rhl")
    s_s = sem("s_s")
    s_e = sem("s_e")
    s_pl = sem("s_pl")
    s_pv = sem("s_pv")
    s_pvs = sem("s_pvs")
    s_pvr = sem("s_pvr")
    s_pvo = sem("s_pvo")
    s_out = sem("s_out")
    s_st = sem("s_st")
    s_mv = sem("s_mv")
    s_ts = sem("s_ts")
    s_tr = sem("s_tr")
    s_tn = sem("s_tn")
    s_tx = sem("s_tx")
    s_te = sem("s_te")
    s_lg = sem("s_lg")
    s_lge = sem("s_lge")
    s_td = sem("s_td")
    s_xd = [sem(f"s_xd{i}") for i in range(NG4)]

    NCONST = 11

    with nc.Block() as block:

        @block.sync
        def _(sp):
            sp.dma_start(REL[:, 0, 0:WIN], hrt).then_inc(s_const, 16)
            sp.dma_start(REL[:, 1, 0:WIN], wrt).then_inc(s_const, 16)
            sp.dma_start(WV[:], wv.rearrange("(k p) n -> p k n", p=P)).then_inc(s_const, 16)
            sp.dma_start(KA[DH:P, :], onehots[0]).then_inc(s_const, 16)
            sp.dma_start(KB[DH:P, :], onehots[0]).then_inc(s_const, 16)
            sp.dma_start(KCC[DH:P, :], onehots[1]).then_inc(s_const, 16)
            sp.dma_start(IDF[:], ident_h).then_inc(s_const, 16)
            sp.dma_start(GW[:], gate_w.rearrange("(k p) e -> p k e", p=P)).then_inc(s_const, 16)
            sp.dma_start(UT[:], utri).then_inc(s_const, 16)
            sp.dma_start(GB[:], gate_b.partition_broadcast(P)).then_inc(s_const, 16)
            sp.dma_start(IE[:], iota_e).then_inc(s_const, 16)
            sp.wait_ge(s_ones, 1)
            sp.dma_start(slot_tab.rearrange("(p t) w -> p (t w)", p=P), ZERO[:, 0:2 * SLOTS // P]).then_inc(s_zero, 16)
            sp.dma_start(y_dram[SLOTS:SLOTS + 1, :], ZERO[0:1, :].bitcast(F32)).then_inc(s_zero, 16)
            with sp.Fori(0, BATCH) as b:
                sp.wait_ge(s_qkl, START + b * (HEADS * NB))
                for k in range(KC):
                    sp.dma_start(XN[:, k, :], xc[bass.ds(b, 1), k * P:(k + 1) * P, :].rearrange("o p n -> p (o n)"))\
                      .then_inc(s_x, 16)
                sp.wait_ge(s_td, START + b * 16)
                sp.wait_ge(s_lge, START + b * (NT // NG4))
                sp.dma_start(T[:], xt[bass.ds(b, 1)].rearrange("o (t p) c -> p (o t) c", p=P)).then_inc(s_t, 16)
                with sp.Fori(0, HEADS) as h:
                    sp.wait_ge(s_qkl, START + (b * HEADS + h) * NB)
                    sp.dma_start(WH[:], whead[bass.ds(h, 1)].rearrange("o (k p) n -> p (o k) n", p=P)).then_inc(s_wh, 16)
                sp.wait_ge(s_out, START + (b + 1) * (HEADS * NB))
                sp.dma_start(t_dram[bass.ds(b * NT, NT)].rearrange("t p c -> p t c"), T[:]).then_inc(s_td, 16)
                with sp.Fori(0, NT // NG4) as i:
                    for q in range(NG4):
                        sp.wait_ge(s_tn, b * NT + i * NG4 + q + 1)
                        sp.dma_start(xn_dram[bass.ds(b * NT + i * NG4 + q, 1)].rearrange("t p c -> p (t c)"),
                                     XNT[:, q, :]).then_inc(s_xd[q], 16)
            sp.wait_ge(s_td, START + BATCH * 16)
            sp.wait_ge(s_zero, 32)
            for q in range(NG4):
                sp.wait_ge(s_xd[q], START + BATCH * (NT // NG4) * 16)

        @block.gpsimd
        def _(pool):
            nc.gpsimd.memset(AVG[:], 1.0 / C)
            nc.gpsimd.memset(ONEH[:], 1.0)
            nc.gpsimd.memset(REL[:, :, WIN:WINP], 0.0)
            nc.gpsimd.memset(EPS6[:], 1e-6)
            nc.gpsimd.memset(EPS5[:], 1e-5)
            nc.gpsimd.memset(V[:, :, :, DH:DH + 1], S16)
            nc.gpsimd.memset(ONE[:], 1.0)
            nc.gpsimd.memset(ONES_T[:], 1.0)
            nc.gpsimd.memset(CNT[:], 0.0)
            nc.gpsimd.memset(ZERO, 0).then_inc(s_ones, 1)
            nc.gpsimd.iota(IDS[:], [[P, TT]], channel_multiplier=1).then_inc(s_ids, 1)
            pool.wait_ge(s_zero, 32)
            with pool.Fori(0, BATCH) as b:
                wait_apart(pool, s_slots, START + b + 1, s_passed)
                for t in range(NT):
                    nc.gpsimd.indirect_dma_start(slot_tab, bass.IndirectOffsetOnAxis(ap=SCAT[:, t:t + 1], axis=0),
                                                 IDW[:, t, :], None, bounds_check=SLOTS - 1, oob_is_err=False)\
                      .then_inc(s_sc, 16)
                pool.wait_ge(s_sc, (b + 1) * (NT * 16))
                pool.sem_inc(s_scd, 1)
            pool.wait_ge(s_sc, TT * 16)

        @block.tensor
        def _(pe):
            mm = nc.tensor.matmul

            def cols(j, size=QB):
                return bass.ds(j * size, size)

            def scores(n, j, jq, u, buf_unit, halves=((), ())):
                bank = 2 * (buf_unit % 2)
                pe.wait_ge(s_e, n * UNITS + buf_unit + NBUF - 1)
                for i in range(2):
                    t = 2 * u + i
                    for k in halves[i]:
                        max_half(n + 1, j + 1, k)
                    out = SP[:, bank + i, :]
                    mm(out, KA[:, t * P:(t + 1) * P], QA[:, cols(jq)], start=True, stop=False)
                    mm(out, KB[:, t * P:(t + 1) * P], QBf[:, cols(jq)], start=False, stop=False)
                    last = mm(out, KCC[:, t * P:(t + 1) * P], QC[t // (NT // 2)][:, cols(jq)], start=False, stop=True)
                last.then_inc(s_s, 1)

            def add_values(n, u):
                pe.wait_ge(s_pl, n * UNITS + u + 1 + NBUF)
                if u == 0:
                    pe.wait_ge(s_pvs, START + n)
                for ns in range(SUB):
                    out = PV[:, ns // 2, (ns % 2) * VW:(ns % 2 + 1) * VW]
                    for i in range(2):
                        t = 2 * u + i
                        first = t == 0 and ns % 2 == 0
                        mm(out, PH[:, u % NBUF, i, ns * P:(ns + 1) * P], VS[:, t, 0:VW], start=first,
                           stop=False, skip_group_check=True)
                        last = mm(out[:, 0:DH + 1], PL[:, u % NBUF, i, ns * P:(ns + 1) * P], VS[:, t, 0:DH + 1], start=False,
                                  stop=(t == NT - 1), skip_group_check=True)
                last.then_inc(s_pv, 1)

            def max_half(n, j, k):
                pe.wait_ge(s_mxr, n * HALVES + k + 1)
                if k == 0:
                    pe.wait_ge(s_rhl, START + n)
                mm(MX[:, k % 2, :], QA[:, bass.ds(j * QB + (k // 8) * P, P)], KA[:, (k % 8) * QB:(k % 8 + 1) * QB],
                   start=True, stop=True).then_inc(s_mx, 1)

            def height_by_token(n, j):
                pe.wait_ge(s_mxr, (n + 1) * HALVES + 2)
                for ns in range(SUB):
                    last = mm(MX[:, 0, ns * (SIDE + 1):(ns + 1) * (SIDE + 1)], QA[0:DH, bass.ds(j * QB + ns * P, P)],
                              RELH[:, 0, bass.ds((SIDE - 2 - 2 * ns) - j * (2 * SUB), SIDE + 1)],
                              start=(ns == 0), stop=(ns == SUB - 1), skip_group_check=True)
                last.then_inc(s_rh, 1)

            def height_minus_max(n, j):
                pe.wait_ge(s_diag, START + n + 1)
                for ns in range(SUB):
                    mm(MX[:, 1, ns * P:(ns + 1) * P], ONEH[:], DIAG[:, ns, :], start=(ns == 0), stop=False,
                       skip_group_check=True)
                for r in range(ROWS):
                    win = bass.ds((SIDE - 1 - r) - j * ROWS, P)
                    tok = bass.ds(j * QB + r * SIDE, SIDE)
                    out = MX[:, 1, r * SIDE:(r + 1) * SIDE]
                    mm(out, RELH[:, 0, win], QA[0:DH, tok], start=False, stop=False, skip_group_check=True)
                    mm(out, RELL[:, 0, win], QA[0:DH, tok], start=False, stop=False, skip_group_check=True)
                    last = mm(out, RELH[:, 0, win], QC[0][0:DH, tok], start=False, stop=True, skip_group_check=True)
                last.then_inc(s_r, 1)

            for s, credit in ((s_e, NBUF), (s_pl, NBUF), (s_pv, NBUF), (s_mxr, 2)):
                pe.sem_inc(s, credit)
            for s in (s_qkl, s_td, s_lge, s_rhl, s_pvs, s_out, s_te, s_cent, s_rwl, s_r, s_diag, s_xn, s_lg, s_scd, s_slots, *s_xd):
                pe.sem_inc(s, START)
            pe.wait_ge(s_ones, 1)
            pe.wait_ge(s_const, NCONST * 16)
            pe.wait_ge(s_rel, 3)
            with pe.Fori(0, BATCH) as b:
                pe.wait_ge(s_x, (b + 1) * (16 * KC))
                wait_apart(pe, s_slots, START + b, s_passed)

                def mean(c):
                    pe.wait_ge(s_cent, START + b * NB + max(c - 1, 0))
                    for k in range(KC):
                        last = mm(SP[:, c % 2, :], AVG[:], XN[:, k, c * QB:(c + 1) * QB], start=(k == 0), stop=(k == KC - 1))
                    last.then_inc(s_mean, 1)
                mean(0)
                for c in range(NB):
                    if c + 1 < NB:
                        mean(c + 1)
                    pe.wait_ge(s_sq, b * NB + c + 1)
                    for k in range(KC):
                        last = mm(SP[:, 2 + c % 2, :], AVG[:], SQ[:, c % 2, k, :], start=(k == 0), stop=(k == KC - 1))
                    last.then_inc(s_var, 1)
                pe.wait_ge(s_xn, START + (b + 1) * NB)
                for t in range(NT):
                    if t % 2 == 0 and t // 2 >= 4:
                        pe.wait_ge(s_vl, b * (NT // 2) + t // 2 - 3)
                    for k in range(KC):
                        last = mm(SP[:, (t // 2) % 4, (t % 2) * C:(t % 2 + 1) * C], XN[:, k, t * P:(t + 1) * P], WV[:, k, :],
                                  start=(k == 0 and t % 2 == 0), stop=(k == KC - 1), skip_group_check=True)
                    if t % 2:
                        last.then_inc(s_vps, 1)
                wait_apart(pe, s_vl, (b + 1) * (NT // 2), s_passed)
                with pe.Fori(0, HEADS) as h:
                    hh = b * HEADS + h
                    pe.wait_ge(s_wh, (hh + 1) * 16)
                    wait_apart(pe, s_e, hh * (NB * UNITS) + NBUF, s_passed)
                    with pe.Fori(0, NB // 4) as i:
                        for q in range(4):
                            pe.wait_ge(s_qkl, START + hh * NB + i * 4 + max(q - 3, 0))
                            for k in range(KC):
                                last = mm(SP[:, q, :], WH[:, k, :], XN[:, k, cols(i * 4 + q)], start=(k == 0),
                                          stop=(k == KC - 1))
                            last.then_inc(s_qk, 1)
                    wait_apart(pe, s_qkl, START + (hh + 1) * NB, s_passed)
                    with pe.Fori(0, NB // 4) as i:
                        for q in range(4):
                            pe.wait_ge(s_rwl, START + hh * NB + i * 4 + max(q - 3, 0))
                            for w in range(ROWS):
                                win = bass.ds((SIDE - 1 - q * ROWS - w) - i * (4 * ROWS), P)
                                tok = bass.ds(i * (4 * ROWS) + q * ROWS + w, SIDE, SIDE)
                                out = SP[:, q, w * SIDE:(w + 1) * SIDE]
                                mm(out, RELH[:, 1, win], QA[0:DH, tok], start=(w == 0), stop=False, skip_group_check=True)
                                mm(out, RELL[:, 1, win], QA[0:DH, tok], start=False, stop=False, skip_group_check=True)
                                last = mm(out, RELH[:, 1, win], QC[0][0:DH, tok], start=False, stop=True, skip_group_check=True)
                            last.then_inc(s_rw, 1)
                    pe.wait_ge(s_rwl, START + (hh + 1) * NB)
                    pe.wait_ge(s_dup, hh + 1)
                    n0 = hh * NB
                    for k in range(HALVES):
                        max_half(n0, 0, k)
                    height_by_token(n0, 0)
                    height_minus_max(n0, 0)
                    pe.wait_ge(s_rhl, START + n0 + 1)
                    scores(n0, 0, 0, 0, 0)
                    scores(n0, 0, 0, 1, 1)

                    def block_of(n, j, more):
                        for u in range(UNITS):
                            now = MAXH[u] if more else []
                            halves = (now[0:1], now[1:2])
                            if u == U_CHAIN and more:
                                height_by_token(n + 1, j + 1)
                            if u < UNITS - 2:
                                scores(n, j, j, u + 2, u + 2, halves)
                            elif more:
                                if u == UNITS - 2:
                                    pe.wait_ge(s_rhl, START + n + 2)
                                scores(n, j, j + 1, u + 2 - UNITS, u + 2)
                            for k in now[2:]:
                                max_half(n + 1, j + 1, k)
                            if u == U_CHAIN and more:
                                height_minus_max(n + 1, j + 1)
                            add_values(n, u)
                    with pe.Fori(0, NB - 1) as j:
                        block_of(n0 + j, j, True)
                    block_of(n0 + NB - 1, NB - 1, False)
                with pe.Fori(0, NT // NG4) as i:
                    def logits(q):
                        pe.wait_ge(s_te, START + b * NT + i * NG4 + q + 1)
                        if q == 0:
                            pe.wait_ge(s_lge, START + b * (NT // NG4) + i)
                        for k in range(KC):
                            last = mm(MX[:, 0, q * EXPERTS:(q + 1) * EXPERTS], XTT[:, q % 2, k * P:(k + 1) * P], GW[:, k, :],
                                      start=(k == 0), stop=(k == KC - 1))
                        last.then_inc(s_lg, 1)
                    for q in range(NG4):
                        pe.wait_ge(s_tn, b * NT + i * NG4 + q + 1)
                        for k in range(KC):
                            last = nc.tensor.transpose(SP[:, q, k * P:(k + 1) * P], XNT[:, q, k * P:(k + 1) * P], IDF[:])
                        last.then_inc(s_tx, 1)
                        if q:
                            logits(q - 1)
                    logits(NG4 - 1)
                pe.wait_ge(s_oh, b + 1)
                oh = OH[:].rearrange("p t e -> p (t e)")
                mm(SP[:, 0, 0:NT * EXPERTS], UT[:], oh, start=True, stop=True)
                mm(SP[:, 1, 0:NT * EXPERTS], ONE[:], oh, start=True, stop=True).then_inc(s_cnt, 1)

        @block.scalar
        def _(act):
            A = nc.scalar.activation

            def exp_unit(n, buf_unit):
                w = n * UNITS + buf_unit
                act.wait_ge(s_s, w + 1)
                act.wait_ge(s_pv, w + 1)
                act.wait_ge(s_pl, w + NBUF - 1)
                src = SP[:, 2 * (buf_unit % 2):2 * (buf_unit % 2) + 2, :]
                A(PH[:, buf_unit % NBUF, :, :], src, ACT.Exp, scale=1.0 / (S16 * S16))
                A(PF[:, buf_unit % 2, :, :], src, ACT.Exp, scale=1.0 / (S16 * S16)).then_inc(s_e, 1)

            def height_high(n, j):
                wait_apart(act, s_r, START + n + 1, s_passed)
                for i in range(2):
                    last = A(QC[i][DH:DH + 32, bass.ds(j * QB, QB)], MX[32 * i:32 * i + 32, 1, :], ACT.Copy)
                last.then_inc(s_rhh, 1)

            def diagonal(n):
                act.wait_ge(s_rel, 3)
                act.wait_ge(s_r, START + n)
                wait_apart(act, s_mneg, n + 1, s_passed)
                for ns in range(SUB):
                    last = A(DIAG[:, ns, :], IDH[:], ACT.Copy, scale=MNEG[:, ns:ns + 1])
                last.then_inc(s_diag, 1)

            act.wait_ge(s_const, NCONST * 16)
            act.wait_ge(s_ones, 1)
            A(RELH[:], REL[:], ACT.Copy).then_inc(s_rel, 1)
            A(IDH[:], IDF[:], ACT.Copy).then_inc(s_rel, 1)
            act.wait_ge(s_zero, 32)
            with act.Fori(0, BATCH) as b:
                def square(c):
                    wait_apart(act, s_cent, START + b * NB + c + 1, s_passed)
                    A(SQ[:, c % 2, :, :], XN[:, :, c * QB:(c + 1) * QB], ACT.Square).then_inc(s_sq, 1)
                square(0)
                for c in range(NB):
                    if c + 1 < NB:
                        if c:
                            act.wait_ge(s_var, b * NB + c)
                        square(c + 1)
                    act.wait_ge(s_var, b * NB + c + 1)
                    act.wait_ge(s_xn, START + b * NB + max(c - 1, 0))
                    A(RS[:, c % 2, :], SP[:, 2 + c % 2, :], ACT.Sqrt, bias=EPS6[:]).then_inc(s_std, 1)
                for i in range(NT // 2):
                    act.wait_ge(s_vps, b * (NT // 2) + i + 1)
                    for t in range(2):
                        last = A(V[:, :, 2 * i + t, 0:DH], SP[:, i % 4, t * C:(t + 1) * C].rearrange("p (h d) -> p h d", h=HEADS),
                                 ACT.Copy, scale=S16)
                    last.then_inc(s_vh, 1)
                with act.Fori(0, HEADS) as h:
                    hh = b * HEADS + h
                    with act.Fori(0, NB // 4) as i:
                        for q in range(4):
                            col = bass.ds((i * 4 + q) * QB, QB)
                            wait_apart(act, s_qk, hh * NB + i * 4 + q + 1, s_passed)
                            A(QA[0:DH, col], SP[0:DH, q, :], ACT.Copy, scale=S16)
                            A(KA[0:DH, col], SP[DH:P, q, :], ACT.Copy, scale=QK).then_inc(s_qkh, 1)
                    with act.Fori(0, NB // 4) as i:
                        for q in range(4):
                            wait_apart(act, s_rw, hh * NB + i * 4 + q + 1, s_passed)
                            A(QA[DH:P, :].rearrange("p (h w) -> p w h", w=SIDE)[:, bass.ds((i * 4 + q) * ROWS, ROWS), :],
                              SP[0:DH, q, :].rearrange("p (w h) -> p w h", w=ROWS), ACT.Copy).then_inc(s_rwh, 1)
                    n0 = hh * NB
                    diagonal(n0)
                    height_high(n0, 0)
                    exp_unit(n0, 0)
                    exp_unit(n0, 1)

                    def block_of(n, j, more):
                        for u in range(UNITS):
                            if u == U_CHAIN and more:
                                diagonal(n + 1)
                            if u < UNITS - 2 or more:
                                exp_unit(n, u + 2)
                            if u == U_CHAIN and more:
                                height_high(n + 1, j + 1)
                        act.wait_ge(s_pv, (n + 1) * UNITS + NBUF)
                        act.wait_ge(s_out, START + n)
                        for i in range(2):
                            last = A(PVS[:, 2 * i:2 * i + 2, :], PV[:, i, 0:2 * VW].rearrange("p (s v) -> p s v", s=2), ACT.Copy)
                        last.then_inc(s_pvs, 1)
                    with act.Fori(0, NB - 1) as j:
                        block_of(n0 + j, j, True)
                    block_of(n0 + NB - 1, NB - 1, False)
                act.wait_ge(s_mv, b + 1)
                A(RSTD[:], MV[:, :, 1], ACT.Sqrt, bias=EPS5[:]).then_inc(s_ts, 1)
                with act.Fori(0, NT // NG4) as i:
                    for q in range(NG4):
                        act.wait_ge(s_tx, b * NT + i * NG4 + q + 1)
                        act.wait_ge(s_lg, START + b * NT + i * NG4 + max(q - 1, 0))
                        A(XTT[:, q % 2, :], SP[:, q, 0:C], ACT.Copy).then_inc(s_te, 1)
                act.wait_ge(s_sh, b + 1)
                A(EX[:], LG[:], ACT.Exp).then_inc(s_ex, 1)

        @block.vector
        def _(dve):
            def low_unit(n, buf_unit):
                dve.wait_ge(s_e, n * UNITS + buf_unit + 1 + NBUF)
                nc.vector.tensor_tensor(PL[:, buf_unit % NBUF, :, :], PF[:, buf_unit % 2, :, :], PH[:, buf_unit % NBUF, :, :],
                                        ALU.subtract).then_inc(s_pl, 1)

            def reduce_half(n, k):
                dve.wait_ge(s_mx, n * HALVES + k + 1)
                nc.vector.tensor_reduce(G[:, k // 8, (k % 8) * 8:(k % 8 + 1) * 8],
                                        MX[:, k % 2, :].rearrange("p (h w) -> p h w", w=SIDE), AX.X, ALU.max).then_inc(s_mxr, 1)

            def row_maximum(n):
                dve.wait_ge(s_rh, n + 1)
                rh = MX[:, 0, 0:SUB * (SIDE + 1)].rearrange("p (s w) -> p s w", s=SUB)
                dve.wait_ge(s_mxr, (n + 1) * HALVES + 2)
                nc.vector.scalar_tensor_tensor(G2[0:64], rh[0:64, :, 1:SIDE + 1], S16, G[0:64], ALU.mult, ALU.add)
                nc.vector.scalar_tensor_tensor(G2[64:P], rh[64:P, :, 0:SIDE], S16, G[64:P], ALU.mult, ALU.add).then_inc(s_g2, 1)
                dve.wait_ge(s_g2, n + 1)
                nc.vector.tensor_reduce(MROW[:], G2[:], AX.X, ALU.max).then_inc(s_mrow, 1)
                dve.wait_ge(s_mrow, n + 1)
                dve.wait_ge(s_diag, START + n)
                nc.vector.tensor_scalar(MNEG[:], MROW[:], -1.0 / S16, S16 * SHIFT, ALU.mult, ALU.add).then_inc(s_mneg, 1)

            def height_low(n, j):
                col = bass.ds(j * QB, QB)
                dve.wait_ge(s_rhh, n + 1)
                for i in range(2):
                    last = nc.vector.tensor_tensor(QC[i][DH + 32:P, col], MX[32 * i:32 * i + 32, 1, :], QC[i][DH:DH + 32, col],
                                                   ALU.subtract)
                last.then_inc(s_rhl, 1)

            dve.wait_ge(s_rel, 1)
            nc.vector.tensor_tensor(RELL[:], REL[:], RELH[:], ALU.subtract).then_inc(s_rel, 1)
            with dve.Fori(0, BATCH) as b:
                def centre(c):
                    dve.wait_ge(s_mean, b * NB + c + 1)
                    for k in range(KC):
                        col = slice(c * QB, (c + 1) * QB)
                        last = nc.vector.tensor_tensor(XN[:, k, col], XN[:, k, col], SP[:, c % 2, :], ALU.subtract)
                    last.then_inc(s_cent, 1)
                centre(0)
                for c in range(NB):
                    if c + 1 < NB:
                        centre(c + 1)
                    dve.wait_ge(s_std, b * NB + c + 1)
                    nc.vector.reciprocal(RS[:, c % 2, :], RS[:, c % 2, :]).then_inc(s_rstd, 1)
                    dve.wait_ge(s_rstd, b * NB + c + 1)
                    for k in range(KC):
                        col = slice(c * QB, (c + 1) * QB)
                        last = nc.vector.tensor_tensor(XN[:, k, col], XN[:, k, col], RS[:, c % 2, :], ALU.mult)
                    last.then_inc(s_xn, 1)
                for i in range(NT // 2):
                    dve.wait_ge(s_vh, b * (NT // 2) + i + 1)
                    for t in range(2):
                        last = nc.vector.scalar_tensor_tensor(
                            V[:, :, 2 * i + t, DH + 1:VW], SP[:, i % 4, t * C:(t + 1) * C].rearrange("p (h d) -> p h d", h=HEADS),
                            S16, V[:, :, 2 * i + t, 0:DH], ALU.mult, ALU.subtract)
                    last.then_inc(s_vl, 1)
                dve.wait_ge(s_t, (b + 1) * 16)
                for q in range(NG4):
                    wait_apart(dve, s_xd[q], START + b * (NT // NG4 * 16), s_passed)
                with dve.Fori(0, HEADS) as h:
                    hh = b * HEADS + h
                    with dve.Fori(0, NB // 4) as i:
                        for q in range(4):
                            col = bass.ds((i * 4 + q) * QB, QB)
                            dve.wait_ge(s_qkh, hh * NB + i * 4 + q + 1)
                            nc.vector.scalar_tensor_tensor(QC[0][0:DH, col], SP[0:DH, q, :], S16, QA[0:DH, col], ALU.mult, ALU.subtract)
                            nc.vector.scalar_tensor_tensor(KB[0:DH, col], SP[DH:P, q, :], QK, KA[0:DH, col], ALU.mult,
                                                           ALU.subtract).then_inc(s_qkl, 1)
                    nc.vector.tensor_copy(VS[:, :, 0:VW], V[:, bass.ds(h, 1), :, 0:VW].rearrange("p o t v -> p (o t) v"))
                    nc.vector.tensor_copy(QBf[0:DH, :], QA[0:DH, :])
                    wait_apart(dve, s_qkl, START + (hh + 1) * NB, s_passed)
                    nc.vector.tensor_copy(QC[1][0:DH, :], QC[0][0:DH, :])
                    nc.vector.tensor_copy(KCC[0:DH, :], KA[0:DH, :]).then_inc(s_dup, 1)
                    with dve.Fori(0, NB // 4) as i:
                        for q in range(4):
                            def wide(t):
                                return t[DH:P, :].rearrange("p (h w) -> p w h", w=SIDE)[:, bass.ds((i * 4 + q) * ROWS, ROWS), :]
                            dve.wait_ge(s_rwh, hh * NB + i * 4 + q + 1)
                            nc.vector.tensor_tensor(wide(QBf), SP[0:DH, q, :].rearrange("p (w h) -> p w h", w=ROWS), wide(QA),
                                                    ALU.subtract).then_inc(s_rwl, 1)
                    n0 = hh * NB
                    for k in range(HALVES):
                        reduce_half(n0, k)
                    row_maximum(n0)
                    height_low(n0, 0)
                    low_unit(n0, 0)

                    def block_of(n, j, more):
                        for u in range(UNITS):
                            now = MAXH[u] if more else []
                            for k in now[:2]:
                                reduce_half(n + 1, k)
                            if u == U_CHAIN and more:
                                row_maximum(n + 1)
                            if u < UNITS - 1 or more:
                                low_unit(n, u + 1)
                            for k in now[2:]:
                                reduce_half(n + 1, k)
                            if u == U_CHAIN and more:
                                height_low(n + 1, j + 1)
                        dve.wait_ge(s_pvs, START + n + 1)
                        nc.vector.reciprocal(PVR[:], PVS[:, :, DH]).then_inc(s_pvr, 1)
                        nc.vector.tensor_tensor(PVO[:], PVS[:, :, 0:DH], PVS[:, :, DH + 1:VW], ALU.add).then_inc(s_pvo, 1)
                        dve.wait_ge(s_pvr, n + 1)
                        dve.wait_ge(s_pvo, n + 1)
                        for ns in range(SUB):
                            res = T[:, bass.ds(j * SUB + ns, 1), bass.ds(h * DH, DH)].rearrange("p o d -> p (o d)")
                            last = nc.vector.scalar_tensor_tensor(res, PVO[:, ns, :], PVR[:, ns:ns + 1], res, ALU.mult, ALU.add)
                        last.then_inc(s_out, 1)
                    with dve.Fori(0, NB - 1) as j:
                        block_of(n0 + j, j, True)
                    block_of(n0 + NB - 1, NB - 1, False)
                dve.wait_ge(s_out, START + (b + 1) * (HEADS * NB))
                for t in range(NT):
                    last = nc.vector.bn_stats(STAT[:, t, :], T[:, t, :])
                last.then_inc(s_st, 1)
                wait_apart(dve, s_st, b + 1, s_passed)
                for t in range(NT):
                    last = nc.vector.bn_aggr(MV[:, t, :], STAT[:, t, :])
                last.then_inc(s_mv, 1)
                dve.wait_ge(s_ts, b + 1)
                nc.vector.reciprocal(RSTD2[:], RSTD[:]).then_inc(s_tr, 1)
                wait_apart(dve, s_tr, b + 1, s_passed)

                with dve.Fori(0, NT // NG4) as i:
                    for q in range(NG4):
                        dve.wait_ge(s_xd[q], START + (b * (NT // NG4) + i) * 16)
                        dve.wait_ge(s_lg, START + b * NT + i * NG4)
                        t1 = bass.ds(i * NG4 + q, 1)
                        nc.vector.tensor_scalar(XNT[:, q, :], T[:, t1, :].rearrange("p o c -> p (o c)"),
                                                MV[:, t1, 0], RSTD2[:, t1], ALU.subtract, ALU.mult).then_inc(s_tn, 1)
                    dve.wait_ge(s_lg, START + b * NT + (i + 1) * NG4)
                    nc.vector.tensor_copy(LG[:, bass.ds(i * NG4, NG4), :].rearrange("p t e -> p (t e)"),
                                          MX[:, 0, 0:NG4 * EXPERTS]).then_inc(s_lge, 1)

                steps = [0]
                NSTEPS = 18

                def link(ins):
                    ins.then_inc(s_v, 1)
                    steps[0] += 1
                    wait_apart(dve, s_v, b * NSTEPS + steps[0], s_passed)

                def wide(a):
                    return a.unsqueeze(2).broadcast_to([P, NT, EXPERTS])

                def per_tile(a):
                    return a.unsqueeze(1).broadcast_to([P, NT, EXPERTS])
                V_ = nc.vector
                wait_apart(dve, s_lge, START + (b + 1) * (NT // NG4), s_passed)
                link(V_.tensor_tensor(LG[:], LG[:], per_tile(GB[:]), ALU.add))
                link(V_.tensor_reduce(R_("max"), LG[:], AX.X, ALU.max))
                link(V_.tensor_tensor(LG[:], LG[:], wide(R_("max")), ALU.subtract))
                V_.tensor_copy(R_("pos"), R_("max")).then_inc(s_sh, 1)
                link(V_.scalar_tensor_tensor(CA[:], LG[:], 0.0, per_tile(IE[:]), ALU.is_ge, ALU.mult))
                link(V_.tensor_reduce(R_("code"), CA[:], AX.X, ALU.max))
                V_.tensor_tensor(OH[:], CA[:], wide(R_("code")), ALU.is_equal).then_inc(s_oh, 1)
                wait_apart(dve, s_ex, b + 1, s_passed)
                link(V_.tensor_reduce(R_("sum"), EX[:], AX.X, ALU.add))
                V_.reciprocal(R_("prob"), R_("sum"))
                wait_apart(dve, s_cnt, b + 1, s_passed)
                link(V_.tensor_copy(TOTS[:], SP[:, 1, 0:NT * EXPERTS].rearrange("p (t e) -> p t e", e=EXPERTS)))
                for e in range(EXPERTS):
                    last = V_.tensor_tensor_scan(CUM[:, e, :], ONES_T[:], TOTS[:, :, e], CNT[:, e:e + 1], ALU.mult, ALU.add)
                link(last)
                V_.tensor_copy(CNT[:], CUM[:, :, NT - 1])
                link(V_.tensor_tensor(POS[:], CUM[:].rearrange("p e t -> p t e"), TOTS[:], ALU.subtract))
                link(V_.tensor_tensor(CA[:], SP[:, 0, 0:NT * EXPERTS].rearrange("p (t e) -> p t e", e=EXPERTS), POS[:], ALU.add))
                link(V_.tensor_tensor(POS[:], CA[:], OH[:], ALU.mult))
                link(V_.tensor_reduce(R_("pos"), POS[:], AX.X, ALU.add))
                link(V_.tensor_scalar(R_("kept"), R_("pos"), float(CAP), None, ALU.is_lt))
                link(V_.scalar_tensor_tensor(R_("rel"), R_("code"), -float(CAP), R_("pos"), ALU.mult, ALU.add))
                link(V_.tensor_tensor(R_("rel2"), R_("rel"), R_("kept"), ALU.mult))
                link(V_.tensor_scalar(R_("slot"), R_("rel2"), float(SLOTS), None, ALU.add))
                link(V_.tensor_tensor(R_("w"), R_("prob"), R_("kept"), ALU.mult))
                wait_apart(dve, s_scd, START + b, s_passed)
                dve.wait_ge(s_ids, 1)
                V_.tensor_copy(SCAT[:], R_("slot"))
                V_.tensor_copy(IDW[:, :, 0], IDS[:, bass.ds(b * NT, NT)])
                V_.tensor_copy(IDW[:, :, 1].bitcast(F32), R_("w"))
                link(V_.tensor_copy(GATH[:, bass.ds(b * NT, NT)], R_("slot")))
                V_.tensor_copy(R_("rel"), R_("w")).then_inc(s_slots, 1)
                assert steps[0] == NSTEPS


def build(nc, xc, xt, whead, wv, hrt, wrt, onehots, ident, utri, iota_e, gate_w, gate_b, w1, b1, w2, b2, out):
    t_dram = nc.dram_tensor("t_dram", [TT, P, C], F32, kind="Internal").ap()
    xn_dram = nc.dram_tensor("xn_dram", [TT, P, C], F32, kind="Internal").ap()
    slot_tab = nc.dram_tensor("slot_tab", [SLOTS, 2], I32, kind="Internal").ap()
    y_dram = nc.dram_tensor("y_dram", [SLOTS + 1, C], F32, kind="Internal").ap()
    with ExitStack() as keep:
        GATH = keep.enter_context(nc.sbuf_tensor("GATH", [P, TT], I32))
        with ExitStack() as ctx:
            attention_and_norm(nc, ctx, xc, xt, whead, wv, hrt, wrt, onehots, ident, utri, iota_e, gate_w, gate_b, t_dram,
                               xn_dram, slot_tab, y_dram, GATH)
        with ExitStack() as ctx:
            experts(nc, ctx, ident, w1, b1, w2, b2, xn_dram, slot_tab, y_dram)
        with ExitStack() as ctx:
            combine(nc, ctx, GATH, y_dram, t_dram, out)


def experts(nc, ctx, ident, w1, b1, w2, b2, xn_dram, slot_tab, y_dram):
    XS, WS, HS = 16.0, 256.0, 16.0
    NXG = 5
    NPC = 8
    PIECE = KC * FF // NPC
    FMAX = 3.4028234663852886e38

    def sbx(name, shape, dt):
        return ctx.enter_context(nc.sbuf_tensor(name, shape, dt))

    def sem(name):
        return ctx.enter_context(nc.semaphore(name))

    ID = sbx("ID", [P, P], F32)
    SLOT = sbx("SLOT", [P, SLOTS // P, 2], I32)
    YT = sbx("YT", [P, C], F32)
    YP_ = sbx("YP_", [P, C], F32)
    YN_ = sbx("YN_", [P, C], F32)
    MP = sbx("MP", [P, C], I32)
    MN = sbx("MN", [P, C], I32)
    LIM = sbx("LIM", [P, 2, C], F32)
    PS = ctx.enter_context(nc.psum_tensor("PS", [P, 8, 512], F32))
    TRP, HP, YP = PS[:, 0:2, :], PS[:, 2:5, :], PS[:, 5:8, :]
    s_lim = sem("e_lim")
    s_idx = sem("e_slots")
    s_y1 = sem("e_y_bias")
    s_y2 = sem("e_y_parts")
    s_y3 = sem("e_y_masks")
    s_y4 = sem("e_y_limits")
    W1F = sbx("W1F", [P, KC * FF], F32)
    W2F = sbx("W2F", [P, KF * C], F32)
    W1P = [sbx(f"W1P{i}", [P, 2, KC * FF], F16) for i in range(2)]
    W2P = [sbx(f"W2P{i}", [P, 2, KF * C], F16) for i in range(2)]
    B1F = sbx("B1F", [P, EXPERTS, KF], F32)
    B1 = sbx("B1", [P, EXPERTS, KF], F32)
    B2 = sbx("B2", [P, EXPERTS, C], F32)
    SLOTC = sbx("SLOTC", [P, 2, ST], I32)
    XG = sbx("XG", [P, NXG, C], F32)
    XTH = sbx("XTH", [P, 2, KC, CAP], F16)
    XTL = sbx("XTL", [P, 2, KC, CAP], F16)
    HH = sbx("HH", [P, 3, KF, 512], F16)
    HL = sbx("HL", [P, 3, KF, 512], F16)
    HF = sbx("HF", [P, 2, 512], F32)
    YS = sbx("YS", [P, NXG, C], F32)

    s_passed = sem("e_passed")
    s_b = sem("e_bias")
    s_b1 = sem("e_bias_scaled")
    s_w = sem("e_weights")
    s_wh = sem("e_w_high")
    s_wl = sem("e_w_low")
    s_xg = [sem(f"e_gathered{i}") for i in range(NXG)]
    s_ic = sem("e_index")
    s_xt = sem("e_turned")
    s_xh = sem("e_x_high")
    s_xl = sem("e_x_low")
    s_h = sem("e_hidden")
    s_hh = sem("e_h_high")
    s_hl = sem("e_h_low")
    s_y = sem("e_y")
    s_ye = sem("e_y_out")
    s_yd = [sem(f"e_y_dram{i}") for i in range(NXG)]
    NCH = len(CHUNKS)
    HU = NCH * KF

    with nc.Block() as block:
        def each_expert(eng, body):
            with eng.Fori(0, EXPERTS // 2 - 1) as i:
                body(i * 2, 0, True)
                body(i * 2 + 1, 1, True)
            body(EXPERTS - 2, 0, True)
            body(EXPERTS - 1, 1, False)

        @block.sync
        def _(sp):
            sp.dma_start(SLOT[:], slot_tab.rearrange("(t p) w -> p t w", p=P)).then_inc(s_idx, 16)
            sp.dma_start(ID[:], ident).then_inc(s_b, 16)
            sp.dma_start(B1F[:], b1).then_inc(s_b, 16)
            sp.dma_start(B2[:], b2.rearrange("e c -> (e c)").partition_broadcast(P).rearrange("p (e c) -> p e c", c=C))\
              .then_inc(s_b, 16)

            def load(m):
                sp.dma_start(W1F[:].rearrange("p (k f) -> p k f", k=KC), w1[m].rearrange("(k p) f -> p k f", p=P)).then_inc(s_w, 16)
                sp.dma_start(W2F[:].rearrange("p (k c) -> p k c", k=KF), w2[m].rearrange("(k p) c -> p k c", p=P)).then_inc(s_w, 16)

            def load_next(m):
                sp.wait_ge(s_wl, START + m * (2 * NPC))
                sp.dma_start(W1F[:].rearrange("p (k f) -> p k f", k=KC),
                             w1[bass.ds(m, 1)].rearrange("o (k p) f -> p (o k) f", p=P)).then_inc(s_w, 16)
                sp.dma_start(W2F[:].rearrange("p (k c) -> p k c", k=KF),
                             w2[bass.ds(m, 1)].rearrange("o (k p) c -> p (o k) c", p=P)).then_inc(s_w, 16)

            def stores(m, lo, hi):
                for s in range(lo, hi):
                    sp.wait_ge(s_ye, START + m * ST + s + 1)
                    sp.dma_start(y_dram[bass.ds(m * CAP + s * P, P), :], YS[:, s % NXG, :]).then_inc(s_yd[s % NXG], 16)

            load(0)
            load_next(1)

            def body(m, par, more):
                stores(m, 0, CHUNKS[0][1])
                if more and not (isinstance(m, int) and m + 2 >= EXPERTS):
                    load_next(m + 2)
                stores(m, CHUNKS[0][1], ST)
            each_expert(sp, body)
            for i in range(NXG):
                sp.wait_ge(s_yd[i], START + EXPERTS * (ST // NXG) * 16)

        @block.gpsimd
        def _(pool):
            xn = xn_dram.rearrange("t p c -> (t p) c")

            def gathers(m, par):
                wait_apart(pool, s_xt, m * ST, s_passed)
                nc.gpsimd.tensor_copy(SLOTC[:, par, :], SLOT[:, bass.ds(m * ST, ST), 0]).then_inc(s_ic, 1)
                wait_apart(pool, s_ic, m + 1, s_passed)
                for s in range(ST):
                    wait_apart(pool, s_xt, m * ST + s + 1, s_passed)
                    nc.gpsimd.indirect_dma_start(XG[:, s % NXG, :], None, xn,
                                                 bass.IndirectOffsetOnAxis(ap=SLOTC[:, par, s:s + 1], axis=0),
                                                 bounds_check=TT * P - 1, oob_is_err=False).then_inc(s_xg[s % NXG], 16)
            nc.gpsimd.memset(LIM[:, 0], 10000.0)
            nc.gpsimd.memset(LIM[:, 1], -10000.0).then_inc(s_lim, 1)
            pool.wait_ge(s_idx, 16)
            with pool.Fori(0, EXPERTS // 2) as i:
                gathers(i * 2, 0)
                gathers(i * 2 + 1, 1)

        @block.tensor
        def _(pe):
            mm = nc.tensor.matmul
            pe.sem_inc(s_xt, NXG)
            pe.sem_inc(s_y, ST)
            pe.sem_inc(s_hh, 3)
            for s in (s_wl, s_xl, s_ye, s_hl, *s_yd):
                pe.sem_inc(s, START)
            pe.wait_ge(s_b, 48)

            def body(m, par, more):
                for s in range(ST):
                    pe.wait_ge(s_xg[s % NXG], (m * (ST // NXG) + s // NXG + 1) * 16)
                    if s >= 2:
                        pe.wait_ge(s_xl, START + m * ST + s - 1)
                    else:
                        pe.wait_ge(s_xl, START + m * ST)
                    for k in range(KC):
                        last = nc.tensor.transpose(TRP[:, s % 2, k * P:(k + 1) * P], XG[:, s % NXG, k * P:(k + 1) * P], ID[:])
                    last.then_inc(s_xt, 1)
                pe.wait_ge(s_wl, START + (m + 1) * (2 * NPC))
                pe.wait_ge(s_xl, START + (m + 1) * ST)
                w1p = W1P[par][:].rearrange("p a (k f) -> p a k f", k=KC)
                w2p = W2P[par][:].rearrange("p a (k c) -> p a k c", k=KF)

                def hidden(c):
                    t0, nt = CHUNKS[c]
                    sl = slice(t0 * P, (t0 + nt) * P)
                    for f in range(KF):
                        g = c * KF + f
                        pe.wait_ge(s_hh, m * HU + g + 1)
                        out = HP[:, g % 3, 0:nt * P]
                        fs = slice(f * P, (f + 1) * P)
                        for k in range(KC):
                            mm(out, w1p[:, 0, k, fs], XTH[:, par, k, sl], start=(k == 0), stop=False)
                            mm(out, w1p[:, 1, k, fs], XTH[:, par, k, sl], start=False, stop=False)
                            last = mm(out, w1p[:, 0, k, fs], XTL[:, par, k, sl], start=False, stop=(k == KC - 1))
                        last.then_inc(s_h, 1)

                def rows(c):
                    t0, nt = CHUNKS[c]
                    pe.wait_ge(s_hl, START + m * HU + (c + 1) * KF)
                    for t in range(nt):
                        s = t0 + t
                        if s >= 3:
                            pe.wait_ge(s_ye, START + m * ST + s - 2)
                        else:
                            pe.wait_ge(s_ye, START + m * ST)
                        out = YP[:, s % 3, 0:C]
                        for f in range(KF):
                            hs = slice(t * P, (t + 1) * P)
                            mm(out, HH[:, c, f, hs], w2p[:, 0, f, :], start=(f == 0), stop=False)
                            mm(out, HH[:, c, f, hs], w2p[:, 1, f, :], start=False, stop=False)
                            last = mm(out, HL[:, c, f, hs], w2p[:, 0, f, :], start=False, stop=(f == KF - 1))
                        last.then_inc(s_y, 1)
                hidden(0)
                hidden(1)
                rows(0)
                hidden(2)
                rows(1)
                rows(2)
            each_expert(pe, body)

        def piece(buf, par, part, q):
            src, dst = (W1F, W1P[par]) if q < NPC else (W2F, W2P[par])
            sl = slice((q % NPC) * PIECE, (q % NPC + 1) * PIECE)
            return src[:, sl], dst[:, part, sl]

        @block.scalar
        def _(act):
            A = nc.scalar.activation

            def split_high(m, par, q):
                act.wait_ge(s_w, (m + 1) * 32)
                act.wait_ge(s_y, m * ST)
                src, dst = piece(None, par, 0, q)
                A(dst, src, ACT.Copy, scale=WS).then_inc(s_wh, 1)

            act.wait_ge(s_b, 48)
            A(B1[:], B1F[:], ACT.Copy, scale=HS).then_inc(s_b1, 1)
            act.wait_ge(s_b1, 1)
            for q in range(2 * NPC):
                split_high(0, 0, q)

            def body(m, par, more):
                for s in range(ST):
                    act.wait_ge(s_xt, m * ST + s + 1 + NXG)
                    A(XTH[:, par, :, s * P:(s + 1) * P], TRP[:, s % 2, 0:C].rearrange("p (k n) -> p k n", k=KC), ACT.Copy,
                      scale=XS).then_inc(s_xh, 1)
                for c in range(NCH):
                    t0, nt = CHUNKS[c]
                    act.wait_ge(s_y, m * ST + t0 + nt)
                    for f in range(KF):
                        g = c * KF + f
                        wait_apart(act, s_h, m * HU + g + 1, s_passed)
                        src = HP[:, g % 3, 0:nt * P]
                        bias = B1[:, bass.ds(m, 1), f]
                        A(HH[:, c, f, 0:nt * P], src, ACT.Relu, bias=bias, scale=HS / (XS * WS))
                        wait_apart(act, s_hl, START + m * HU + max(g - 1, 0), s_passed)
                        A(HF[:, g % 2, 0:nt * P], src, ACT.Relu, bias=bias, scale=HS / (XS * WS)).then_inc(s_hh, 1)
                        if more and g < 2 * NPC:
                            split_high(m + 1, 1 - par, g)
            each_expert(act, body)

        @block.vector
        def _(dve):
            V_ = nc.vector

            def split_low(m, par, q):
                dve.wait_ge(s_wh, m * (2 * NPC) + q + 1)
                src, lo = piece(None, par, 1, q)
                _, hi = piece(None, par, 0, q)
                V_.scalar_tensor_tensor(lo, src, WS, hi, ALU.mult, ALU.subtract).then_inc(s_wl, 1)

            for q in range(2 * NPC):
                split_low(0, 0, q)

            def body(m, par, more):
                for s in range(ST):
                    dve.wait_ge(s_xh, m * ST + s + 1)
                    V_.scalar_tensor_tensor(XTL[:, par, :, s * P:(s + 1) * P],
                                            TRP[:, s % 2, 0:C].rearrange("p (k n) -> p k n", k=KC), XS,
                                            XTH[:, par, :, s * P:(s + 1) * P], ALU.mult, ALU.subtract).then_inc(s_xl, 1)

                def low(c):
                    t0, nt = CHUNKS[c]
                    for f in range(KF):
                        g = c * KF + f
                        dve.wait_ge(s_hh, m * HU + g + 1 + 3)
                        V_.tensor_tensor(HL[:, c, f, 0:nt * P], HF[:, g % 2, 0:nt * P], HH[:, c, f, 0:nt * P],
                                         ALU.subtract).then_inc(s_hl, 1)
                        if more and g < 2 * NPC:
                            split_low(m + 1, 1 - par, g)

                def rows(c):
                    t0, nt = CHUNKS[c]
                    for s in range(t0, t0 + nt):
                        dve.wait_ge(s_y, m * ST + s + 1 + ST)
                        dve.wait_ge(s_yd[s % NXG], START + (m * (ST // NXG) + s // NXG) * 16)
                        n = m * ST + s
                        V_.scalar_tensor_tensor(YT[:], YP[:, s % 3, 0:C], 1.0 / (HS * WS),
                                                B2[:, bass.ds(m, 1), :].rearrange("p o c -> p (o c)"), ALU.mult, ALU.add)\
                          .then_inc(s_y1, 1)
                        w = SLOT[:, bass.ds(n, 1), 1].bitcast(F32)
                        wait_apart(dve, s_y1, n + 1, s_passed)
                        V_.tensor_scalar(YP_[:], YT[:], w, 0.0, ALU.mult, ALU.max)
                        V_.tensor_scalar(YN_[:], YT[:], w, 0.0, ALU.mult, ALU.min).then_inc(s_y2, 1)
                        wait_apart(dve, s_y2, n + 1, s_passed)
                        V_.tensor_scalar(MP[:], YP_[:], FMAX, None, ALU.is_gt)
                        V_.tensor_scalar(MN[:], YN_[:], -FMAX, None, ALU.is_lt).then_inc(s_y3, 1)
                        wait_apart(dve, s_y3, n + 1, s_passed)
                        V_.copy_predicated(YP_[:], MP[:], LIM[:, 0])
                        V_.copy_predicated(YN_[:], MN[:], LIM[:, 1]).then_inc(s_y4, 1)
                        dve.wait_ge(s_y4, n + 1)
                        V_.tensor_tensor(YS[:, s % NXG, :], YP_[:], YN_[:], ALU.add).then_inc(s_ye, 1)
                low(0)
                low(1)
                rows(0)
                low(2)
                rows(1)
                rows(2)
            dve.wait_ge(s_b, 48)
            dve.wait_ge(s_idx, 16)
            dve.wait_ge(s_lim, 1)
            each_expert(dve, body)


def combine(nc, ctx, GATH, y_dram, t_dram, out):
    GRP = 4
    NG = TT // GRP
    NBF = 4

    def sb(name, shape, dt):
        return ctx.enter_context(nc.sbuf_tensor(name, shape, dt))

    def sem(name):
        return ctx.enter_context(nc.semaphore(name))
    Y = sb("Y", [P, NBF, GRP, C], F32)
    TX = sb("TX", [P, NBF, GRP, C], F32)
    GATHC = sb("GATHC", [P, NBF, GRP], I32)
    s_g = [sem(f"c_rows{i}") for i in range(NBF)]
    s_t = [sem(f"c_t{i}") for i in range(NBF)]
    s_o = [sem(f"c_out{i}") for i in range(NBF)]
    s_passed = sem("c_passed")
    s_ic = sem("c_index")
    s_f = sem("c_final")

    with nc.Block() as block:
        @block.sync
        def _(sp):
            for s in (*s_o, s_f):
                sp.sem_inc(s, START)
            with sp.Fori(0, NG // NBF) as i:
                for b in range(NBF):
                    sp.wait_ge(s_o[b], START + i * 16)
                    sp.dma_start(TX[:, b], t_dram[bass.ds((i * NBF + b) * GRP, GRP)].rearrange("t p c -> p t c")).then_inc(s_t[b], 16)

        @block.scalar
        def _(act):
            with act.Fori(0, NG // NBF) as i:
                for b in range(NBF):
                    act.wait_ge(s_f, START + i * NBF + b + 1)
                    act.dma_start(out[bass.ds((i * NBF + b) * GRP, GRP)].rearrange("t p c -> p t c"), TX[:, b]).then_inc(s_o[b], 16)
            for b in range(NBF):
                act.wait_ge(s_o[b], START + NG // NBF * 16)

        @block.gpsimd
        def _(pool):
            with pool.Fori(0, NG // NBF) as i:
                for b in range(NBF):
                    wait_apart(pool, s_f, START + i * NBF + max(b + 1 - NBF, 0), s_passed)
                    nc.gpsimd.tensor_copy(GATHC[:, b, :], GATH[:, bass.ds((i * NBF + b) * GRP, GRP)]).then_inc(s_ic, 1)
                    wait_apart(pool, s_ic, i * NBF + b + 1, s_passed)
                    for g in range(GRP):
                        nc.gpsimd.indirect_dma_start(Y[:, b, g, :], None, y_dram,
                                                     bass.IndirectOffsetOnAxis(ap=GATHC[:, b, g:g + 1], axis=0),
                                                     bounds_check=SLOTS, oob_is_err=False).then_inc(s_g[b], 16)

        @block.vector
        def _(dve):
            with dve.Fori(0, NG // NBF) as i:
                for b in range(NBF):
                    dve.wait_ge(s_g[b], (i + 1) * (16 * GRP))
                    dve.wait_ge(s_t[b], (i + 1) * 16)
                    nc.vector.tensor_tensor(TX[:, b], TX[:, b], Y[:, b], ALU.add).then_inc(s_f, 1)


def kernel(**inputs):
    import numpy as np
    import concourse.bacc as bacc
    from concourse.bass_utils import run_bass_kernel_spmd

    nc = bacc.Bacc("TRN2", target_bir_lowering=False, num_devices=1)
    x = np.asarray(inputs["x"]).reshape(BATCH, C, TOK)
    qkv = np.asarray(inputs["L0_conv_qkv_w"])
    heads = qkv.reshape(3, HEADS, DH, C)
    col = np.arange(TOK) % SIDE
    row = np.arange(TOK) // SIDE
    side = np.arange(SIDE)[:, None]
    arrays = {
        "xc": x,
        "xt": x.transpose(0, 2, 1),
        "whead": heads[:2].transpose(1, 3, 0, 2).reshape(HEADS, C, 2 * DH),
        "wv": heads[2].transpose(2, 0, 1).reshape(C, HEADS * DH),
        "hrt": np.asarray(inputs["L0_conv_height_rel"]).T,
        "wrt": np.asarray(inputs["L0_conv_width_rel"]).T,
        "onehots": (S16 * np.stack([side == col, side % (SIDE // 2) == row % (SIDE // 2)])).astype(np.float16),
        "ident": np.eye(P, dtype=np.float32),
        "utri": np.triu(np.ones((P, P), np.float32), 1),
        "iota_e": np.tile(np.arange(EXPERTS, 0, -1, dtype=np.float32), (P, 1)),
        "gate_w": np.asarray(inputs["L0_ffn_gate_w"]),
        "gate_b": np.asarray(inputs["L0_ffn_gate_b"]),
        "w1": np.asarray(inputs["L0_ffn_w1"]),
        "b1": np.asarray(inputs["L0_ffn_b1"]).reshape(EXPERTS, KF, P).transpose(2, 0, 1),
        "w2": np.asarray(inputs["L0_ffn_w2"]),
        "b2": np.asarray(inputs["L0_ffn_b2"]),
    }
    feeds, args = {}, []
    for name, a in arrays.items():
        a = np.ascontiguousarray(a)
        feeds["in_" + name] = a
        args.append(nc.dram_tensor("in_" + name, a.shape, mybir.dt.from_np(a.dtype), kind="ExternalInput").ap())
    out = nc.dram_tensor("out_dram", (TT, P, C), F32, kind="ExternalOutput").ap()
    build(nc, *args, out)
    r = run_bass_kernel_spmd(nc, [feeds], core_ids=[0])
    y = r.results[0]["out_dram"].reshape(BATCH, TOK, C).transpose(0, 2, 1)
    return np.ascontiguousarray(y).reshape(BATCH, C, SIDE, SIDE)
```

```python
import concourse.bass as bass
from concourse import mybir
from contextlib import ExitStack

F32 = mybir.dt.float32
F16 = mybir.dt.float16
I32 = mybir.dt.int32
ALU = mybir.AluOpType
ACT = mybir.ActivationFunctionType
AX = mybir.AxisListType

P = 128
BATCH, C, SIDE = 2, 256, 64
TOK = SIDE * SIDE
HEADS, DH = 4, 64
KC = C // P
NT = TOK // P
QB = 512
NB = TOK // QB
SUB = QB // P
ROWS = QB // SIDE
UNITS = TOK // (2 * P)
NBUF = 4
VW = 2 * DH + 1
WIN = 2 * SIDE - 1
WINP = SIDE - 1 + P

EXPERTS, FF, CAP = 8, 1024, 1280
TT = BATCH * NT
ST = CAP // P
SLOTS = EXPERTS * CAP
KF = FF // P
NONE = 1 << 20
CHUNKS = [(0, 4), (4, 3), (7, 3)]

S16 = 16.0
QK = S16 * DH ** -0.5
SHIFT = 7.0

POOL_UNITS = UNITS // 4
VEC_UNITS = UNITS - POOL_UNITS
HALVES = 2 * UNITS
AHEAD = 6
U_CHAIN = 11


def halves_in(u, more, more2):
    if u < U_CHAIN:
        wide = u in (6, 10)
        first = AHEAD + 2 * u + 2 * (u > 6)
        return [(1, first + i) for i in range(4 if wide else 2)] if more else []
    return [(2, k) for k in {11: (), 12: (), 13: (), 14: (0, 1, 2, 3), 15: (4, 5)}[u]] if more2 else []


def by_pool(u):
    return u % 4 == 3


def vec_index(u):
    return u - (u + 1) // 4


assert VEC_UNITS % 2 == 0
assert AHEAD + 2 * U_CHAIN + 4 == HALVES and UNITS == 16
SG = 8
NSG = NT // SG
NG4 = 4
START = 1


def wait_apart(eng, sem, count, passed):
    eng.wait_ge(sem, count)
    eng.sem_inc(passed, 1)


def attention_and_norm(nc, ctx, xt, whead, wv, hrt, wrt, onehots, ident_h, utri, iota_e, gate_w, gate_b, t_dram, xn_dram,
                       slot_tab, out):
    def sb(name, shape, dt):
        return ctx.enter_context(nc.sbuf_tensor(name, shape, dt))

    def sem(name):
        return ctx.enter_context(nc.semaphore(name))

    XN = sb("XN", [P, KC, TOK], F32)
    T = sb("T", [P, NT, C], F32)
    V = sb("V", [P, HEADS, NT, VW + 1], F16)
    VS = sb("VS", [P, NT, VW + 1], F16)
    QA = sb("QA", [P, TOK], F16)
    QBf = sb("QBf", [P, TOK], F16)
    QC = [sb(f"QC{i}", [P, TOK], F16) for i in range(2)]
    KA = sb("KA", [P, TOK], F16)
    KB = sb("KB", [P, TOK], F16)
    KCC = sb("KCC", [P, TOK], F16)
    PH = sb("PH", [P, NBUF, 2, QB], F16)
    PL = sb("PL", [P, NBUF, 2, QB], F16)
    PF = sb("PF", [P, 2, 2, QB], F32)
    PFP = sb("PFP", [P, 2, QB], F32)
    WH = sb("WH", [P, KC, 2 * DH], F32)
    WV = sb("WV", [P, KC, HEADS * DH], F32)
    RELH = sb("RELH", [DH, 2, WINP], F16)
    RELL = sb("RELL", [DH, 2, WINP], F16)
    G = sb("G", [P, SUB, SIDE], F32)
    G2 = sb("G2", [P, SUB, SIDE], F32)
    MROW = sb("MROW", [P, SUB], F32)
    MNEG = sb("MNEG", [P, SUB], F32)
    DIAG = sb("DIAG", [P, SUB, P], F16)
    IDH = sb("IDH", [P, P], F16)
    IDF = sb("IDF", [P, P], F32)
    ONEH = sb("ONEH", [P, P], F16)
    WB = sb("WB", [DH, 2, 2 * P], F16)
    QS = sb("QS", [DH, 2, QB], F16)
    PVS = sb("PVS", [P, SUB, VW], F32)
    PVR = sb("PVR", [P, SUB], F32)
    PVO = G2
    EPS6 = sb("EPS6", [P, 1], F32)
    EPS5 = sb("EPS5", [P, 1], F32)
    MV = sb("MV", [P, NT, 2], F32)
    RSTD = sb("RSTD", [P, NT], F32)
    RSTD2 = sb("RSTD2", [P, NT], F32)
    PLF = PL[:].rearrange("p a b n -> p (a b n)").bitcast(F32)
    XNT = QBf[:].bitcast(F32).rearrange("p (a c) -> p a c", a=2 * NG4)
    REL = PLF[0:DH, 0:2 * WINP].rearrange("p (a w) -> p a w", a=2)
    XTT = PLF[:, 2 * C:6 * C].rearrange("p (a c) -> p a c", a=4)
    STAT = PLF[:, 6 * C:6 * C + 6 * NT].rearrange("p (t s) -> p t s", s=6)
    GW = sb("GW", [P, KC, EXPERTS], F32)

    SP = ctx.enter_context(nc.psum_tensor("SP", [P, 4, 512], F32))
    MX = ctx.enter_context(nc.psum_tensor("MX", [P, 2, 512], F32))
    PV = ctx.enter_context(nc.psum_tensor("PV", [P, 2, 512], F32))

    def value_bank(i):
        return MX[:, i % 2, :] if i % 4 < 2 else PV[:, i % 2, :]

    def pair_banks(k):
        i = (k // 2) % 3
        return SP[:, 2 * i:2 * i + 2, :] if i < 2 else MX[:]

    def ahead_banks(k):
        i = (k // 2) % 2
        return SP[:, 2 * i:2 * i + 2, :]

    UT = sb("UT", [P, P], F32)
    ONE = sb("ONE", [P, P], F32)
    GB = sb("GB", [P, EXPERTS], F32)
    IE = sb("IE", [P, EXPERTS], F32)
    IDS = sb("IDS", [P, TT], I32)
    LG = sb("LG", [P, NT, EXPERTS], F32)
    CNT = sb("CNT", [P, EXPERTS], F32)
    ONES_T = sb("ONES_T", [P, NT], F32)
    SCAT = sb("SCAT", [P, NT], I32)
    IDW = sb("IDW", [P, NT, 2], I32)
    EMPTY = PH[:].rearrange("p a b n -> p (a b n)").bitcast(I32)[:, 0:2 * SLOTS // P]
    PFF = PF[:].rearrange("p a b n -> p (a b n)")
    EX, CA, OH, TOTS, POS = (PFF[:, i * NT * EXPERTS:(i + 1) * NT * EXPERTS].rearrange("p (t e) -> p t e", e=EXPERTS)
                             for i in range(5))
    CUM = PFF[:, 5 * NT * EXPERTS:6 * NT * EXPERTS].rearrange("p (e t) -> p e t", e=EXPERTS)
    RTAB = sb("RTAB", [P, 10, NT], F32)
    RNAMES = ("max", "sum", "prob", "code", "pos", "kept", "rel", "rel2", "slot", "w")

    def R_(name):
        return RTAB[:, RNAMES.index(name), :]

    s_passed = sem("s_passed")
    s_zero = sem("s_zero")
    s_ids = sem("s_ids")
    s_v = sem("s_v")
    s_sh = sem("s_sh")
    s_ex = sem("s_ex")
    s_oh = sem("s_oh")
    s_cnt = sem("s_cnt")
    s_slots = sem("s_slots")
    s_sc = sem("s_sc")
    s_scd = sem("s_scd")
    s_const = sem("s_const")
    s_ones = sem("s_ones")
    s_rel = sem("s_rel")
    s_t = sem("s_t")
    s_wh = sem("s_wh")
    s_vps = sem("s_vps")
    s_vh = sem("s_vh")
    s_vl = sem("s_vl")
    s_qk = sem("s_qk")
    s_qkh = sem("s_qkh")
    s_qkl = sem("s_qkl")
    s_dup = sem("s_dup")
    s_rw = sem("s_rw")
    s_rwh = sem("s_rwh")
    s_rwl = sem("s_rwl")
    s_mx = sem("s_mx")
    s_mxr = sem("s_mxr")
    s_rh = sem("s_rh")
    s_g2 = sem("s_g2")
    s_mrow = sem("s_mrow")
    s_mneg = sem("s_mneg")
    s_diag = sem("s_diag")
    s_win = sem("s_win")
    s_r = sem("s_r")
    s_rhh = sem("s_rhh")
    s_rhl = sem("s_rhl")
    s_s = sem("s_s")
    s_e = sem("s_e")
    s_pl = sem("s_pl")
    s_plp = sem("s_plp")
    s_pv = sem("s_pv")
    s_pvs = sem("s_pvs")
    s_pvr = sem("s_pvr")
    s_pvo = sem("s_pvo")
    s_out = sem("s_out")
    s_st = sem("s_st")
    s_mv = sem("s_mv")
    s_ts = sem("s_ts")
    s_tr = sem("s_tr")
    s_tn = sem("s_tn")
    s_tx = sem("s_tx")
    s_te = sem("s_te")
    s_lg = sem("s_lg")
    s_lge = sem("s_lge")
    s_td = sem("s_td")
    s_xd = [sem(f"s_xd{i}") for i in range(2)]

    NCONST = 11

    with nc.Block() as block:

        @block.sync
        def _(sp):
            sp.dma_start(REL[:, 0, 0:WIN], hrt).then_inc(s_const, 16)
            sp.dma_start(REL[:, 1, 0:WIN], wrt).then_inc(s_const, 16)
            sp.dma_start(WV[:], wv.rearrange("(k p) n -> p k n", p=P)).then_inc(s_const, 16)
            sp.dma_start(KA[DH:P, :], onehots[0]).then_inc(s_const, 16)
            sp.dma_start(KB[DH:P, :], onehots[0]).then_inc(s_const, 16)
            sp.dma_start(KCC[DH:P, :], onehots[1]).then_inc(s_const, 16)
            sp.dma_start(IDF[:], ident_h).then_inc(s_const, 16)
            sp.dma_start(GW[:], gate_w.rearrange("(k p) e -> p k e", p=P)).then_inc(s_const, 16)
            sp.dma_start(UT[:], utri).then_inc(s_const, 16)
            sp.dma_start(GB[:], gate_b.partition_broadcast(P)).then_inc(s_const, 16)
            sp.dma_start(IE[:], iota_e).then_inc(s_const, 16)
            sp.wait_ge(s_ones, 1)
            sp.dma_start(slot_tab.rearrange("(p t) w -> p (t w)", p=P), EMPTY).then_inc(s_zero, 16)
            with sp.Fori(0, BATCH) as b:
                wait_apart(sp, s_td, START + b * 32, s_passed)
                sp.wait_ge(s_lge, START + b)
                sp.dma_start(T[:], xt[bass.ds(b, 1)].rearrange("o (t p) c -> p (o t) c", p=P)).then_inc(s_t, 16)
                with sp.Fori(0, HEADS) as h:
                    sp.wait_ge(s_qkl, START + (b * HEADS + h) * NB)
                    sp.dma_start(WH[:], whead[bass.ds(h, 1)].rearrange("o (k p) n -> p (o k) n", p=P)).then_inc(s_wh, 16)
                sp.wait_ge(s_out, START + (b + 1) * (HEADS * NB))
                sp.dma_start(t_dram[bass.ds(b * NT, NT)].rearrange("t p c -> p t c"), T[:]).then_inc(s_td, 16)
                for g in range(NT // NG4):
                    sp.wait_ge(s_tn, (b * 2 + 1) * NT + (g + 1) * NG4)
                    half = XNT[:, (g % 2) * NG4:(g % 2 + 1) * NG4, :]
                    sp.dma_start(xn_dram[bass.ds(b * NT + g * NG4, NG4)].rearrange("t p c -> p t c"), half)\
                      .then_inc(s_xd[g % 2], 16)
                sp.dma_start(out[bass.ds(b * NT, NT)].rearrange("t p c -> p t c"), T[:]).then_inc(s_td, 16)
            sp.wait_ge(s_td, START + BATCH * 32)
            sp.wait_ge(s_zero, 16)
            for i in range(2):
                sp.wait_ge(s_xd[i], START + BATCH * (NT // NG4 // 2) * 16)

        @block.gpsimd
        def _(pool):
            nc.gpsimd.memset(ONEH[:], 1.0)
            nc.gpsimd.memset(REL[:, :, WIN:WINP], 0.0)
            nc.gpsimd.memset(EPS6[:], 1e-6)
            nc.gpsimd.memset(EPS5[:], 1e-5)
            nc.gpsimd.memset(V[:, :, :, DH:DH + 1], S16)
            nc.gpsimd.memset(ONE[:], 1.0)
            nc.gpsimd.memset(ONES_T[:], 1.0)
            nc.gpsimd.memset(CNT[:], 0.0)
            slots = EMPTY.rearrange("p (t w) -> p t w", w=2)
            nc.gpsimd.memset(slots[:, :, 1], 0)
            nc.gpsimd.memset(slots[:, :, 0], NONE).then_inc(s_ones, 1)
            nc.gpsimd.iota(IDS[:], [[P, TT]], channel_multiplier=1).then_inc(s_ids, 1)
            pool.wait_ge(s_zero, 16)
            with pool.Fori(0, BATCH) as b:
                def windows(h, n, j):
                    pool.wait_ge(s_rel, 3)
                    pool.wait_ge(s_dup, b * HEADS + h + 1)
                    wait_apart(pool, s_r, START + n, s_passed)
                    win = bass.ds(j * (-ROWS) + (SIDE - ROWS), 2 * SIDE)
                    nc.gpsimd.tensor_copy(WB[:, 0, 0:2 * SIDE], RELH[:, 0, win])
                    nc.gpsimd.tensor_copy(WB[:, 1, 0:2 * SIDE], RELL[:, 0, win])
                    nc.gpsimd.tensor_copy(QS[:, 0, :], QA[0:DH, bass.ds(j * QB, QB)])
                    nc.gpsimd.tensor_copy(QS[:, 1, :], QC[0][0:DH, bass.ds(j * QB, QB)]).then_inc(s_win, 1)

                def low_units(n, lo, hi):
                    for i in range(lo, hi):
                        wait_apart(pool, s_e, n * UNITS + 4 * i + 4 + NBUF, s_passed)
                        nc.gpsimd.tensor_tensor(PL[:, 3, :, :], PFP[:], PH[:, 3, :, :], ALU.subtract).then_inc(s_plp, 1)
                with pool.Fori(0, HEADS) as h:
                    n0 = (b * HEADS + h) * NB
                    windows(h, n0, 0)
                    with pool.Fori(0, NB - 1) as j:
                        low_units(n0 + j, 0, 2)
                        windows(h, n0 + j + 1, j + 1)
                        low_units(n0 + j, 2, POOL_UNITS)
                    low_units(n0 + NB - 1, 0, POOL_UNITS)
                wait_apart(pool, s_slots, START + b + 1, s_passed)
                for t in range(NT):
                    nc.gpsimd.indirect_dma_start(slot_tab, bass.IndirectOffsetOnAxis(ap=SCAT[:, t:t + 1], axis=0),
                                                 IDW[:, t, :], None, bounds_check=SLOTS - 1, oob_is_err=False)\
                      .then_inc(s_sc, 16)
                pool.wait_ge(s_sc, (b + 1) * (NT * 16))
                pool.sem_inc(s_scd, 1)
            pool.wait_ge(s_sc, TT * 16)

        @block.tensor
        def _(pe):
            mm = nc.tensor.matmul

            def cols(j, size=QB):
                return bass.ds(j * size, size)

            def scores(n, j, jq, u, buf_unit, halves=((), ()), height=None):
                bank = 2 * (buf_unit % 2)
                if height:
                    pe.wait_ge(s_e, n * UNITS + buf_unit + NBUF - 1)
                    for t in (0, 1):
                        out = SP[:, bank + t, :]
                        mm(out, KA[:, t * P:(t + 1) * P], QA[:, cols(jq)], start=True, stop=False)
                        mm(out, KB[:, t * P:(t + 1) * P], QBf[:, cols(jq)], start=False, stop=False)
                    height()
                    for t in (0, 1):
                        last = mm(SP[:, bank + t, :], KCC[:, t * P:(t + 1) * P], QC[0][:, cols(jq)], start=False, stop=True)
                    last.then_inc(s_s, 1)
                    return
                pe.wait_ge(s_e, n * UNITS + buf_unit + NBUF - 1)
                for i in range(2):
                    t = 2 * u + i
                    for d, k in halves[i]:
                        max_half(n + d, j + d, k)
                    out = SP[:, bank + i, :]
                    mm(out, KA[:, t * P:(t + 1) * P], QA[:, cols(jq)], start=True, stop=False)
                    mm(out, KB[:, t * P:(t + 1) * P], QBf[:, cols(jq)], start=False, stop=False)
                    last = mm(out, KCC[:, t * P:(t + 1) * P], QC[t // (NT // 2)][:, cols(jq)], start=False, stop=True)
                last.then_inc(s_s, 1)

            def add_values(n, u):
                if by_pool(u):
                    pe.wait_ge(s_plp, START + n * POOL_UNITS + u // 4 + 1)
                else:
                    pe.wait_ge(s_pl, n * VEC_UNITS + vec_index(u) + 1 + NBUF)
                if u == 0:
                    pe.wait_ge(s_pvs, START + n)
                for ns in range(SUB):
                    out = PV[:, ns // 2, (ns % 2) * VW:(ns % 2 + 1) * VW]
                    for i in range(2):
                        t = 2 * u + i
                        first = t == 0 and ns % 2 == 0
                        mm(out, PH[:, u % NBUF, i, ns * P:(ns + 1) * P], VS[:, t, 0:VW], start=first,
                           stop=False, skip_group_check=True)
                        last = mm(out[:, 0:DH + 1], PL[:, u % NBUF, i, ns * P:(ns + 1) * P], VS[:, t, 0:DH + 1], start=False,
                                  stop=(t == NT - 1), skip_group_check=True)
                last.then_inc(s_pv, 1)

            def max_half(n, j, k):
                pe.wait_ge(s_mxr, n * HALVES + k + 1)
                if k == 0:
                    pe.wait_ge(s_rhl, START + n)
                mm(MX[:, k % 2, :], QA[:, bass.ds(j * QB + (k // 8) * P, P)], KA[:, (k % 8) * QB:(k % 8 + 1) * QB],
                   start=True, stop=True).then_inc(s_mx, 1)

            def height_by_token(n):
                pe.wait_ge(s_mxr, (n + 1) * HALVES + 2)
                pe.wait_ge(s_win, n + 1)
                for ns in range(SUB):
                    win = ROWS - 2 - 2 * ns
                    last = mm(MX[:, 0, ns * (SIDE + 1):(ns + 1) * (SIDE + 1)], QS[:, 0, ns * P:(ns + 1) * P],
                              WB[:, 0, win:win + SIDE + 1], start=(ns == 0), stop=(ns == SUB - 1), skip_group_check=True)
                last.then_inc(s_rh, 1)

            def height_minus_max(n):
                pe.wait_ge(s_diag, START + n + 1)
                for ns in range(SUB):
                    mm(MX[:, 1, ns * P:(ns + 1) * P], ONEH[:], DIAG[:, ns, :], start=(ns == 0), stop=False,
                       skip_group_check=True)
                for r in range(ROWS):
                    hi, lo = (WB[:, i, ROWS - 1 - r:ROWS - 1 - r + SIDE] for i in range(2))
                    qh, ql = (QS[:, i, r * SIDE:(r + 1) * SIDE] for i in range(2))
                    out = MX[0:DH, 1, r * SIDE:(r + 1) * SIDE]
                    mm(out, hi, qh, start=False, stop=False, skip_group_check=True)
                    mm(out, lo, qh, start=False, stop=False, skip_group_check=True)
                    last = mm(out, hi, ql, start=False, stop=True, skip_group_check=True)
                last.then_inc(s_r, 1)

            for s, credit in ((s_e, NBUF), (s_pl, NBUF), (s_pv, NBUF), (s_mxr, 2)):
                pe.sem_inc(s, credit)
            for s in (s_qkl, s_td, s_lge, s_rhl, s_pvs, s_out, s_te, s_rwl, s_r, s_diag, s_lg, s_scd, s_slots, s_plp, *s_xd):
                pe.sem_inc(s, START)
            pe.wait_ge(s_ones, 1)
            pe.wait_ge(s_const, NCONST * 16)
            pe.wait_ge(s_rel, 3)
            with pe.Fori(0, BATCH) as b:
                wait_apart(pe, s_slots, START + b, s_passed)

                def turn_tile(phase, t):
                    pe.wait_ge(s_tn, (b * 2 + phase) * NT + t + 1)
                    pe.wait_ge(s_te, START + (b * 2 + phase) * NT + max(t - 3, 0))
                    for k in range(KC):
                        last = nc.tensor.transpose(SP[:, t % 4, k * P:(k + 1) * P], XNT[:, t % (2 * NG4), k * P:(k + 1) * P], IDF[:])
                    last.then_inc(s_tx, 1)

                def values(i):
                    pe.wait_ge(s_te, START + b * (2 * NT) + 2 * i + 2)
                    if i >= 4:
                        pe.wait_ge(s_vl, b * (NT // 2) + i - 3)
                    for t in range(2):
                        for k in range(KC):
                            last = mm(value_bank(i)[:, t * C:(t + 1) * C], XN[:, k, (2 * i + t) * P:(2 * i + t + 1) * P], WV[:, k, :],
                                      start=(k == 0 and t == 0), stop=(k == KC - 1), skip_group_check=True)
                    last.then_inc(s_vps, 1)
                for t in range(NT):
                    turn_tile(0, t)
                    if t % 2 and t >= 3:
                        values((t - 3) // 2)
                values(NT // 2 - 1)
                wait_apart(pe, s_vl, (b + 1) * (NT // 2), s_passed)
                with pe.Fori(0, HEADS) as h:
                    hh = b * HEADS + h
                    pe.wait_ge(s_wh, (hh + 1) * 16)
                    wait_apart(pe, s_e, hh * (NB * UNITS) + NBUF, s_passed)
                    for c in range(NB):
                        pe.wait_ge(s_qkl, START + hh * NB + max(c - 3, 0))
                        for k in range(KC):
                            last = mm(SP[:, c % 4, :], WH[:, k, :], XN[:, k, c * QB:(c + 1) * QB], start=(k == 0),
                                      stop=(k == KC - 1))
                        last.then_inc(s_qk, 1)
                    wait_apart(pe, s_qkl, START + (hh + 1) * NB, s_passed)
                    for g in range(NB):
                        wait_apart(pe, s_rwl, START + hh * NB + max(g - 3, 0), s_passed)
                        for w in range(ROWS):
                            col = g * ROWS + w
                            hi, lo = (t[:, 1, SIDE - 1 - col:2 * SIDE - 1 - col] for t in (RELH, RELL))
                            qh, ql = (t[0:DH, col:col + SIDE * (SIDE - 1) + 1:SIDE] for t in (QA, QC[0]))
                            out = SP[0:DH, g % 4, w * SIDE:(w + 1) * SIDE]
                            mm(out, hi, qh, start=(w == 0), stop=False, skip_group_check=True)
                            mm(out, lo, qh, start=False, stop=False, skip_group_check=True)
                            last = mm(out, hi, ql, start=False, stop=True, skip_group_check=True)
                        last.then_inc(s_rw, 1)
                    pe.wait_ge(s_rwl, START + (hh + 1) * NB)
                    n0 = hh * NB
                    pe.wait_ge(s_rhl, START + n0)

                    def max_pair(jj, k, banks):
                        for i in range(2):
                            last = mm(banks[:, i, :], QA[:, jj * QB + (k // 8) * P:jj * QB + (k // 8 + 1) * P],
                                      KA[:, (k % 8 + i) * QB:(k % 8 + i + 1) * QB], start=True, stop=True)
                        last.then_inc(s_mx, 2)
                    for k in range(0, HALVES, 2):
                        if k >= 6:
                            pe.wait_ge(s_mxr, n0 * HALVES + 2 + k - 4)
                        max_pair(0, k, pair_banks(k))
                    height_by_token(n0)
                    for k in range(0, 4, 2):
                        max_pair(1, k, ahead_banks(k))
                    height_minus_max(n0)
                    pe.wait_ge(s_mxr, (n0 + 1) * HALVES + 2 + 2)

                    def first_height():
                        pe.wait_ge(s_rhl, START + n0 + 1)
                    pe.wait_ge(s_dup, hh + 1)
                    scores(n0, 0, 0, 0, 0, height=first_height)
                    pe.wait_ge(s_mxr, (n0 + 1) * HALVES + 2 + 4)
                    for k in range(4, AHEAD):
                        max_half(n0 + 1, 1, k)
                    scores(n0, 0, 0, 1, 1)

                    def block_of(n, j, more, more2):
                        for u in range(UNITS):
                            now = halves_in(u, more, more2)
                            inner = ([], []) if u == UNITS - 2 else (now[0:1], now[1:2])
                            if u < UNITS - 2:
                                scores(n, j, j, u + 2, u + 2, inner)
                            elif more:
                                def next_height():
                                    pe.wait_ge(s_rhl, START + n + 2)
                                scores(n, j, j + 1, u + 2 - UNITS, u + 2, inner, next_height if u == UNITS - 2 else None)
                            for d, k in now[len(inner[0] + inner[1]):]:
                                max_half(n + d, j + d, k)
                            if u == U_CHAIN and more:
                                height_by_token(n + 1)
                            if u == U_CHAIN + 1 and more:
                                height_minus_max(n + 1)
                            add_values(n, u)
                    with pe.Fori(0, NB - 2) as j:
                        block_of(n0 + j, j, True, True)
                    block_of(n0 + NB - 2, NB - 2, True, False)
                    block_of(n0 + NB - 1, NB - 1, False, False)
                def logits(t):
                    pe.wait_ge(s_te, START + (b * 2 + 1) * NT + t + 1)
                    for k in range(KC):
                        last = mm(MX[:, 0, t * EXPERTS:(t + 1) * EXPERTS], XTT[:, t % 4, k * P:(k + 1) * P], GW[:, k, :],
                                  start=(k == 0), stop=(k == KC - 1))
                    last.then_inc(s_lg, 1)
                for t in range(NT):
                    turn_tile(1, t)
                    if t >= 2:
                        logits(t - 2)
                logits(NT - 2)
                logits(NT - 1)
                pe.wait_ge(s_oh, b + 1)
                oh = OH[:].rearrange("p t e -> p (t e)")
                mm(SP[:, 0, 0:NT * EXPERTS], UT[:], oh, start=True, stop=True)
                mm(SP[:, 1, 0:NT * EXPERTS], ONE[:], oh, start=True, stop=True).then_inc(s_cnt, 1)

        @block.scalar
        def _(act):
            A = nc.scalar.activation

            def exp_unit(n, buf_unit):
                w = n * UNITS + buf_unit
                act.wait_ge(s_s, w + 1)
                act.wait_ge(s_pv, w + 1)
                if by_pool(buf_unit):
                    wait_apart(act, s_plp, START + n * POOL_UNITS + buf_unit // 4, s_passed)
                    pf = PFP[:]
                else:
                    act.wait_ge(s_pl, n * VEC_UNITS + vec_index(buf_unit) + NBUF - 1)
                    pf = PF[:, vec_index(buf_unit) % 2, :, :]
                src = SP[:, 2 * (buf_unit % 2):2 * (buf_unit % 2) + 2, :]
                A(PH[:, buf_unit % NBUF, :, :], src, ACT.Exp, scale=1.0 / (S16 * S16))
                A(pf, src, ACT.Exp, scale=1.0 / (S16 * S16)).then_inc(s_e, 1)

            def height_high(n, j):
                wait_apart(act, s_r, START + n + 1, s_passed)
                for i in range(2):
                    last = A(QC[i][DH:DH + 32, bass.ds(j * QB, QB)], MX[32 * i:32 * i + 32, 1, :], ACT.Copy)
                last.then_inc(s_rhh, 1)

            def diagonal(n):
                act.wait_ge(s_rel, 3)
                act.wait_ge(s_r, START + n)
                wait_apart(act, s_mneg, n + 1, s_passed)
                for ns in range(SUB):
                    last = A(DIAG[:, ns, :], IDH[:], ACT.Copy, scale=MNEG[:, ns:ns + 1])
                last.then_inc(s_diag, 1)

            act.wait_ge(s_const, NCONST * 16)
            act.wait_ge(s_ones, 1)
            A(RELH[:], REL[:], ACT.Copy).then_inc(s_rel, 1)
            A(IDH[:], IDF[:], ACT.Copy).then_inc(s_rel, 1)
            act.wait_ge(s_zero, 16)
            with act.Fori(0, BATCH) as b:
                def root(phase, g):
                    act.wait_ge(s_mv, (b * 2 + phase) * NSG + g + 1)
                    A(RSTD[:, g * SG:(g + 1) * SG], MV[:, g * SG:(g + 1) * SG, 1], ACT.Sqrt,
                      bias=(EPS5 if phase else EPS6)[:]).then_inc(s_ts, 1)

                root(0, 0)
                root(0, 1)

                def value_high(i):
                    act.wait_ge(s_vps, b * (NT // 2) + i + 1)
                    for t in range(2):
                        last = A(V[:, :, 2 * i + t, 0:DH], value_bank(i)[:, t * C:(t + 1) * C].rearrange("p (h d) -> p h d", h=HEADS),
                                 ACT.Copy, scale=S16)
                    last.then_inc(s_vh, 1)
                for t in range(NT):
                    if t % SG == 0 and 0 < t < NT - SG:
                        root(0, t // SG + 1)
                    act.wait_ge(s_tx, b * (2 * NT) + t + 1)
                    A(XN[:, :, t * P:(t + 1) * P], SP[:, t % 4, 0:C].rearrange("p (k n) -> p k n", k=KC), ACT.Copy).then_inc(s_te, 1)
                    if t % 2 and t >= 5:
                        value_high((t - 5) // 2)
                value_high(NT // 2 - 2)
                value_high(NT // 2 - 1)
                with act.Fori(0, HEADS) as h:
                    hh = b * HEADS + h
                    for c in range(NB):
                        col = slice(c * QB, (c + 1) * QB)
                        act.wait_ge(s_qk, hh * NB + c + 1)
                        A(QA[0:DH, col], SP[0:DH, c % 4, :], ACT.Copy, scale=S16)
                        A(KA[0:DH, col], SP[DH:P, c % 4, :], ACT.Copy, scale=QK).then_inc(s_qkh, 1)
                    for g in range(NB):
                        act.wait_ge(s_rw, hh * NB + g + 1)
                        A(QA[DH:P, :].rearrange("p (h w) -> p w h", w=SIDE)[:, g * ROWS:(g + 1) * ROWS, :],
                          SP[0:DH, g % 4, :].rearrange("p (w h) -> p w h", w=ROWS), ACT.Copy).then_inc(s_rwh, 1)
                    n0 = hh * NB
                    A(VS[:, :, 0:VW], V[:, bass.ds(h, 1), :, 0:VW].rearrange("p o t v -> p (o t) v"), ACT.Copy)
                    for i in range(2):
                        wait_apart(act, s_xd[i], START + b * (NT // NG4 // 2 * 16), s_passed)
                    A(QBf[0:DH, :], QA[0:DH, :], ACT.Copy)
                    A(KCC[0:DH, :], KA[0:DH, :], ACT.Copy)
                    wait_apart(act, s_qkl, START + (hh + 1) * NB, s_passed)
                    A(QC[1][0:DH, :], QC[0][0:DH, :], ACT.Copy).then_inc(s_dup, 1)
                    diagonal(n0)
                    height_high(n0, 0)
                    exp_unit(n0, 0)
                    exp_unit(n0, 1)

                    def block_of(n, j, more):
                        for u in range(UNITS):
                            if u < UNITS - 2 or more:
                                exp_unit(n, u + 2)
                            if u == U_CHAIN and more:
                                diagonal(n + 1)
                            if u == U_CHAIN + 1 and more:
                                height_high(n + 1, j + 1)
                        act.wait_ge(s_pv, (n + 1) * UNITS + NBUF)
                        act.wait_ge(s_out, START + n)
                        for i in range(2):
                            last = A(PVS[:, 2 * i:2 * i + 2, :], PV[:, i, 0:2 * VW].rearrange("p (s v) -> p s v", s=2), ACT.Copy)
                        last.then_inc(s_pvs, 1)
                    with act.Fori(0, NB - 1) as j:
                        block_of(n0 + j, j, True)
                    block_of(n0 + NB - 1, NB - 1, False)
                root(1, 0)
                root(1, 1)
                for t in range(NT):
                    if t % SG == 0 and 0 < t < NT - SG:
                        root(1, t // SG + 1)
                    act.wait_ge(s_tx, b * (2 * NT) + NT + t + 1)
                    act.wait_ge(s_lg, START + b * NT + max(t - 3, 0))
                    A(XTT[:, t % 4, :], SP[:, t % 4, 0:C], ACT.Copy).then_inc(s_te, 1)
                act.wait_ge(s_sh, b + 1)
                A(EX[:], LG[:], ACT.Exp).then_inc(s_ex, 1)

        @block.vector
        def _(dve):
            def low_unit(n, buf_unit):
                if by_pool(buf_unit):
                    return
                dve.wait_ge(s_e, n * UNITS + buf_unit + 1 + NBUF)
                nc.vector.tensor_tensor(PL[:, buf_unit % NBUF, :, :], PF[:, vec_index(buf_unit) % 2, :, :], PH[:, buf_unit % NBUF, :, :],
                                        ALU.subtract).then_inc(s_pl, 1)

            def reduce_half(n, k):
                dve.wait_ge(s_mx, n * HALVES + k + 1)
                nc.vector.tensor_reduce(G[:, k // 8, (k % 8) * 8:(k % 8 + 1) * 8],
                                        MX[:, k % 2, :].rearrange("p (h w) -> p h w", w=SIDE), AX.X, ALU.max).then_inc(s_mxr, 1)

            def row_maximum(n):
                dve.wait_ge(s_rh, n + 1)
                rh = MX[:, 0, 0:SUB * (SIDE + 1)].rearrange("p (s w) -> p s w", s=SUB)
                dve.wait_ge(s_mxr, (n + 1) * HALVES + 2)
                nc.vector.scalar_tensor_tensor(G2[0:64], rh[0:64, :, 1:SIDE + 1], S16, G[0:64], ALU.mult, ALU.add)
                nc.vector.scalar_tensor_tensor(G2[64:P], rh[64:P, :, 0:SIDE], S16, G[64:P], ALU.mult, ALU.add).then_inc(s_g2, 1)
                dve.wait_ge(s_g2, n + 1)
                nc.vector.tensor_reduce(MROW[:], G2[:], AX.X, ALU.max).then_inc(s_mrow, 1)
                dve.wait_ge(s_mrow, n + 1)
                dve.wait_ge(s_diag, START + n)
                nc.vector.tensor_scalar(MNEG[:], MROW[:], -1.0 / S16, S16 * SHIFT, ALU.mult, ALU.add).then_inc(s_mneg, 1)

            def height_low(n, j):
                col = bass.ds(j * QB, QB)
                dve.wait_ge(s_rhh, n + 1)
                for i in range(2):
                    last = nc.vector.tensor_tensor(QC[i][DH + 32:P, col], MX[32 * i:32 * i + 32, 1, :], QC[i][DH:DH + 32, col],
                                                   ALU.subtract)
                last.then_inc(s_rhl, 1)

            dve.wait_ge(s_rel, 1)
            nc.vector.tensor_tensor(RELL[:], REL[:], RELH[:], ALU.subtract).then_inc(s_rel, 1)
            with dve.Fori(0, BATCH) as b:
                def token_norm(phase, after):
                    m = b * 2 + phase

                    def stats(g):
                        for t in range(g * SG, (g + 1) * SG):
                            last = nc.vector.bn_stats(STAT[:, t, :], T[:, t, :])
                        last.then_inc(s_st, 1)
                        wait_apart(dve, s_st, m * NSG + g + 1, s_passed)
                        for t in range(g * SG, (g + 1) * SG):
                            last = nc.vector.bn_aggr(MV[:, t, :], STAT[:, t, :])
                        last.then_inc(s_mv, 1)
                    stats(0)
                    for g in range(NSG):
                        if g + 1 < NSG:
                            stats(g + 1)
                        dve.wait_ge(s_ts, m * NSG + g + 1)
                        nc.vector.reciprocal(RSTD2[:, g * SG:(g + 1) * SG], RSTD[:, g * SG:(g + 1) * SG]).then_inc(s_tr, 1)
                        wait_apart(dve, s_tr, m * NSG + g + 1, s_passed)
                        for t in range(g * SG, (g + 1) * SG):
                            if phase and t % NG4 == 0:
                                i = t // NG4
                                dve.wait_ge(s_xd[i % 2], START + (b * (NT // NG4 // 2) + i // 2) * 16)
                            dve.wait_ge(s_te, START + m * NT + max(t - 2 * NG4 + 1, 0))
                            nc.vector.tensor_scalar(XNT[:, t % (2 * NG4), :], T[:, t, :], MV[:, t, 0:1], RSTD2[:, t:t + 1],
                                                    ALU.subtract, ALU.mult).then_inc(s_tn, 1)
                            after(t)

                def value_low(i):
                    dve.wait_ge(s_vh, b * (NT // 2) + i + 1)
                    for t in range(2):
                        last = nc.vector.scalar_tensor_tensor(
                            V[:, :, 2 * i + t, DH + 1:VW], value_bank(i)[:, t * C:(t + 1) * C].rearrange("p (h d) -> p h d", h=HEADS),
                            S16, V[:, :, 2 * i + t, 0:DH], ALU.mult, ALU.subtract)
                    last.then_inc(s_vl, 1)

                def value_low_after(t):
                    if t % 2 and t >= 7:
                        value_low((t - 7) // 2)
                dve.wait_ge(s_t, (b + 1) * 16)
                for i in range(2):
                    wait_apart(dve, s_xd[i], START + b * (NT // NG4 // 2 * 16), s_passed)
                token_norm(0, value_low_after)
                for i in range(NT // 2 - 3, NT // 2):
                    value_low(i)
                with dve.Fori(0, HEADS) as h:
                    hh = b * HEADS + h
                    for c in range(NB):
                        col = slice(c * QB, (c + 1) * QB)
                        dve.wait_ge(s_qkh, hh * NB + c + 1)
                        nc.vector.scalar_tensor_tensor(QC[0][0:DH, col], SP[0:DH, c % 4, :], S16, QA[0:DH, col], ALU.mult,
                                                       ALU.subtract)
                        nc.vector.scalar_tensor_tensor(KB[0:DH, col], SP[DH:P, c % 4, :], QK, KA[0:DH, col], ALU.mult,
                                                       ALU.subtract).then_inc(s_qkl, 1)
                    for g in range(NB):
                        def wide(t):
                            return t[DH:P, :].rearrange("p (h w) -> p w h", w=SIDE)[:, g * ROWS:(g + 1) * ROWS, :]
                        dve.wait_ge(s_rwh, hh * NB + g + 1)
                        nc.vector.tensor_tensor(wide(QBf), SP[0:DH, g % 4, :].rearrange("p (w h) -> p w h", w=ROWS), wide(QA),
                                                ALU.subtract).then_inc(s_rwl, 1)
                    n0 = hh * NB

                    def reduce_pair(n, k, banks):
                        dve.wait_ge(s_mx, n * HALVES + k + 2)
                        nc.vector.tensor_reduce(G[:, k // 8, (k % 8) * 8:(k % 8 + 2) * 8],
                                                banks.rearrange("p a (h w) -> p (a h) w", w=SIDE), AX.X, ALU.max).then_inc(s_mxr, 2)
                    for k in range(0, HALVES, 2):
                        reduce_pair(n0, k, pair_banks(k))
                    row_maximum(n0)
                    for k in range(0, 4, 2):
                        reduce_pair(n0 + 1, k, ahead_banks(k))
                    height_low(n0, 0)
                    for k in range(4, AHEAD):
                        reduce_half(n0 + 1, k)
                    low_unit(n0, 0)

                    def attention_out(n, j):
                        dve.wait_ge(s_pvs, START + n + 1)
                        nc.vector.reciprocal(PVR[:], PVS[:, :, DH]).then_inc(s_pvr, 1)
                        nc.vector.tensor_tensor(PVO[:], PVS[:, :, 0:DH], PVS[:, :, DH + 1:VW], ALU.add).then_inc(s_pvo, 1)
                        dve.wait_ge(s_pvr, n + 1)
                        dve.wait_ge(s_pvo, n + 1)
                        for ns in range(SUB):
                            res = T[:, bass.ds(j * SUB + ns, 1), bass.ds(h * DH, DH)].rearrange("p o d -> p (o d)")
                            last = nc.vector.scalar_tensor_tensor(res, PVO[:, ns, :], PVR[:, ns:ns + 1], res, ALU.mult, ALU.add)
                        last.then_inc(s_out, 1)

                    def block_of(n, j, more, more2, out):
                        for u in range(UNITS):
                            now = halves_in(u, more, more2)
                            early = 0 if u == UNITS - 2 else 2
                            for d, k in now[:early]:
                                reduce_half(n + d, k)
                            if u == U_CHAIN and more:
                                row_maximum(n + 1)
                            if u < UNITS - 1 or more:
                                low_unit(n, u + 1)
                            for d, k in now[early:]:
                                reduce_half(n + d, k)
                            if u == U_CHAIN + 1 and more:
                                height_low(n + 1, j + 1)
                            if u == 2 and out:
                                attention_out(n - 1, j - 1)
                    block_of(n0, 0, True, True, False)
                    with dve.Fori(1, NB - 2) as j:
                        block_of(n0 + j, j, True, True, True)
                    block_of(n0 + NB - 2, NB - 2, True, False, True)
                    block_of(n0 + NB - 1, NB - 1, False, False, True)
                    attention_out(n0 + NB - 1, NB - 1)
                dve.wait_ge(s_out, START + (b + 1) * (HEADS * NB))
                token_norm(1, lambda t: None)
                dve.wait_ge(s_lg, START + (b + 1) * NT)
                nc.vector.tensor_copy(LG[:].rearrange("p t e -> p (t e)"), MX[:, 0, 0:NT * EXPERTS]).then_inc(s_lge, 1)

                steps = [0]
                NSTEPS = 18

                def link(ins):
                    ins.then_inc(s_v, 1)
                    steps[0] += 1
                    wait_apart(dve, s_v, b * NSTEPS + steps[0], s_passed)

                def wide(a):
                    return a.unsqueeze(2).broadcast_to([P, NT, EXPERTS])

                def per_tile(a):
                    return a.unsqueeze(1).broadcast_to([P, NT, EXPERTS])
                V_ = nc.vector
                wait_apart(dve, s_lge, START + b + 1, s_passed)
                link(V_.tensor_tensor(LG[:], LG[:], per_tile(GB[:]), ALU.add))
                link(V_.tensor_reduce(R_("max"), LG[:], AX.X, ALU.max))
                link(V_.tensor_tensor(LG[:], LG[:], wide(R_("max")), ALU.subtract))
                V_.tensor_copy(R_("pos"), R_("max")).then_inc(s_sh, 1)
                link(V_.scalar_tensor_tensor(CA[:], LG[:], 0.0, per_tile(IE[:]), ALU.is_ge, ALU.mult))
                link(V_.tensor_reduce(R_("code"), CA[:], AX.X, ALU.max))
                V_.tensor_tensor(OH[:], CA[:], wide(R_("code")), ALU.is_equal).then_inc(s_oh, 1)
                wait_apart(dve, s_ex, b + 1, s_passed)
                link(V_.tensor_reduce(R_("sum"), EX[:], AX.X, ALU.add))
                V_.reciprocal(R_("prob"), R_("sum"))
                wait_apart(dve, s_cnt, b + 1, s_passed)
                link(V_.tensor_copy(TOTS[:], SP[:, 1, 0:NT * EXPERTS].rearrange("p (t e) -> p t e", e=EXPERTS)))
                for e in range(EXPERTS):
                    last = V_.tensor_tensor_scan(CUM[:, e, :], ONES_T[:], TOTS[:, :, e], CNT[:, e:e + 1], ALU.mult, ALU.add)
                link(last)
                V_.tensor_copy(CNT[:], CUM[:, :, NT - 1])
                link(V_.tensor_tensor(POS[:], CUM[:].rearrange("p e t -> p t e"), TOTS[:], ALU.subtract))
                link(V_.tensor_tensor(CA[:], SP[:, 0, 0:NT * EXPERTS].rearrange("p (t e) -> p t e", e=EXPERTS), POS[:], ALU.add))
                link(V_.tensor_tensor(POS[:], CA[:], OH[:], ALU.mult))
                link(V_.tensor_reduce(R_("pos"), POS[:], AX.X, ALU.add))
                link(V_.tensor_scalar(R_("kept"), R_("pos"), float(CAP), None, ALU.is_lt))
                link(V_.scalar_tensor_tensor(R_("rel"), R_("code"), -float(CAP), R_("pos"), ALU.mult, ALU.add))
                link(V_.tensor_tensor(R_("rel2"), R_("rel"), R_("kept"), ALU.mult))
                link(V_.tensor_scalar(R_("slot"), R_("rel2"), float(SLOTS), None, ALU.add))
                link(V_.tensor_tensor(R_("w"), R_("prob"), R_("kept"), ALU.mult))
                wait_apart(dve, s_scd, START + b, s_passed)
                dve.wait_ge(s_ids, 1)
                V_.tensor_copy(SCAT[:], R_("slot"))
                V_.tensor_copy(IDW[:, :, 0], IDS[:, bass.ds(b * NT, NT)])
                link(V_.tensor_copy(IDW[:, :, 1].bitcast(F32), R_("w")))
                V_.tensor_copy(R_("rel"), R_("w")).then_inc(s_slots, 1)
                assert steps[0] == NSTEPS


def build(nc, xt, whead, wv, hrt, wrt, onehots, ident, utri, iota_e, gate_w, gate_b, w1, b1, w2, b2, out):
    t_dram = nc.dram_tensor("t_dram", [TT, P, C], F32, kind="Internal").ap()
    xn_dram = nc.dram_tensor("xn_dram", [TT, P, C], F32, kind="Internal").ap()
    slot_tab = nc.dram_tensor("slot_tab", [SLOTS, 2], I32, kind="Internal").ap()
    with ExitStack() as ctx:
        attention_and_norm(nc, ctx, xt, whead, wv, hrt, wrt, onehots, ident, utri, iota_e, gate_w, gate_b, t_dram,
                           xn_dram, slot_tab, out)
    with ExitStack() as ctx:
        experts(nc, ctx, ident, w1, b1, w2, b2, xn_dram, t_dram, slot_tab, out)


def experts(nc, ctx, ident, w1, b1, w2, b2, xn_dram, t_dram, slot_tab, out):
    XS, WS, HS = 16.0, 256.0, 16.0
    NY = 5
    NPC = 8
    PIECE = KC * FF // NPC
    FMAX = 3.4028234663852886e38
    NCH = len(CHUNKS)
    HU = NCH * KF
    SPLIT_AT = {(3 * q) // 2: q for q in range(2 * NPC)}
    TURN_AT = {0: 0, 2: 1, 4: 2, 6: 3, 8: 4, 16: 5, 18: 6, 20: 7, 22: 8}
    LAST_TURN = ST - 1
    POOL_PIECES = (1, 4, 7, 10, 13)
    VEC_PIECES = tuple(q for q in range(2 * NPC) if q not in POOL_PIECES)
    NVP, NPP = len(VEC_PIECES), len(POOL_PIECES)
    VEC_W1, POOL_W1 = (len([q for q in pieces if q < NPC]) for pieces in (VEC_PIECES, POOL_PIECES))
    assert len(TURN_AT) == ST - 1 and max(SPLIT_AT) < HU

    def sb(name, shape, dt):
        return ctx.enter_context(nc.sbuf_tensor(name, shape, dt))

    def sem(name):
        return ctx.enter_context(nc.semaphore(name))

    ID = sb("ID", [P, P], F32)
    SLOT = sb("SLOT", [P, SLOTS // P, 2], I32)
    FROM = sb("FROM", [P, SLOTS // P], I32)
    XC = sb("XC", [P, 2, ST], I32)
    TC = sb("TC", [P, ST], I32)
    OC = sb("OC", [P, ST], I32)
    XG = sb("XG", [P, ST, C], F32)
    TG = sb("TG", [P, ST, C], F32)
    XTH = sb("XTH", [P, 2, KC, CAP], F16)
    XTL = sb("XTL", [P, 2, KC, CAP], F16)
    W1F = sb("W1F", [P, KC * FF], F32)
    W2F = sb("W2F", [P, KF * C], F32)
    W1P = [sb(f"W1P{i}", [P, 2, KC * FF], F16) for i in range(2)]
    W2P = [sb(f"W2P{i}", [P, 2, KF * C], F16) for i in range(2)]
    B1F = sb("B1F", [P, EXPERTS, KF], F32)
    B1 = sb("B1", [P, EXPERTS, KF], F32)
    B2 = sb("B2", [P, EXPERTS, C], F32)
    HH = sb("HH", [P, NCH, KF, 512], F16)
    HL = sb("HL", [P, NCH, KF, 512], F16)
    HF = sb("HF", [P, 2, 512], F32)
    YT = sb("YT", [P, C], F32)
    YP_ = sb("YP_", [P, C], F32)
    YN_ = sb("YN_", [P, C], F32)
    MP = sb("MP", [P, C], I32)
    MN = sb("MN", [P, C], I32)
    LIM = sb("LIM", [P, 2, C], F32)
    YS = sb("YS", [P, NY, C], F32)
    OS = sb("OS", [P, NY, C], F32)
    PS = ctx.enter_context(nc.psum_tensor("PS", [P, 8, 512], F32))
    TRP, HP, YP = PS[:, 0:2, :], PS[:, 2:5, :], PS[:, 5:8, :]

    s_passed = sem("e_passed")
    s_lim = sem("e_lim")
    s_idx = sem("e_slots")
    s_from = sem("e_from")
    s_b = sem("e_bias")
    s_b1 = sem("e_bias_scaled")
    s_w1 = sem("e_w1")
    s_w2 = sem("e_w2")
    s_wh = sem("e_w_high")
    s_wl = sem("e_w_low")
    s_wlp = sem("e_w_low_pool")
    s_ws = sem("e_w_scaled")
    s_xc = sem("e_x_index")
    s_oc = sem("e_out_index")
    s_xg = [sem(f"e_gathered{i}") for i in range(ST)]
    s_tg = [sem(f"e_residual{i}") for i in range(ST)]
    s_xt = sem("e_turned")
    s_xh = sem("e_x_high")
    s_xl = sem("e_x_low")
    s_h = sem("e_hidden")
    s_hh = sem("e_h_high")
    s_hl = sem("e_h_low")
    s_y = sem("e_y")
    s_y1 = sem("e_y_bias")
    s_y2 = sem("e_y_parts")
    s_y3 = sem("e_y_masks")
    s_y4 = sem("e_y_limits")
    s_ye = sem("e_y_out")
    s_add = sem("e_added")
    s_od = [sem(f"e_out_dram{i}") for i in range(NY)]

    with nc.Block() as block:
        def each_expert(eng, body):
            with eng.Fori(0, EXPERTS // 2 - 1) as i:
                body(i * 2, 0, True, True)
                body(i * 2 + 1, 1, True, True)
            body(EXPERTS - 2, 0, True, False)
            body(EXPERTS - 1, 1, False, False)

        def piece(par, q):
            src, dst = (W1F, W1P[par]) if q < NPC else (W2F, W2P[par])
            sl = slice((q % NPC) * PIECE, (q % NPC + 1) * PIECE)
            return src[:, sl], dst[:, 1, sl], dst[:, 0, sl]

        @block.sync
        def _(sp):
            sp.sem_inc(s_wl, START)
            sp.sem_inc(s_wlp, START)
            sp.dma_start(SLOT[:], slot_tab.rearrange("(t p) w -> p t w", p=P)).then_inc(s_idx, 16)

            def load_w1(m):
                sp.dma_start(W1F[:].rearrange("p (k f) -> p k f", k=KC),
                             w1[bass.ds(m, 1)].rearrange("o (k p) f -> p (o k) f", p=P)).then_inc(s_w1, 16)

            def load_w2(m):
                sp.dma_start(W2F[:].rearrange("p (k c) -> p k c", k=KF),
                             w2[bass.ds(m, 1)].rearrange("o (k p) c -> p (o k) c", p=P)).then_inc(s_w2, 16)
            load_w1(0)
            load_w2(0)
            sp.dma_start(ID[:], ident).then_inc(s_b, 16)
            sp.dma_start(B1F[:], b1).then_inc(s_b, 16)
            sp.dma_start(B2[:], b2.rearrange("e c -> (e c)").partition_broadcast(P).rearrange("p (e c) -> p e c", c=C))\
              .then_inc(s_b, 16)

            def load_next(m):
                wait_apart(sp, s_wl, START + m * NVP + VEC_W1, s_passed)
                wait_apart(sp, s_wlp, START + m * NPP + POOL_W1, s_passed)
                load_w1(m + 1)
                wait_apart(sp, s_wl, START + (m + 1) * NVP, s_passed)
                wait_apart(sp, s_wlp, START + (m + 1) * NPP, s_passed)
                load_w2(m + 1)
            with sp.Fori(0, EXPERTS - 1) as m:
                load_next(m)

        @block.gpsimd
        def _(pool):
            xn = xn_dram.rearrange("t p c -> (t p) c")
            tt = t_dram.rearrange("t p c -> (t p) c")
            rows_out = out.rearrange("t p c -> (t p) c")

            def split_low(m, par, q):
                wait_apart(pool, s_wh, m * (2 * NPC) + q + 1, s_passed)
                src, lo, hi = piece(par, q)
                nc.gpsimd.tensor_scalar(src, src, WS, None, ALU.mult).then_inc(s_ws, 1)
                wait_apart(pool, s_ws, m * NPP + POOL_PIECES.index(q) + 1, s_passed)
                nc.gpsimd.tensor_tensor(lo, src, hi, ALU.subtract).then_inc(s_wlp, 1)

            def take_index(m, par):
                nc.gpsimd.tensor_copy(XC[:, par, :], FROM[:, bass.ds(m * ST, ST)]).then_inc(s_xc, 1)
                wait_apart(pool, s_xc, m + 1, s_passed)

            def gather(m, par, s):
                wait_apart(pool, s_xt, m * ST + s + 1, s_passed)
                nc.gpsimd.indirect_dma_start(XG[:, s, :], None, xn, bass.IndirectOffsetOnAxis(ap=XC[:, par, s:s + 1], axis=0),
                                             bounds_check=TT * P - 1, oob_is_err=False).then_inc(s_xg[s], 16)

            def residual(s):
                nc.gpsimd.indirect_dma_start(TG[:, s, :], None, tt, bass.IndirectOffsetOnAxis(ap=TC[:, s:s + 1], axis=0),
                                             bounds_check=TT * P - 1, oob_is_err=False).then_inc(s_tg[s], 16)

            def finish(m, s):
                wait_apart(pool, s_tg[s], (m + 1) * 16, s_passed)
                if s >= NY:
                    wait_apart(pool, s_od[s % NY], m * (ST // NY * 16) + 16, s_passed)
                wait_apart(pool, s_ye, START + m * ST + s + 1, s_passed)
                nc.gpsimd.tensor_tensor(OS[:, s % NY, :], YS[:, s % NY, :], TG[:, s, :], ALU.add).then_inc(s_add, 1)
                wait_apart(pool, s_add, m * ST + s + 1 + NY, s_passed)
                nc.gpsimd.indirect_dma_start(rows_out, bass.IndirectOffsetOnAxis(ap=OC[:, s:s + 1], axis=0), OS[:, s % NY, :],
                                             None, bounds_check=TT * P - 1, oob_is_err=False).then_inc(s_od[s % NY], 16)

            nc.gpsimd.memset(LIM[:, 0], 10000.0)
            nc.gpsimd.memset(LIM[:, 1], -10000.0).then_inc(s_lim, 1)
            pool.wait_ge(s_from, 1)
            take_index(0, 0)
            for s in range(ST):
                gather(0, 0, s)
            for q in POOL_PIECES:
                split_low(0, 0, q)
            take_index(1, 1)
            for s in range(ST):
                gather(1, 1, s)

            def body(m, par, more, more2):
                def split(q):
                    if more:
                        split_low(m + 1, 1 - par, q)

                def gathers(lo, hi):
                    if more2:
                        for s in range(lo, hi):
                            gather(m + 2, par, s)
                nc.gpsimd.tensor_copy(TC[:], FROM[:, bass.ds(m * ST, ST)])
                nc.gpsimd.tensor_copy(OC[:], SLOT[:, bass.ds(m * ST, ST), 0]).then_inc(s_oc, 1)
                if more2:
                    wait_apart(pool, s_xt, (m + 1) * ST + ST, s_passed)
                    take_index(m + 2, par)
                wait_apart(pool, s_oc, m + 1, s_passed)
                for s in range(ST // 2):
                    residual(s)
                split(1)
                for s in range(ST // 2, ST):
                    residual(s)
                split(4)
                gathers(0, 5)
                split(7)
                split(10)
                for s in range(0, 4):
                    finish(m, s)
                split(13)
                gathers(5, 9)
                for s in range(4, 7):
                    finish(m, s)
                gathers(9, 10)
                for s in range(7, ST):
                    finish(m, s)
                for i in range(NY):
                    wait_apart(pool, s_od[i], (m + 1) * (ST // NY * 16), s_passed)
            each_expert(pool, body)

        @block.tensor
        def _(pe):
            mm = nc.tensor.matmul
            pe.sem_inc(s_xt, ST)
            pe.sem_inc(s_y, ST)
            pe.sem_inc(s_hh, 3)
            pe.sem_inc(s_add, NY)
            for s in (s_xl, s_ye, s_hl):
                pe.sem_inc(s, START)
            pe.wait_ge(s_b, 48)

            def turn(mt, s):
                pe.wait_ge(s_xg[s], (mt + 1) * 16)
                pe.wait_ge(s_xl, START + mt * ST + max(s - 1, 0))
                for k in range(KC):
                    last = nc.tensor.transpose(TRP[:, s % 2, k * P:(k + 1) * P], XG[:, s, k * P:(k + 1) * P], ID[:])
                last.then_inc(s_xt, 1)

            def body(m, par, more, more2):
                pe.wait_ge(s_wl, START + (m + 1) * NVP)
                pe.wait_ge(s_wlp, START + (m + 1) * NPP)
                pe.wait_ge(s_xl, START + (m + 1) * ST)
                w1p = W1P[par][:].rearrange("p a (k f) -> p a k f", k=KC)
                w2p = W2P[par][:].rearrange("p a (k c) -> p a k c", k=KF)

                def hidden(c):
                    t0, nt = CHUNKS[c]
                    sl = slice(t0 * P, (t0 + nt) * P)
                    for f in range(KF):
                        g = c * KF + f
                        pe.wait_ge(s_hh, m * HU + g + 1)
                        to = HP[:, g % 3, 0:nt * P]
                        fs = slice(f * P, (f + 1) * P)
                        for k in range(KC):
                            mm(to, w1p[:, 0, k, fs], XTH[:, par, k, sl], start=(k == 0), stop=False)
                            mm(to, w1p[:, 1, k, fs], XTH[:, par, k, sl], start=False, stop=False)
                            last = mm(to, w1p[:, 0, k, fs], XTL[:, par, k, sl], start=False, stop=(k == KC - 1))
                        last.then_inc(s_h, 1)
                        if more and g in TURN_AT:
                            turn(m + 1, TURN_AT[g])

                def rows(c):
                    t0, nt = CHUNKS[c]
                    pe.wait_ge(s_hl, START + m * HU + (c + 1) * KF)
                    for t in range(nt):
                        s = t0 + t
                        pe.wait_ge(s_ye, START + m * ST + max(s - 2, 0))
                        to = YP[:, s % 3, 0:C]
                        hs = slice(t * P, (t + 1) * P)
                        for f in range(KF):
                            mm(to, HH[:, c, f, hs], w2p[:, 0, f, :], start=(f == 0), stop=False)
                            mm(to, HH[:, c, f, hs], w2p[:, 1, f, :], start=False, stop=False)
                            last = mm(to, HL[:, c, f, hs], w2p[:, 0, f, :], start=False, stop=(f == KF - 1))
                        last.then_inc(s_y, 1)
                hidden(0)
                hidden(1)
                rows(0)
                hidden(2)
                rows(1)
                if more:
                    turn(m + 1, LAST_TURN)
                rows(2)
            for s in range(ST):
                turn(0, s)
            each_expert(pe, body)

        @block.scalar
        def _(act):
            A = nc.scalar.activation

            def split_high(m, par, q):
                act.wait_ge(s_w1 if q < NPC else s_w2, (m + 1) * 16)
                act.wait_ge(s_y, m * ST)
                src, _, hi = piece(par, q)
                A(hi, src, ACT.Copy, scale=WS).then_inc(s_wh, 1)

            def turned(mt, par, s):
                act.wait_ge(s_xt, mt * ST + s + 1 + ST)
                A(XTH[:, par, :, s * P:(s + 1) * P], TRP[:, s % 2, 0:C].rearrange("p (k n) -> p k n", k=KC), ACT.Copy,
                  scale=XS).then_inc(s_xh, 1)

            def body(m, par, more, more2):
                for c in range(NCH):
                    t0, nt = CHUNKS[c]
                    act.wait_ge(s_y, m * ST + t0 + nt)
                    for f in range(KF):
                        g = c * KF + f
                        wait_apart(act, s_h, m * HU + g + 1, s_passed)
                        src = HP[:, g % 3, 0:nt * P]
                        bias = B1[:, bass.ds(m, 1), f]
                        A(HH[:, c, f, 0:nt * P], src, ACT.Relu, bias=bias, scale=HS / (XS * WS))
                        wait_apart(act, s_hl, START + m * HU + max(g - 1, 0), s_passed)
                        A(HF[:, g % 2, 0:nt * P], src, ACT.Relu, bias=bias, scale=HS / (XS * WS)).then_inc(s_hh, 1)
                        if more and g in SPLIT_AT:
                            split_high(m + 1, 1 - par, SPLIT_AT[g])
                        if more and g in TURN_AT:
                            turned(m + 1, 1 - par, TURN_AT[g])
                if more:
                    turned(m + 1, 1 - par, LAST_TURN)
            act.wait_ge(s_b, 48)
            A(B1[:], B1F[:], ACT.Copy, scale=HS).then_inc(s_b1, 1)
            act.wait_ge(s_b1, 1)
            for q in range(2 * NPC):
                split_high(0, 0, q)
            for s in range(ST):
                turned(0, 0, s)
            each_expert(act, body)

        @block.vector
        def _(dve):
            V_ = nc.vector

            def split_low(m, par, q):
                if q in POOL_PIECES:
                    return
                dve.wait_ge(s_wh, m * (2 * NPC) + q + 1)
                src, lo, hi = piece(par, q)
                V_.scalar_tensor_tensor(lo, src, WS, hi, ALU.mult, ALU.subtract).then_inc(s_wl, 1)

            def turned(mt, par, s):
                dve.wait_ge(s_xh, mt * ST + s + 1)
                V_.scalar_tensor_tensor(XTL[:, par, :, s * P:(s + 1) * P], TRP[:, s % 2, 0:C].rearrange("p (k n) -> p k n", k=KC),
                                        XS, XTH[:, par, :, s * P:(s + 1) * P], ALU.mult, ALU.subtract).then_inc(s_xl, 1)

            def body(m, par, more, more2):
                def low(c):
                    t0, nt = CHUNKS[c]
                    for f in range(KF):
                        g = c * KF + f
                        dve.wait_ge(s_hh, m * HU + g + 1 + 3)
                        V_.tensor_tensor(HL[:, c, f, 0:nt * P], HF[:, g % 2, 0:nt * P], HH[:, c, f, 0:nt * P],
                                         ALU.subtract).then_inc(s_hl, 1)
                        if more and g in SPLIT_AT:
                            split_low(m + 1, 1 - par, SPLIT_AT[g])
                        if more and g in TURN_AT:
                            turned(m + 1, 1 - par, TURN_AT[g])

                def rows(c):
                    t0, nt = CHUNKS[c]
                    for s in range(t0, t0 + nt):
                        dve.wait_ge(s_y, m * ST + s + 1 + ST)
                        n = m * ST + s
                        V_.scalar_tensor_tensor(YT[:], YP[:, s % 3, 0:C], 1.0 / (HS * WS),
                                                B2[:, bass.ds(m, 1), :].rearrange("p o c -> p (o c)"), ALU.mult, ALU.add)\
                          .then_inc(s_y1, 1)
                        w = SLOT[:, bass.ds(n, 1), 1].bitcast(F32)
                        wait_apart(dve, s_y1, n + 1, s_passed)
                        V_.tensor_scalar(YP_[:], YT[:], w, 0.0, ALU.mult, ALU.max)
                        V_.tensor_scalar(YN_[:], YT[:], w, 0.0, ALU.mult, ALU.min).then_inc(s_y2, 1)
                        wait_apart(dve, s_y2, n + 1, s_passed)
                        V_.tensor_scalar(MP[:], YP_[:], FMAX, None, ALU.is_gt)
                        V_.tensor_scalar(MN[:], YN_[:], -FMAX, None, ALU.is_lt).then_inc(s_y3, 1)
                        wait_apart(dve, s_y3, n + 1, s_passed)
                        V_.copy_predicated(YP_[:], MP[:], LIM[:, 0])
                        V_.copy_predicated(YN_[:], MN[:], LIM[:, 1]).then_inc(s_y4, 1)
                        dve.wait_ge(s_y4, n + 1)
                        dve.wait_ge(s_add, n + 1)
                        V_.tensor_tensor(YS[:, s % NY, :], YP_[:], YN_[:], ALU.add).then_inc(s_ye, 1)
                low(0)
                low(1)
                rows(0)
                low(2)
                rows(1)
                if more:
                    turned(m + 1, 1 - par, LAST_TURN)
                rows(2)
            dve.wait_ge(s_idx, 16)
            V_.tensor_scalar(FROM[:], SLOT[:, :, 0], TT * P - 1, None, ALU.min).then_inc(s_from, 1)
            for q in range(2 * NPC):
                split_low(0, 0, q)
            for s in range(ST):
                turned(0, 0, s)
            dve.wait_ge(s_b, 48)
            dve.wait_ge(s_lim, 1)
            each_expert(dve, body)


def kernel(**inputs):
    import numpy as np
    import concourse.bacc as bacc
    from concourse.bass_utils import run_bass_kernel_spmd

    nc = bacc.Bacc("TRN2", target_bir_lowering=False, num_devices=1)
    x = np.asarray(inputs["x"]).reshape(BATCH, C, TOK)
    qkv = np.asarray(inputs["L0_conv_qkv_w"])
    heads = qkv.reshape(3, HEADS, DH, C)
    col = np.arange(TOK) % SIDE
    row = np.arange(TOK) // SIDE
    side = np.arange(SIDE)[:, None]
    arrays = {
        "xt": x.transpose(0, 2, 1),
        "whead": heads[:2].transpose(1, 3, 0, 2).reshape(HEADS, C, 2 * DH),
        "wv": heads[2].transpose(2, 0, 1).reshape(C, HEADS * DH),
        "hrt": np.asarray(inputs["L0_conv_height_rel"]).T,
        "wrt": np.asarray(inputs["L0_conv_width_rel"]).T,
        "onehots": (S16 * np.stack([side == col, side % (SIDE // 2) == row % (SIDE // 2)])).astype(np.float16),
        "ident": np.eye(P, dtype=np.float32),
        "utri": np.triu(np.ones((P, P), np.float32), 1),
        "iota_e": np.tile(np.arange(EXPERTS, 0, -1, dtype=np.float32), (P, 1)),
        "gate_w": np.asarray(inputs["L0_ffn_gate_w"]),
        "gate_b": np.asarray(inputs["L0_ffn_gate_b"]),
        "w1": np.asarray(inputs["L0_ffn_w1"]),
        "b1": np.asarray(inputs["L0_ffn_b1"]).reshape(EXPERTS, KF, P).transpose(2, 0, 1),
        "w2": np.asarray(inputs["L0_ffn_w2"]),
        "b2": np.asarray(inputs["L0_ffn_b2"]),
    }
    feeds, args = {}, []
    for name, a in arrays.items():
        a = np.ascontiguousarray(a)
        feeds["in_" + name] = a
        args.append(nc.dram_tensor("in_" + name, a.shape, mybir.dt.from_np(a.dtype), kind="ExternalInput").ap())
    out = nc.dram_tensor("out_dram", (TT, P, C), F32, kind="ExternalOutput").ap()
    build(nc, *args, out)
    r = run_bass_kernel_spmd(nc, [feeds], core_ids=[0])
    y = r.results[0]["out_dram"].reshape(BATCH, TOK, C).transpose(0, 2, 1)
    return np.ascontiguousarray(y).reshape(BATCH, C, SIDE, SIDE)
```
